# Optimizing a Trainium2 kernel written in Bass

```python
import numpy as np
import jax
import jax.numpy as jnp

def _softmax(x, axis=-1):
    return jax.nn.softmax(x, axis=axis)

def _gelu(x):
    return jax.nn.gelu(x, approximate=True)

def _silu(x):
    return jax.nn.silu(x)

def _sigmoid(x):
    return jax.nn.sigmoid(x)

def _layernorm(x, axis=-1, eps=1e-05):
    m = jnp.mean(x, axis=axis, keepdims=True)
    v = jnp.var(x, axis=axis, keepdims=True)
    return (x - m) / jnp.sqrt(v + eps)

def _scatter_add(tgt, idx, src, axis=0):
    return tgt.at[idx].add(src)

def _segment_sum(src, seg, n):
    return jax.ops.segment_sum(src, seg, n)
kernel_name = 'mk_macaron_d2_jaxref_r8_507706'

def setup_inputs(seed: int=0):
    np.random.seed(seed)
    _w = jnp.asarray

    def _L0_attn_setup():
        import jax, jax.numpy as jnp
        import numpy as np
        DIM = 128
        HEADS = 16
        HEAD_DIM = DIM // HEADS
        B, S = (4, 512)
        key = jax.random.key(seed)
        ks = jax.random.split(key, 8)
        sc = 1.0 / np.sqrt(DIM)
        return {'x': jax.random.normal(ks[0], (B, S, DIM), dtype=jnp.float32), 'Wq': jax.random.normal(ks[1], (DIM, DIM), dtype=jnp.float32) * sc, 'Wk': jax.random.normal(ks[2], (DIM, DIM), dtype=jnp.float32) * sc, 'Wv': jax.random.normal(ks[3], (DIM, DIM), dtype=jnp.float32) * sc, 'Wp': jax.random.normal(ks[4], (DIM, DIM), dtype=jnp.float32) * sc, 'bp': jnp.zeros((DIM,), dtype=jnp.float32), 'conv_w': jax.random.normal(ks[5], (DIM, 3), dtype=jnp.float32) * (1.0 / np.sqrt(3.0)), 'conv_b': jnp.zeros((DIM,), dtype=jnp.float32)}
    _L0_attn_in = _L0_attn_setup()

    def _L0_ffn_setup():
        import jax, jax.numpy as jnp
        import numpy as np
        B, S, H, F, G = (8, 256, 128, 512, 128)
        EPS = 1e-05

        def _dequant(q, scales, g):
            K, N = q.shape
            w = (q.astype(jnp.float32) - 128.0).reshape(K // g, g, N) * scales[:, None, :]
            return w.reshape(K, N)
        key = jax.random.key(seed)
        ks = jax.random.split(key, 8)
        x = jax.random.normal(ks[0], (B, S, H), dtype=jnp.float32)
        ln_gamma = jnp.ones((H,), jnp.float32)
        ln_beta = jnp.zeros((H,), jnp.float32)
        fc1_q = jax.random.randint(ks[1], (H, F), 0, 32, dtype=jnp.int32)
        fc2_q = jax.random.randint(ks[2], (F, H), 0, 32, dtype=jnp.int32)
        fc1_scales = jax.random.uniform(ks[3], (H // G, F), jnp.float32) * 0.02 + 0.001
        fc2_scales = jax.random.uniform(ks[4], (F // G, H), jnp.float32) * 0.02 + 0.001
        fc1_bias = jax.random.normal(ks[5], (F,), jnp.float32) * 0.02
        fc2_bias = jax.random.normal(ks[6], (H,), jnp.float32) * 0.02
        return {'x': x, 'ln_gamma': ln_gamma, 'ln_beta': ln_beta, 'fc1_q': fc1_q, 'fc1_scales': fc1_scales, 'fc1_bias': fc1_bias, 'fc2_q': fc2_q, 'fc2_scales': fc2_scales, 'fc2_bias': fc2_bias}
    _L0_ffn_in = _L0_ffn_setup()

    def _L1_attn_setup():
        import jax, jax.numpy as jnp
        import numpy as np
        N_HEAD = 16
        ROPE_BASE = 10000.0

        def _rotate_half(t):
            d = t.shape[-1] // 2
            return jnp.concatenate([-t[..., d:], t[..., :d]], axis=-1)

        def _rope_cos_sin(T, D, dtype):
            half = D // 2
            theta = 1.0 / ROPE_BASE ** (jnp.arange(half, dtype=dtype) / half)
            pos = jnp.arange(T, dtype=dtype)
            freqs = pos[:, None] * theta[None, :]
            cos = jnp.repeat(jnp.cos(freqs), 2, axis=-1)
            sin = jnp.repeat(jnp.sin(freqs), 2, axis=-1)
            return (cos, sin)
        key = jax.random.key(seed)
        k1, k2, k3 = jax.random.split(key, 3)
        B, T, C = (2, 256, 128)
        x = jax.random.normal(k1, (B, T, C), dtype=jnp.float32)
        w_qkv = jax.random.normal(k2, (C, 3 * C), dtype=jnp.float32) * C ** (-0.5)
        w_proj = jax.random.normal(k3, (C, C), dtype=jnp.float32) * C ** (-0.5)
        return {'x': x, 'w_qkv': w_qkv, 'w_proj': w_proj}
    _L1_attn_in = _L1_attn_setup()

    def _L1_ffn_setup():
        import jax, jax.numpy as jnp
        import numpy as np
        B, S, D = (4, 256, 128)
        E = 16
        K = 2
        F = 64
        FS = 256
        key = jax.random.key(seed)
        ks = jax.random.split(key, 9)
        s = 0.02
        return {'hidden_states': jax.random.normal(ks[0], (B, S, D), jnp.float32), 'router_w': jax.random.normal(ks[1], (E, D), jnp.float32) * s, 'Wg': jax.random.normal(ks[2], (E, D, F), jnp.float32) * s, 'Wu': jax.random.normal(ks[3], (E, D, F), jnp.float32) * s, 'Wd': jax.random.normal(ks[4], (E, F, D), jnp.float32) * s, 'Sg': jax.random.normal(ks[5], (D, FS), jnp.float32) * s, 'Su': jax.random.normal(ks[6], (D, FS), jnp.float32) * s, 'Sd': jax.random.normal(ks[7], (FS, D), jnp.float32) * s, 'shared_gate_w': jax.random.normal(ks[8], (D, 1), jnp.float32) * s}
    _L1_ffn_in = _L1_ffn_setup()
    _d = {'L0_attn_x': _L0_attn_in['x'], 'L0_attn_Wq': _L0_attn_in['Wq'], 'L0_attn_Wk': _L0_attn_in['Wk'], 'L0_attn_Wv': _L0_attn_in['Wv'], 'L0_attn_Wp': _L0_attn_in['Wp'], 'L0_attn_bp': _L0_attn_in['bp'], 'L0_attn_conv_w': _L0_attn_in['conv_w'], 'L0_attn_conv_b': _L0_attn_in['conv_b'], 'L0_ffn_ln_gamma': _L0_ffn_in['ln_gamma'], 'L0_ffn_ln_beta': _L0_ffn_in['ln_beta'], 'L0_ffn_fc1_q': _L0_ffn_in['fc1_q'], 'L0_ffn_fc1_scales': _L0_ffn_in['fc1_scales'], 'L0_ffn_fc1_bias': _L0_ffn_in['fc1_bias'], 'L0_ffn_fc2_q': _L0_ffn_in['fc2_q'], 'L0_ffn_fc2_scales': _L0_ffn_in['fc2_scales'], 'L0_ffn_fc2_bias': _L0_ffn_in['fc2_bias'], 'L1_attn_w_qkv': _L1_attn_in['w_qkv'], 'L1_attn_w_proj': _L1_attn_in['w_proj'], 'L1_ffn_router_w': _L1_ffn_in['router_w'], 'L1_ffn_Wg': _L1_ffn_in['Wg'], 'L1_ffn_Wu': _L1_ffn_in['Wu'], 'L1_ffn_Wd': _L1_ffn_in['Wd'], 'L1_ffn_Sg': _L1_ffn_in['Sg'], 'L1_ffn_Su': _L1_ffn_in['Su'], 'L1_ffn_Sd': _L1_ffn_in['Sd'], 'L1_ffn_shared_gate_w': _L1_ffn_in['shared_gate_w']}
    _x0 = _d['L0_attn_x']
    _d['L0_attn_x'] = jax.random.normal(jax.random.fold_in(jax.random.key(seed), 1), (2, 1024, 128), dtype=_x0.dtype)
    del _x0
    return _d

def reference(L0_attn_x, L0_attn_Wq, L0_attn_Wk, L0_attn_Wv, L0_attn_Wp, L0_attn_bp, L0_attn_conv_w, L0_attn_conv_b, L0_ffn_ln_gamma, L0_ffn_ln_beta, L0_ffn_fc1_q, L0_ffn_fc1_scales, L0_ffn_fc1_bias, L0_ffn_fc2_q, L0_ffn_fc2_scales, L0_ffn_fc2_bias, L1_attn_w_qkv, L1_attn_w_proj, L1_ffn_router_w, L1_ffn_Wg, L1_ffn_Wu, L1_ffn_Wd, L1_ffn_Sg, L1_ffn_Su, L1_ffn_Sd, L1_ffn_shared_gate_w):

    def _L0_attn_ref(x, Wq, Wk, Wv, Wp, bp, conv_w, conv_b):
        import jax, jax.numpy as jnp
        import numpy as np
        DIM = 128
        HEADS = 16
        HEAD_DIM = DIM // HEADS
        B, S = (4, 512)
        b, s, d = x.shape

        def split_heads(t):
            return t.reshape(b, s, HEADS, HEAD_DIM).transpose(0, 2, 1, 3)
        q = split_heads(x @ Wq.T)
        k = split_heads(x @ Wk.T)
        v = split_heads(x @ Wv.T)
        q = jax.nn.elu(q) + 1.0
        k = jax.nn.elu(k) + 1.0
        kv_state = jnp.einsum('bhnd,bhne->bhde', k, v)
        k_state = k.sum(axis=2)
        attn_out = jnp.einsum('bhnd,bhde->bhne', q, kv_state)
        denom = jnp.maximum(jnp.einsum('bhnd,bhd->bhn', q, k_state), 1e-06)[..., None]
        attn_out = (attn_out / denom).transpose(0, 2, 1, 3).reshape(b, s, d)
        xp = jnp.pad(x, ((0, 0), (1, 1), (0, 0)))
        local = xp[:, :-2, :] * conv_w[:, 0] + xp[:, 1:-1, :] * conv_w[:, 1] + xp[:, 2:, :] * conv_w[:, 2] + conv_b
        return (attn_out + local) @ Wp.T + bp

    def _L0_ffn_ref(x, ln_gamma, ln_beta, fc1_q, fc1_scales, fc1_bias, fc2_q, fc2_scales, fc2_bias):
        import jax, jax.numpy as jnp
        import numpy as np
        B, S, H, F, G = (8, 256, 128, 512, 128)
        EPS = 1e-05

        def _dequant(q, scales, g):
            K, N = q.shape
            w = (q.astype(jnp.float32) - 128.0).reshape(K // g, g, N) * scales[:, None, :]
            return w.reshape(K, N)
        residual = x
        mu = jnp.mean(x, axis=-1, keepdims=True)
        var = jnp.mean(jnp.square(x - mu), axis=-1, keepdims=True)
        h = (x - mu) * jax.lax.rsqrt(var + EPS) * ln_gamma + ln_beta
        hf = h.reshape(-1, H)
        w1 = _dequant(fc1_q, fc1_scales, G)
        y = hf @ w1 + fc1_bias
        y = jax.nn.silu(y)
        w2 = _dequant(fc2_q, fc2_scales, G)
        z = y @ w2 + fc2_bias
        return residual + 0.5 * z.reshape(residual.shape)

    def _L1_attn_ref(x, w_qkv, w_proj):
        import jax, jax.numpy as jnp
        import numpy as np
        N_HEAD = 16
        ROPE_BASE = 10000.0

        def _rotate_half(t):
            d = t.shape[-1] // 2
            return jnp.concatenate([-t[..., d:], t[..., :d]], axis=-1)

        def _rope_cos_sin(T, D, dtype):
            half = D // 2
            theta = 1.0 / ROPE_BASE ** (jnp.arange(half, dtype=dtype) / half)
            pos = jnp.arange(T, dtype=dtype)
            freqs = pos[:, None] * theta[None, :]
            cos = jnp.repeat(jnp.cos(freqs), 2, axis=-1)
            sin = jnp.repeat(jnp.sin(freqs), 2, axis=-1)
            return (cos, sin)
        B, T, C = x.shape
        H = N_HEAD
        D = C // H
        scale = D ** (-0.5)
        qkv = x @ w_qkv
        q, k, v = jnp.split(qkv, 3, axis=-1)
        to_heads = lambda t: t.reshape(B, T, H, D).transpose(0, 2, 1, 3)
        q, k, v = (to_heads(q), to_heads(k), to_heads(v))
        cos, sin = _rope_cos_sin(T, D, x.dtype)
        q = q * cos + _rotate_half(q) * sin
        k = k * cos + _rotate_half(k) * sin
        att = jnp.einsum('bhtd,bhsd->bhts', q, k) * scale
        causal = jnp.tril(jnp.ones((T, T), dtype=bool))
        att = jnp.where(causal, att, jnp.finfo(att.dtype).min)
        att = jax.nn.softmax(att, axis=-1)
        y = jnp.einsum('bhts,bhsd->bhtd', att, v)
        y = y.transpose(0, 2, 1, 3).reshape(B, T, C)
        return y @ w_proj

    def _L1_ffn_ref(hidden_states, router_w, Wg, Wu, Wd, Sg, Su, Sd, shared_gate_w):
        import jax, jax.numpy as jnp
        import numpy as np
        B, S, D = (4, 256, 128)
        E = 16
        K = 2
        F = 64
        FS = 256
        b, s, d = hidden_states.shape
        x = hidden_states.reshape(-1, d)
        T = x.shape[0]
        logits = jnp.einsum('td,ed->te', x.astype(jnp.float32), router_w.astype(jnp.float32))
        probs = jax.nn.softmax(logits, axis=-1)
        top_w, top_i = jax.lax.top_k(probs, K)
        top_w = top_w / jnp.sum(top_w, axis=-1, keepdims=True)
        top_w = top_w.astype(x.dtype)
        dense_w = jnp.zeros((T, E), x.dtype).at[jnp.arange(T)[:, None], top_i].add(top_w)

        def body(acc, params):
            wg, wu, wd, cw = params
            h = jax.nn.silu(x @ wg) * (x @ wu)
            return (acc + cw[:, None] * (h @ wd), None)
        expert_out, _ = jax.lax.scan(body, jnp.zeros_like(x), (Wg, Wu, Wd, dense_w.T))
        shared = jax.nn.silu(x @ Sg) * (x @ Su) @ Sd
        shared = jax.nn.sigmoid(x @ shared_gate_w) * shared
        out = expert_out + shared
        return out.reshape(b, s, d)
    x = L0_attn_x
    x = x + 0.5 * _L0_ffn_ref(_layernorm(x, axis=-1), L0_ffn_ln_gamma, L0_ffn_ln_beta, L0_ffn_fc1_q, L0_ffn_fc1_scales, L0_ffn_fc1_bias, L0_ffn_fc2_q, L0_ffn_fc2_scales, L0_ffn_fc2_bias)
    x = x + _L0_attn_ref(_layernorm(x, axis=-1), L0_attn_Wq, L0_attn_Wk, L0_attn_Wv, L0_attn_Wp, L0_attn_bp, L0_attn_conv_w, L0_attn_conv_b)
    x = x + 0.5 * _L0_ffn_ref(_layernorm(x, axis=-1), L0_ffn_ln_gamma, L0_ffn_ln_beta, L0_ffn_fc1_q, L0_ffn_fc1_scales, L0_ffn_fc1_bias, L0_ffn_fc2_q, L0_ffn_fc2_scales, L0_ffn_fc2_bias)
    x = x + 0.5 * _L1_ffn_ref(_layernorm(x, axis=-1), L1_ffn_router_w, L1_ffn_Wg, L1_ffn_Wu, L1_ffn_Wd, L1_ffn_Sg, L1_ffn_Su, L1_ffn_Sd, L1_ffn_shared_gate_w)
    x = x + _L1_attn_ref(_layernorm(x, axis=-1), L1_attn_w_qkv, L1_attn_w_proj)
    x = x + 0.5 * _L1_ffn_ref(_layernorm(x, axis=-1), L1_ffn_router_w, L1_ffn_Wg, L1_ffn_Wu, L1_ffn_Wd, L1_ffn_Sg, L1_ffn_Su, L1_ffn_Sd, L1_ffn_shared_gate_w)
    return x

_drawn_inputs = setup_inputs


def setup_inputs(seed=0):
    import zlib

    import numpy as np

    out = dict(_drawn_inputs(seed))
    spreads = {'L0_attn_bp': (0.0, 0.696),
     'L0_attn_conv_b': (0.0, 0.326),
     'L0_ffn_ln_gamma': (1.0, 0.2),
     'L0_ffn_ln_beta': (0.0, 0.1)}
    factors = {'L0_attn_Wq': 5.612,
     'L0_attn_Wv': 4.074,
     'L0_ffn_fc1_bias': 8.0,
     'L0_ffn_fc2_bias': 8.0,
     'L1_attn_w_qkv': 8.0,
     'L1_attn_w_proj': 8.0,
     'L1_ffn_router_w': 8.0,
     'L1_ffn_Wg': 8.0,
     'L1_ffn_Wu': 8.0,
     'L1_ffn_Wd': 8.0,
     'L1_ffn_Sg': 8.0,
     'L1_ffn_Su': 8.0,
     'L1_ffn_Sd': 8.0,
     'L1_ffn_shared_gate_w': 8.0}
    for name, (base, spread) in spreads.items():
        noise = np.random.default_rng([zlib.crc32(name.encode()), seed]).standard_normal(out[name].shape)
        drawn = base * np.exp(spread * noise) if base else spread * noise
        out[name] = jnp.asarray(drawn.astype(out[name].dtype))
    for name, factor in factors.items():
        out[name] = (out[name] * factor).astype(out[name].dtype)
    return out
```

```python
import concourse.bass as bass
from concourse import mybir
from contextlib import ExitStack

F32 = mybir.dt.float32
F32R = mybir.dt.float32r
BF16 = mybir.dt.bfloat16
I32 = mybir.dt.int32
U32 = mybir.dt.uint32
ALU = mybir.AluOpType
ACT = mybir.ActivationFunctionType
AX = mybir.AxisListType

P = 128
D = 128
B, S = 2, 1024
TILES = B * S // P
CT = 4
CW = CT * P
NC = TILES // CT
H, HD = 16, 8
F = 512
FB = F // P
E_, FE, FS = 16, 64, 256
NU = E_ * FE // P + FS // P
NR = E_ + 1
EPS = 1e-5
TB = S // P
G, GH = 4, 4
SL = 32
SCALE = HD ** -0.5
FFN0, LIN, FFN1, MOE0, CAUSAL, MOE1 = range(6)
FFNS = (FFN0, FFN1)
MOES = (MOE0, MOE1)
W_Q, W_KV, W_QKV, W_R, W_END = 0, 128, 384, 768, 786
C_ID, C_MA, C_MB, C_BM, C_HS, C_IO, C_COS, C_SIN, C_SEL = 0, 128, 256, 384, 512, 528, 544, 608, 672
C_END = C_SEL + NU * P
S_S1, S_B1, S_GA, S_BE, S_CW, S_CB, S_END = 0, 4, 8, 9, 10, 13, 14
R_B2, R_BP, R_S2, R_END = 0, 128, 256, 768

B_BLOCKS = [(c, j) for c in range(2) for j in range(4 * c + 4)]
A_BLOCKS = [(3, 0), (2, 0), (1, 0), (0, 0), (4, 0), (5, 0), (6, 0), (7, 0), (7, 1), (6, 1), (5, 1), (4, 1)]
NBLK = len(B_BLOCKS)
STEPS = B * G


def extras(s, k):
    todo = []
    if k == 5 and s + 1 < STEPS:
        todo.append(("max", s + 1, 0))
    if s >= 0:
        if k == 1:
            todo.append(("max", s, 1))
        if k == 6:
            todo.append(("yout", s, 0))
        if s > 0 and k == 3:
            todo.append(("yout", s - 1, 1))
    if s == -1 and k in (3, 8):
        todo.append(("ln", 18 if k == 3 else 19))
    if 0 <= s <= 2 and k in (2, 7, 9) and 3 * s + (2, 7, 9).index(k) < TB:
        todo.append(("tile", 1, 3 * s + (2, 7, 9).index(k)))
    if (s, k) in ((3, 9), (7, 9)):
        todo.append(("final", s // 4, 0))
    if (s, k) == (4, 5):
        todo.append(("final", 0, 1))
    if (s, k) == (4, 8):
        todo.append(("norm", 20))
    if (s, k) == (5, 2):
        todo.append(("norm", 21))
    if (s, k) == (5, 7):
        todo.append(("ln", 20))
    return todo


def macaron(nc, x_in, wa_in, wp_in, gw_in, uw_in, dw_in, q1_in, q2_in, small_in, rows_in, const_in, out):
    ctx = ExitStack()
    with ctx:
        def sb(name, shape, dt=F32):
            return ctx.enter_context(nc.sbuf_tensor(name, shape, dt))

        def sem(name):
            return ctx.enter_context(nc.semaphore(name))

        x = sb("x", [P, TILES, D])
        uh = sb("uh", [P, TILES * P], F32R)
        ul = sb("ul", [P, TILES * P], F32R)
        stats = sb("stats", [P, CT, 6])
        mv = sb("mv", [P, 2, CT, 2])
        rs = sb("rs", [P, 2, 3, CT])
        rtmp = sb("rtmp", [P, 2, CT])
        nhalf = sb("nhalf", [P, CT])
        hn = sb("hn", [P, 2, CT, D])
        ft = sb("ft", [P, CW])

        wh = sb("wh", [P, W_END], F32R)
        wl = sb("wl", [P, W_END], F32R)
        wp = sb("wp", [P, 2, P])
        late = sb("late", [P, 2 * 2 * H * SL], F32R)
        w1h, w1l = late[:, 0:F], late[:, F:2 * F]
        stg = late[:, :].rearrange("p (r h n) -> p r h n", r=2, h=2 * H)
        gh = sb("gh", [P, NU * P], F32R)
        gl = sb("gl", [P, NU * P], F32R)
        vh = sb("vh", [P, NU * P], F32R)
        vl = sb("vl", [P, NU * P], F32R)
        dw = sb("dw", [P, NU, D])
        small = sb("small", [P, S_END])
        bprow = sb("bprow", [P, D])
        b2q = sb("b2q", [P, D])
        ident = sb("ident", [P, P])
        identr = sb("identr", [P, P], F32R)
        identb = sb("identb", [P, P], BF16)
        masks = sb("masks", [P, 2, P], BF16)
        bmask = sb("bmask", [P, P + H])
        iota = sb("iota", [P, E_])
        rope = sb("rope", [P, 2, TB, HD])
        sel = sb("sel", [3 * NR, NU, P], BF16)

        VX = 2 * TB * H * (HD + 1)
        arena = sb("arena", [P, 3 * GH * CW + VX])
        work = sb("work", [P, 8 * CW])
        hbuf = work[:, 0:4 * CW].rearrange("p (r n) -> p r n", r=4)
        sg = work[:, 4 * CW:6 * CW].rearrange("p (r n) -> p r n", r=2)
        su = work[:, 6 * CW:8 * CW].rearrange("p (r n) -> p r n", r=2)
        ub = work[:, 4 * CW:5 * CW].rearrange("p (t d) -> p t d", t=CT)
        w2 = work[:, 5 * CW:6 * CW].rearrange("p (k d) -> p k d", k=FB)
        o = CW
        qkv = work[:, o:o + 6 * D].rearrange("p (r n) -> p r n", r=2); o += 6 * D
        ysb = work[:, o:o + 2 * CW].rearrange("p (r n) -> p r n", r=2); o += 2 * CW
        ytok = work[:, o:o + TB * D].rearrange("p (t d) -> p t d", t=TB); o += TB * D
        ra = work[:, o:o + 2 * D].rearrange("p (h d) -> p h d", d=HD); o += 2 * D
        rb = work[:, o:o + 2 * D].rearrange("p (h d) -> p h d", d=HD); o += 2 * D
        assert o <= 8 * CW

        lg = sb("lg", [P, CT, NR + 1])
        m8 = sb("m8", [P, CT, 8])
        ix = sb("ix", [P, CT, 8], U32)
        ixf = sb("ixf", [P, CT, 2])
        dd = sb("dd", [P, 2, CT])
        th = sb("th", [P, 2, CT])
        tw = sb("tw", [P, 3, CT])
        oh = sb("oh", [P, 2, CT, E_])
        cw = sb("cw", [P, CT, NR])
        cr = sb("cr", [P, 2, CT, NR])
        cs = sb("cs", [P, CT, 3, NR], BF16)
        cwt = sb("cwt", [3 * NR, 2, CW], BF16)

        qta = sb("qta", [P, 2, G, S], F32R)
        kt = sb("kt", [P, 2, G, S], F32R)
        qtb = sb("qtb", [P, 2, S], F32R)
        stm = sb("stm", [P, 2, CT, GH, SL], F32R)
        mx = sb("mx", [P, 2, TB, GH, 2])
        mm8 = sb("mm8", [P, CT, GH])
        yrec = sb("yrec", [P, CT, GH])

        raw_a = arena[:, 0:W_END]
        raw_c = arena[:, 1024:1024 + C_END]
        raw_g = arena[:, 3072:3072 + NU * P]
        raw_u = arena[:, 4352:4352 + NU * P]
        raw_q = arena[:, 5632:5632 + 2 * F].bitcast(I32).rearrange("p (a n) -> p a n", a=2)
        w1f = arena[:, 6656:6656 + F]
        rows = arena[:, 7168:7168 + R_END]
        PADS = S + 2
        uf = arena[:, 0:2 * PADS].rearrange("p (b t) -> p b t", b=B)
        o = 2 * PADS
        qf = arena[:, o:o + S]; o += S
        kf = arena[:, o:o + S].rearrange("p (t d) -> p t d", t=TB); o += S
        vx = arena[:, o:o + TB * (D + 1)].rearrange("p (t d) -> p t d", t=TB); o += TB * (D + 1)
        neg = arena[:, o:o + 2 * CW].rearrange("p (r n) -> p r n", r=2); o += 2 * CW
        loc = arena[:, o:o + S]; o += S
        mix = arena[:, o:o + S]; o += S
        yt = work[:, 0:4 * D].rearrange("p (r t d) -> p r t d", r=2, t=2)
        assert o <= 3 * GH * CW + VX
        kx = work[:, CW:CW + P + H]
        den = work[:, 2 * CW:2 * CW + 4 * H].rearrange("p (r e h) -> p r e h", r=2, e=2)
        rden = work[:, 3 * CW:3 * CW + 4 * H].rearrange("p (r e h) -> p r e h", r=2, e=2)
        pb = arena[:, 0:3 * GH * CW].rearrange("p (r h n) -> p r h n", r=3, h=GH)
        va = arena[:, 3 * GH * CW:].rearrange("p (b t h d) -> p b t h d", b=B, t=TB, h=H)

        bank = [ctx.enter_context(nc.psum_tensor(f"bank{i}", [P, CW], F32)) for i in range(8)]
        T, ACC = bank[0], bank[7]

        x_loaded = [sem(f"x_loaded{c}") for c in range(NC)]
        q_loaded, small_loaded, a_loaded = sem("q_loaded"), sem("small_loaded"), sem("a_loaded")
        c_loaded, g_loaded = sem("c_loaded"), sem("g_loaded")
        dw_loaded, stored = sem("dw_loaded"), sem("stored")
        consts, w1_ready, w1_hi, w2_ready, prep = (
            sem("consts"), sem("w1_ready"), sem("w1_hi"), sem("w2_ready"), sem("prep"))
        hi_ready = sem("hi_ready")
        stats_ready, rstd_ready, norm_ready, xadd_ready = (
            sem("stats_ready"), sem("rstd_ready"), sem("norm_ready"), sem("xadd_ready"))
        ub_ready = sem("ub_ready")
        ln_t, ft_ready, split_ready = sem("ln_t"), sem("ft_ready"), sem("split_ready")
        lg_ready = sem("lg_ready")
        x_ready, acc_ready = sem("x_ready"), sem("acc_ready")
        dch, pch, ach = sem("dve_chain"), sem("pool_chain"), sem("act_chain")
        y_full, h_ready = sem("y_full"), sem("h_ready")
        g_full, sg_ready, hm_ready = sem("g_full"), sem("sg_ready"), sem("hm_ready")
        down_done = sem("down_done")
        lg_full, dd_ready, th_ready, cs_ready, cw_full, cwt_ready = (
            sem("lg_full"), sem("dd_ready"), sem("th_ready"), sem("cs_ready"), sem("cw_full"), sem("cwt_ready"))
        q_full, eq_ready, qf_ready = sem("q_full"), sem("eq_ready"), sem("qf_ready")
        kv_full, ek_ready, kv_ready = sem("kv_full"), sem("ek_ready"), sem("kv_ready")
        s_full, kx_ready, o_full, yt_ready, yt_full, mix_ready = (
            sem("s_full"), sem("kx_ready"), sem("o_full"), sem("yt_ready"), sem("yt_full"), sem("mix_ready"))
        qkv_full, qkv_ready, stg_hi, stg_lo, stg_ready, v_ready = (
            sem("qkv_full"), sem("qkv_ready"), sem("stg_hi"), sem("stg_lo"), sem("stg_ready"), sem("v_ready"))
        stg_clear = sem("stg_clear")
        kt_full, kt_ready = sem("kt_full"), sem("kt_ready")
        a_full, a_free = sem("a_full"), sem("a_free")
        stm_ready, mx_full, qtb_ready = sem("stm_ready"), sem("mx_full"), sem("qtb_ready")
        b_full, p_ready, pv_done = sem("b_full"), sem("p_ready"), sem("pv_done")
        ysb_ready, yo_full, y_norm = sem("ysb_ready"), sem("yo_full"), sem("y_norm")
        fin_full, fin_ready = sem("fin_full"), sem("fin_ready")

        block = ctx.enter_context(nc.Block())

        def acc_done(L):
            p, c = divmod(L, 4)
            if p in FFNS:
                return down_done, FB * (L - 4 * p + 1) + (NC * FB if p == FFN1 else 0)
            if p in MOES:
                return down_done, 2 * NC * FB + NU * (c + 1) + (NC * NU if p == MOE1 else 0)
            return acc_ready, c + 1 + (NC if p == CAUSAL else 0)

        def tok(c):
            return slice(c * CW, (c + 1) * CW)

        @block.sync
        def _(sp):
            xv = x_in.rearrange("(t p) d -> p t d", p=P)
            ov = out.rearrange("b (t p) d -> p b t d", p=P)
            for c in range(NC):
                sp.dma_start(x[:, c * CT:(c + 1) * CT, :], xv[:, c * CT:(c + 1) * CT, :]).then_inc(x_loaded[c], 16)
                if c == 0:
                    sp.dma_start(raw_q[:, 0, :], q1_in).then_inc(q_loaded, 16)
                    sp.dma_start(raw_q[:, 1, :], q2_in).then_inc(q_loaded, 16)
            sp.dma_start(raw_g, gw_in).then_inc(g_loaded, 16)
            sp.dma_start(raw_u, uw_in).then_inc(g_loaded, 16)
            sp.dma_start(dw[:, :, :].rearrange("p u d -> p (u d)"), dw_in).then_inc(dw_loaded, 16)
            for c in range(NC):
                sp.wait_ge(x_ready, 4 * MOE1 + c + 1)
                sp.dma_start(ov[:, c // 2, (c % 2) * CT:(c % 2 + 1) * CT, :],
                             x[:, c * CT:(c + 1) * CT, :]).then_inc(stored, 16)
            sp.wait_ge(stored, 16 * NC)

        @block.gpsimd
        def _(pool):
            chain = [0]

            def link(ins):
                chain[0] += 1
                ins.then_inc(pch, 1)
                pool.wait_ge(pch, chain[0])

            def rstd(L):
                r = L % 2
                pool.wait_ge(stats_ready, L + 1)
                var = mv[:, r, :, 1]
                r1, r2, r3 = (rs[:, r, n, :] for n in range(3))
                t = rtmp[:, r, :]
                link(pool.tensor_scalar(t, var, EPS, None, ALU.add))
                p = pool.tensor_tensor(r1, t, nhalf[:, :], ALU.pow)
                if L // 4 not in FFNS:
                    p.then_inc(rstd_ready, 1)
                    if L // 4 == LIN:
                        xadd(L, bprow[:, :])
                    return
                link(p)
                link(pool.tensor_tensor(t, r1, r1, ALU.mult))
                link(pool.tensor_tensor(t, t, var, ALU.mult))
                link(pool.tensor_scalar(t, t, EPS, None, ALU.add))
                link(pool.tensor_tensor(r2, t, nhalf[:, :], ALU.pow))
                pool.tensor_tensor(r3, r1, r2, ALU.mult).then_inc(rstd_ready, 1)
                xadd(L, b2q[:, :])

            def xadd(L, row):
                c = L % 4
                pool.wait_ge(norm_ready, L + 1)
                if L // 4 in FFNS:
                    pool.wait_ge(ub_ready, L % 4 + 1 + (4 if L // 4 == FFN1 else 0))
                xc = x[:, c * CT:(c + 1) * CT, :]
                pool.tensor_tensor(xc, xc, row.unsqueeze(1).to_broadcast([P, CT, D]), ALU.add).then_inc(xadd_ready, 1)

            def tile(b, i):
                n = TB * b + i
                pool.wait_ge(qkv_ready, n + 1)
                pool.tensor_copy(va[:, b, i, :, 0:HD],
                                 qkv[:, n % 2, 2 * D:].rearrange("p (h d) -> p h d", h=H)).then_inc(v_ready, 1)
                pool.wait_ge(stg_hi, n + 1)
                s = stg[:, n % 2, :, :].bitcast(F32)
                pool.tensor_copy(stg[:, n % 2, 0:H, HD:2 * HD], s[:, 0:H, 0:HD])
                pool.tensor_copy(stg[:, n % 2, H:, 2 * HD:3 * HD], s[:, H:, 0:HD]).then_inc(stg_ready, 1)

            pool.memset(nhalf[:, :], -0.5)
            pool.memset(stm[:, :, :, :, :].bitcast(F32), 0.0)
            pool.wait_ge(c_loaded, 16)
            pool.tensor_copy(ident[:, :], raw_c[:, C_ID:C_ID + P])
            pool.tensor_copy(identr[:, :], raw_c[:, C_ID:C_ID + P]).then_inc(consts, 1)
            pool.wait_ge(small_loaded, 32)
            pool.tensor_scalar(b2q[:, :], rows[:, R_B2:R_B2 + D], 0.25, None, ALU.mult)
            pool.tensor_copy(bprow[:, :], rows[:, R_BP:R_BP + D]).then_inc(consts, 1)
            rstd(0)
            rstd(1)
            pool.tensor_copy(identb[:, :], raw_c[:, C_ID:C_ID + P])
            pool.tensor_copy(masks[:, :, :], raw_c[:, C_MA:C_MA + 2 * P].rearrange("p (a n) -> p a n", a=2))
            pool.tensor_copy(bmask[:, :], raw_c[:, C_BM:C_BM + P + H])
            pool.tensor_copy(iota[:, :], raw_c[:, C_IO:C_IO + E_])
            pool.tensor_copy(rope[:, :, :, :], raw_c[:, C_COS:C_COS + 2 * TB * HD]
                             .rearrange("p (a t d) -> p a t d", a=2, t=TB))
            pool.tensor_copy(sel[:, :, :], raw_c[0:3 * NR, C_SEL:C_END].rearrange("p (u n) -> p u n", u=NU))\
                .then_inc(consts, 1)

            def low(part, hi, lo, raw, last=False):
                pool.wait_ge(hi_ready, part)
                pool.tensor_tensor(lo, raw, hi.bitcast(F32), ALU.subtract).then_inc(prep, 1)

            low(1, wh[:, :], wl[:, :], raw_a)
            rstd(2)
            low(2, gh[:, :], gl[:, :], raw_g)
            rstd(3)
            low(3, vh[:, :], vl[:, :], raw_u)
            for L in range(4, 20):
                if L == 16:
                    pool.wait_ge(x_ready, 4 * LIN + 4)
                    pool.memset(va[:, :, :, :, HD:HD + 1], 1.0)
                    pool.wait_ge(x_ready, 4 * FFN1 + 4)
                    link(pool.memset(stg[:, :, :, :].bitcast(F32), 0.0))
                    pool.memset(stg[:, :, H:, 3 * HD:3 * HD + 2].bitcast(F32), 1.0).then_inc(stg_clear, 1)
                if L < 18:
                    rstd(L)
            rstd(18)
            for i in range(TB):
                tile(0, i)
            rstd(19)
            for s in range(-1, STEPS):
                for k in range(NBLK):
                    for todo in extras(s, k):
                        if todo[0] == "tile":
                            tile(*todo[1:])
                        if todo[0] == "norm":
                            rstd(todo[1])
            rstd(22)
            rstd(23)

        @block.scalar
        def _(act):
            chain = [0]

            def link(ins):
                chain[0] += 1
                ins.then_inc(ach, 1)
                act.wait_ge(ach, chain[0])

            act.dma_start(small[:, :], small_in).then_inc(small_loaded, 16)
            act.dma_start(rows, rows_in.to_broadcast([P, R_END])).then_inc(small_loaded, 16)
            act.dma_start(raw_c, const_in).then_inc(c_loaded, 16)
            act.dma_start(raw_a, wa_in).then_inc(a_loaded, 16)
            act.dma_start(wp[:, :, :].rearrange("p a n -> p (a n)"), wp_in).then_inc(a_loaded, 16)

            def ln(L):
                p, c = divmod(L, 4)
                act.wait_ge(ln_t, L + 1)
                if L >= 1:
                    act.wait_ge(split_ready, L)
                dst = ft[:, :]
                if p == LIN:
                    dst = uf[:, c // 2, 1 + (c % 2) * CW:1 + (c % 2 + 1) * CW]
                    act.wait_ge(prep, 3)
                    act.wait_ge(consts, 3)
                    act.wait_ge(w2_ready, 2)
                if p in FFNS:
                    ins = act.activation(dst, T[:, :], ACT.Identity, bias=small[:, S_BE:S_BE + 1],
                                         scale=small[:, S_GA:S_GA + 1])
                else:
                    ins = act.activation(dst, T[:, :], ACT.Copy)
                ins.then_inc(ft_ready, 1)

            def ffn(p):
                for n in range(NC * FB):
                    k, m = n % FB, n + (16 if p == FFN1 else 0)
                    act.wait_ge(y_full, m + 1)
                    if m >= 4:
                        act.wait_ge(down_done, m - 3)
                    act.activation(hbuf[:, m % 4, :], bank[1 + m % 4][:, :], ACT.Silu,
                                   bias=small[:, S_B1 + k:S_B1 + k + 1],
                                   scale=small[:, S_S1 + k:S_S1 + k + 1]).then_inc(h_ready, 1)
                    if k == 1:
                        ln(4 * p + n // FB + 1)

            def linear(b):
                if b == 1:
                    ln(4 * LIN + 2)
                ln(4 * LIN + 2 * b + 1)
                for c in range(2):
                    n = 2 * b + c
                    act.wait_ge(q_full, n + 1)
                    if n >= 1:
                        act.wait_ge(kv_ready, 4 * b if c == 0 else 0) if b and c == 0 else act.wait_ge(qf_ready, n)
                    link(act.activation(neg[:, 0, :], bank[1 + c][:, :], ACT.Relu, scale=-1.0))
                    act.activation(neg[:, 1, :], neg[:, 0, :], ACT.Exp, scale=-1.0).then_inc(eq_ready, 1)
                for t in range(4):
                    n = 4 * b + t
                    act.wait_ge(kv_full, n + 1)
                    act.wait_ge(qf_ready, 2 * b + 2) if t == 0 else act.wait_ge(kv_ready, n)
                    kp = bank[3 + t % 2][:, :].rearrange("p (t n) -> p t n", t=2)[:, :, 0:D]
                    n0 = neg[:, 0, 0:2 * D].rearrange("p (t n) -> p t n", t=2)
                    n1 = neg[:, 1, 0:2 * D].rearrange("p (t n) -> p t n", t=2)
                    link(act.activation(n0, kp, ACT.Relu, scale=-1.0))
                    act.activation(n1, n0, ACT.Exp, scale=-1.0).then_inc(ek_ready, 1)

            def route(r):
                act.wait_ge(dd_ready, r + 1)
                act.activation(th[:, :, :], dd[:, :, :], ACT.Tanh, scale=0.5).then_inc(th_ready, 1)

            def weights(r):
                act.wait_ge(cw_full, r + 1)
                act.activation(cwt[:, r % 2, :], T[0:3 * NR, 0:CW // 2].bitcast(BF16), ACT.Copy)\
                    .then_inc(cwt_ready, 1)

            def moe(p):
                r0 = 4 if p == MOE1 else 0
                route(r0)
                weights(r0)
                for n in range(NC * NU):
                    c, u = divmod(n, NU)
                    m = n + (NC * NU if p == MOE1 else 0)
                    act.wait_ge(g_full, m + 1)
                    if m >= 2:
                        act.wait_ge(hm_ready, m - 1)
                    act.activation(sg[:, m % 2, :], bank[1 + m % 2][:, :], ACT.Silu).then_inc(sg_ready, 1)
                    L = 4 * p + c + 1
                    if u == 1 and L < 24:
                        ln(L)
                    if c < 3 and u == 5:
                        route(r0 + c + 1)
                    if c < 3 and u == 8:
                        weights(r0 + c + 1)

            def tile(b, i):
                n = TB * b + i
                act.wait_ge(qkv_full, n + 1)
                if n >= 2:
                    act.wait_ge(stg_ready, n - 1)
                act.activation(qkv[:, n % 2, :], bank[7][:, 0:3 * D], ACT.Copy).then_inc(qkv_ready, 1)
                for which, dst in enumerate((kt, qta)):
                    act.wait_ge(kt_full, 2 * n + which + 1)
                    act.activation(dst[:, b, :, i * P:(i + 1) * P],
                                   T[:, :].rearrange("p (g t) -> p g t", g=G), ACT.Copy)\
                        .then_inc(kt_ready, 1)

            def causal():
                ln(17)
                for i in range(TB):
                    tile(0, i)
                for s in range(-1, STEPS):
                    for k, (c, j) in enumerate(B_BLOCKS):
                        if s >= 0:
                            blk = s * NBLK + k
                            w = min(CW, CW * (c + 1) - j * P)
                            for h in range(GH):
                                n = blk * GH + h
                                act.wait_ge(b_full, n + 1)
                                if h == 0 and blk >= 3:
                                    act.wait_ge(pv_done, blk - 2)
                                act.activation(pb[:, blk % 3, h, 0:w], bank[1 + n % 3][:, 0:w], ACT.Exp,
                                               scale=SCALE).then_inc(p_ready, 1)
                            if k == 4:
                                yraw(s, 0)
                            if k == 1 and s > 0:
                                yraw(s - 1, 1)
                        for todo in extras(s, k):
                            if todo[0] == "ln":
                                ln(todo[1])
                            if todo[0] == "tile":
                                tile(*todo[1:])
                            if todo[0] == "final":
                                final(*todo[1:])
                yraw(STEPS - 1, 1)
                final(1, 1)

            def yraw(s, c):
                n = 2 * s + c
                act.wait_ge(pv_done, s * NBLK + (4 if c == 0 else 12))
                if n >= 2:
                    act.wait_ge(yo_full, n - 1)
                act.activation(ysb[:, n % 2, :], bank[6][:, :], ACT.Copy).then_inc(ysb_ready, 1)

            def final(b, c):
                f = 2 * b + c
                act.wait_ge(fin_full, f + 1)
                if f >= 1:
                    act.wait_ge(*acc_done(4 * CAUSAL + f - 1))
                act.activation(hbuf[:, 0, :], T[:, :], ACT.Copy).then_inc(fin_ready, 1)

            act.wait_ge(w1_ready, 1)
            act.activation(w1h[:, :], w1f[:, :], ACT.Copy).then_inc(w1_hi, 1)
            ln(0)
            act.wait_ge(a_loaded, 32)
            act.activation(wh[:, :], raw_a, ACT.Copy).then_inc(hi_ready, 1)
            act.wait_ge(g_loaded, 32)
            act.activation(gh[:, :], raw_g, ACT.Copy).then_inc(hi_ready, 1)
            act.activation(vh[:, :], raw_u, ACT.Copy).then_inc(hi_ready, 1)
            ffn(FFN0)
            linear(0)
            linear(1)
            ln(8)
            ffn(FFN1)
            moe(MOE0)
            causal()
            moe(MOE1)

        @block.vector
        def _(dve):
            chain = [0]

            def link(ins):
                chain[0] += 1
                ins.then_inc(dch, 1)
                dve.wait_ge(dch, chain[0])

            def norm(L):
                p, c = divmod(L, 4)
                r = L % 2
                if p == 0:
                    dve.wait_ge(x_loaded[c], 16)
                else:
                    dve.wait_ge(x_ready, L - 3)
                for t in range(CT):
                    ins = dve.bn_stats(stats[:, t, :], x[:, c * CT + t, :])
                link(ins)
                for t in range(CT):
                    ins = dve.bn_aggr(mv[:, r, t, :], stats[:, t, :])
                ins.then_inc(stats_ready, 1)
                dve.wait_ge(rstd_ready, L + 1)
                dve.wait_ge(stats_ready, L + 1)
                if L >= 2:
                    dve.wait_ge(ln_t, L - 1)
                for t in range(CT):
                    ins = dve.tensor_scalar(hn[:, r, t, :], x[:, c * CT + t, :], mv[:, r, t, 0:1],
                                            rs[:, r, 2 if p in FFNS else 0, t:t + 1], ALU.subtract, ALU.mult)
                ins.then_inc(norm_ready, 1)
                if p in FFNS:
                    for t in range(CT):
                        ins = dve.tensor_scalar(ub[:, t, :], x[:, c * CT + t, :], mv[:, r, t, 0:1],
                                                rs[:, r, 0, t:t + 1], ALU.subtract, ALU.mult)
                    link(ins)
                    xc = x[:, c * CT:(c + 1) * CT, :]
                    dve.scalar_tensor_tensor(out=xc, in0=ub[:, :, :], scalar=0.5, in1=xc,
                                             op0=ALU.mult, op1=ALU.add).then_inc(ub_ready, 1)

            def split(L):
                p, c = divmod(L, 4)
                dve.wait_ge(ft_ready, L + 1)
                src = ft[:, :]
                if p == LIN:
                    src = uf[:, c // 2, 1 + (c % 2) * CW:1 + (c % 2 + 1) * CW]
                link(dve.tensor_copy(uh[:, tok(c)], src))
                dve.tensor_tensor(ul[:, tok(c)], src, uh[:, tok(c)].bitcast(F32), ALU.subtract)\
                    .then_inc(split_ready, 1)

            def update(L, scale):
                c = L % 4
                dve.wait_ge(*acc_done(L))
                if L < 12:
                    dve.wait_ge(xadd_ready, L + 1)
                xc = x[:, c * CT:(c + 1) * CT, :]
                dve.scalar_tensor_tensor(out=xc, in0=ACC[:, :].rearrange("p (t d) -> p t d", t=CT), scalar=scale,
                                         in1=xc, op0=ALU.mult, op1=ALU.add).then_inc(x_ready, 1)

            def ffn(p):
                for c in range(NC):
                    split(4 * p + c + 1)
                    norm(4 * p + c + 2)
                    update(4 * p + c, 0.25)

            def linear(b):
                if b == 1:
                    split(4 * LIN + 2)
                split(4 * LIN + 2 * b + 1)
                norm(4 * LIN + 2 * b + 2)
                norm(4 * LIN + 2 * b + 3)
                for c in range(2):
                    n = 2 * b + c
                    dve.wait_ge(eq_ready, n + 1)
                    dve.scalar_tensor_tensor(out=qf[:, tok(c)], in0=bank[1 + c][:, :], scalar=0.0, in1=neg[:, 1, :],
                                             op0=ALU.max, op1=ALU.add).then_inc(qf_ready, 1)
                for t in range(4):
                    n = 4 * b + t
                    dve.wait_ge(ek_ready, n + 1)
                    kvp = bank[3 + t % 2][:, :].rearrange("p (t n) -> p t n", t=2)
                    n1 = neg[:, 1, 0:2 * D].rearrange("p (t n) -> p t n", t=2)
                    dve.scalar_tensor_tensor(out=kf[:, 2 * t:2 * t + 2, :], in0=kvp[:, :, 0:D], scalar=0.0, in1=n1,
                                             op0=ALU.max, op1=ALU.add)
                    dve.tensor_copy(vx[:, 2 * t:2 * t + 2, 0:D], kvp[:, :, D:2 * D]).then_inc(kv_ready, 1)
                u = uf[:, b, :]
                link(dve.tensor_scalar(loc, u[:, 0:S], small[:, S_CW:S_CW + 1], small[:, S_CB:S_CB + 1],
                                       ALU.mult, ALU.add))
                for w in range(1, 3):
                    link(dve.scalar_tensor_tensor(out=loc, in0=u[:, w:w + S],
                                                  scalar=small[:, S_CW + w:S_CW + w + 1], in1=loc,
                                                  op0=ALU.mult, op1=ALU.add))
                dve.wait_ge(s_full, b + 1)
                sv = bank[5]
                dve.tensor_tensor(kx[:, 0:P], sv[:, 0:P], bmask[:, 0:P], ALU.mult)
                dve.tensor_scalar(kx[:, P:P + H], bmask[:, P:P + H], sv[:, P:P + 1], None, ALU.mult)\
                    .then_inc(kx_ready, 1)
                for t in range(4):
                    n = 4 * b + t
                    dve.wait_ge(o_full, n + 1)
                    ov = bank[1 + t][:, :].rearrange("p (t n) -> p t n", t=2)
                    link(dve.tensor_scalar(den[:, t % 2, :, :], ov[:, :, P:P + H], 1e-6, None, ALU.max))
                    link(dve.reciprocal(rden[:, t % 2, :, :], den[:, t % 2, :, :]))
                    if t >= 2:
                        dve.wait_ge(yt_full, n - 1)
                    for e in range(2):
                        ins = dve.tensor_tensor(
                            yt[:, t % 2, e, :].rearrange("p (h d) -> p h d", h=H),
                            ov[:, e, 0:P].rearrange("p (h d) -> p h d", h=H),
                            rden[:, t % 2, e, :].unsqueeze(2).to_broadcast([P, H, HD]), ALU.mult)
                    ins.then_inc(yt_ready, 1)
                    if t >= 1:
                        add_local(b, t - 1)
                add_local(b, 3)
                if b == 1:
                    split(8)

            def add_local(b, t):
                n = 4 * b + t
                dve.wait_ge(yt_full, n + 1)
                cols = slice(t * 2 * P, (t + 1) * 2 * P)
                dve.tensor_tensor(mix[:, cols], bank[5 + t % 2][:, 256:512], loc[:, cols], ALU.add)\
                    .then_inc(mix_ready, 1)
                if t % 2:
                    update(4 * LIN + 2 * b + t // 2, 1.0)

            def route(r):
                dve.wait_ge(lg_full, r + 1)
                if r >= 1:
                    dve.wait_ge(cs_ready, r)
                lv = T[:, 0:CT * 32].rearrange("p (t n) -> p t n", t=CT)
                dve.tensor_copy(dd[:, 1, :], lv[:, :, E_])
                dve.tensor_copy(lg[:, :, :], lv[:, :, 0:NR + 1]).then_inc(lg_ready, 1)
                dve.wait_ge(lg_ready, r + 1)
                for t in range(CT):
                    ins = dve.max(m8[:, t, :], lg[:, t, 0:E_])
                link(ins)
                for t in range(CT):
                    dve.max_index(ix[:, t, :], m8[:, t, :], lg[:, t, 0:E_])
                dve.tensor_tensor(dd[:, 0, :], m8[:, :, 0], m8[:, :, 1], ALU.subtract).then_inc(dd_ready, 1)

            def weigh(r):
                dve.wait_ge(dd_ready, r + 1)
                dve.tensor_copy(ixf[:, :, :], ix[:, :, 0:2])
                dve.wait_ge(th_ready, r + 1)
                dve.tensor_scalar(tw[:, 0, :], th[:, 0, :], 0.5, 0.5, ALU.mult, ALU.add)
                dve.tensor_scalar(cw[:, :, E_], th[:, 1, :], 0.5, 0.5, ALU.mult, ALU.add)
                link(dve.tensor_scalar(tw[:, 1, :], th[:, 0, :], -0.5, 0.5, ALU.mult, ALU.add))
                io = iota[:, :].unsqueeze(1).to_broadcast([P, CT, E_])
                for a in range(2):
                    ins = dve.tensor_tensor(oh[:, a, :, :], io, ixf[:, :, a].unsqueeze(2).to_broadcast([P, CT, E_]),
                                            ALU.is_equal)
                link(ins)
                for a in range(2):
                    ins = dve.tensor_tensor(oh[:, a, :, :], oh[:, a, :, :],
                                            tw[:, a, :].unsqueeze(2).to_broadcast([P, CT, E_]), ALU.mult)
                link(ins)
                link(dve.tensor_tensor(cw[:, :, 0:E_], oh[:, 0, :, :], oh[:, 1, :, :], ALU.add))
                link(dve.tensor_copy(cs[:, :, 0, :], cw[:, :, :]))
                link(dve.tensor_tensor(cr[:, 0, :, :], cw[:, :, :], cs[:, :, 0, :], ALU.subtract))
                link(dve.tensor_copy(cs[:, :, 1, :], cr[:, 0, :, :]))
                dve.tensor_tensor(cs[:, :, 2, :], cr[:, 0, :, :], cs[:, :, 1, :], ALU.subtract).then_inc(cs_ready, 1)

            def moe(p):
                r0 = 4 if p == MOE1 else 0
                route(r0)
                weigh(r0)
                for n in range(NC * NU):
                    c, u = divmod(n, NU)
                    m = n + (NC * NU if p == MOE1 else 0)
                    L = 4 * p + c
                    dve.wait_ge(sg_ready, m + 1)
                    link(dve.tensor_tensor(su[:, m % 2, :], sg[:, m % 2, :], bank[3 + m % 2][:, :], ALU.mult))
                    if m >= 3:
                        dve.wait_ge(down_done, 32 + m - 2)
                    dve.tensor_tensor(hbuf[:, m % 3, :], su[:, m % 2, :], bank[5 + m % 2][:, :], ALU.mult)\
                        .then_inc(hm_ready, 1)
                    if u == 1 and c > 0:
                        update(L - 1, 0.5)
                    if u == 1 and L + 1 < 24:
                        split(L + 1)
                    if u == 2 and L + 2 < 24:
                        norm(L + 2)
                    if c < 3 and u == 4:
                        route(r0 + c + 1)
                    if c < 3 and u == 5:
                        weigh(r0 + c + 1)
                update(4 * p + 3, 0.5)

            def tile(b, i):
                n = TB * b + i
                dve.wait_ge(qkv_ready, n + 1)
                dve.wait_ge(stg_clear, 1)
                if n >= 1:
                    dve.wait_ge(stg_lo, n)
                s = stg[:, n % 2, :, :]
                qk = qkv[:, n % 2, 0:2 * D].rearrange("p (h d) -> p h d", d=HD)
                cos = rope[:, 0, i, :].unsqueeze(1).to_broadcast([P, 2 * H, HD])
                dve.tensor_tensor(ra[:, :, :], qk, cos, ALU.mult)
                hh = HD // 2
                for a in range(2):
                    src = slice((1 - a) * hh, (2 - a) * hh)
                    dst = slice(a * hh, (a + 1) * hh)
                    sin = rope[:, 1, i, dst].unsqueeze(1).to_broadcast([P, 2 * H, hh])
                    ins = dve.tensor_tensor(rb[:, :, dst], qk[:, :, src], sin, ALU.mult)
                link(ins)
                link(dve.tensor_tensor(ra[:, :, :], ra[:, :, :], rb[:, :, :], ALU.add))
                if n >= 2:
                    dve.wait_ge(kt_full, 2 * n - 2)
                dve.tensor_copy(s[:, :, 0:HD], ra[:, :, :]).then_inc(stg_hi, 1)
                dve.wait_ge(stg_hi, n + 1)
                sf = s.bitcast(F32)
                dve.tensor_tensor(s[:, 0:H, 2 * HD:3 * HD], ra[:, 0:H, :], sf[:, 0:H, 0:HD], ALU.subtract)
                dve.tensor_tensor(s[:, H:, HD:2 * HD], ra[:, H:, :], sf[:, H:, 0:HD], ALU.subtract)\
                    .then_inc(stg_lo, 1)

            def maxima(s, half):
                n = 2 * s + half
                b, g = divmod(s, G)
                t0 = half * CT
                dve.wait_ge(a_free, s * NBLK * GH + (4 if half == 0 else NBLK) * GH)
                m = mx[:, s % 2, t0:t0 + CT, :, 0]
                if half:
                    link(dve.tensor_tensor(mm8[:, :, :], m, mx[:, s % 2, t0:t0 + CT, :, 1], ALU.max))
                    m = mm8[:, :, :]
                if n >= 2:
                    dve.wait_ge(mx_full, n - 1)
                    dve.wait_ge(stm_ready, n - 1)
                st = stm[:, half, :, :, :]
                link(dve.tensor_scalar(st[:, :, :, 3 * HD], m, -1.0, None, ALU.mult))
                dve.scalar_tensor_tensor(out=st[:, :, :, 3 * HD + 1], in0=m, scalar=-1.0,
                                         in1=st[:, :, :, 3 * HD].bitcast(F32), op0=ALU.mult, op1=ALU.subtract)\
                    .then_inc(stm_ready, 1)
                dve.wait_ge(mx_full, n + 1)
                dve.tensor_tensor(qtb[:, s % 2, tok(half)], T[:, :], qta[:, b, g, tok(half)].bitcast(F32), ALU.add)\
                    .then_inc(qtb_ready, 1)

            def yout(s, c):
                n = 2 * s + c
                b, g = divmod(s, G)
                dve.wait_ge(yo_full, n + 1)
                if n >= 1:
                    dve.wait_ge(y_norm, n)
                v = T[:, :].rearrange("p (t h d) -> p t h d", t=CT, h=GH)
                if b:
                    dve.wait_ge(fin_full, c + 1)
                link(dve.reciprocal(yrec[:, :, :], v[:, :, :, HD]))
                dst = ytok[:, c * CT:(c + 1) * CT, g * GH * HD:(g + 1) * GH * HD]
                dve.tensor_tensor(dst.rearrange("p t (h d) -> p t h d", h=GH), v[:, :, :, 0:HD],
                                  yrec[:, :, :].unsqueeze(3).to_broadcast([P, CT, GH, HD]), ALU.mult)\
                    .then_inc(y_norm, 1)

            def causal():
                split(17)
                norm(18)
                for i in range(TB):
                    tile(0, i)
                norm(19)
                for s in range(-1, STEPS):
                    for k in range(NBLK):
                        if s + 1 < STEPS:
                            i, half = A_BLOCKS[k]
                            w = min(CW, (i + 1) * P - half * CW)
                            for h in range(GH):
                                n = ((s + 1) * NBLK + k) * GH + h
                                dve.wait_ge(a_full, n + 1)
                                dve.tensor_reduce(mx[:, (s + 1) % 2, i, h, half:half + 1],
                                                  bank[4 + n % 2][:, 0:w], AX.X, ALU.max).then_inc(a_free, 1)
                        for todo in extras(s, k):
                            if todo[0] == "ln":
                                split(todo[1])
                            if todo[0] == "norm":
                                norm(todo[1])
                            if todo[0] == "tile":
                                tile(*todo[1:])
                            if todo[0] == "max":
                                maxima(*todo[1:])
                            if todo[0] == "yout":
                                yout(*todo[1:])
                            if todo[0] == "final":
                                b, c = todo[1:]
                                update(4 * CAUSAL + 2 * b + c, 1.0)
                yout(STEPS - 1, 1)
                update(4 * CAUSAL + 3, 1.0)

            dve.wait_ge(q_loaded, 32)
            dve.tensor_scalar(w1f[:, :], raw_q[:, 0, :], -128.0, None, ALU.add).then_inc(w1_ready, 1)
            norm(0)
            dve.wait_ge(w1_hi, 1)
            dve.tensor_tensor(w1l[:, :], w1f[:, :], w1h[:, :].bitcast(F32), ALU.subtract).then_inc(w2_ready, 1)
            dve.wait_ge(small_loaded, 32)
            dve.scalar_tensor_tensor(out=w2[:, :, :].rearrange("p k n -> p (k n)"), in0=raw_q[:, 1, :], scalar=-128.0,
                                     in1=rows[:, R_S2:R_S2 + F], op0=ALU.add, op1=ALU.mult).then_inc(w2_ready, 1)
            split(0)
            norm(1)
            ffn(FFN0)
            dve.wait_ge(prep, 3)
            dve.wait_ge(consts, 3)
            dve.memset(uf[:, :, 0:1], 0.0)
            dve.memset(uf[:, :, S + 1:S + 2], 0.0)
            link(dve.memset(vx[:, :, D:D + 1], 1.0))
            linear(0)
            linear(1)
            ffn(FFN1)
            moe(MOE0)
            causal()
            moe(MOE1)

        @block.tensor
        def _(pe):
            drain = [None]

            def t_take(drained, value):
                if drain[0]:
                    pe.wait_ge(*drain[0])
                drain[0] = (drained, value)

            def mm3(dst, ah, al, bh, bl, start=True, stop=True):
                pe.matmul(dst, ah, bl, start=start, stop=False)
                pe.matmul(dst, al, bh, start=False, stop=False)
                return pe.matmul(dst, ah, bh, start=False, stop=stop)

            def ln(L):
                pe.wait_ge(norm_ready, L + 1)
                t_take(ft_ready, L + 1)
                for t in range(CT):
                    ins = pe.transpose(T[:, t * P:(t + 1) * P], hn[:, L % 2, t, :], ident[:, :])
                ins.then_inc(ln_t, 1)

            def acc_take(L):
                if L:
                    pe.wait_ge(x_ready, L)

            def ffn(p):
                if p:
                    pe.wait_ge(x_ready, 4 * p)
                for n in range(NC * FB + 2):
                    if n < NC * FB:
                        c, k = divmod(n, FB)
                        m = n + (16 if p == FFN1 else 0)
                        if k == 0:
                            pe.wait_ge(split_ready, 4 * p + c + 1)
                        if n >= 4:
                            pe.wait_ge(h_ready, m - 3)
                        f = slice(k * P, (k + 1) * P)
                        mm3(bank[1 + m % 4][:, :], w1h[:, f], w1l[:, f], uh[:, tok(c)], ul[:, tok(c)])\
                            .then_inc(y_full, 1)
                        if k == 1:
                            ln(4 * p + c + 1)
                    if n >= 2:
                        c, k = divmod(n - 2, FB)
                        m = n - 2 + (16 if p == FFN1 else 0)
                        if k == 0:
                            acc_take(4 * p + c)
                        pe.wait_ge(h_ready, m + 1)
                        for t in range(CT):
                            ins = pe.matmul(ACC[:, t * P:(t + 1) * P], hbuf[:, m % 4, t * P:(t + 1) * P], w2[:, k, :],
                                            start=(k == 0 and t == 0), stop=(k == FB - 1), skip_group_check=True)
                        ins.then_inc(down_done, 1)

            def linear(b):
                if b == 1:
                    ln(4 * LIN + 2)
                ln(4 * LIN + 2 * b + 1)
                pe.wait_ge(x_ready, 4 * LIN + 2 * b)
                pe.wait_ge(split_ready, 4 * LIN + 2 * b + 2)
                pe.wait_ge(prep, 1)
                for c in range(2):
                    mm3(bank[1 + c][:, :], wh[:, W_Q:W_Q + P], wl[:, W_Q:W_Q + P],
                        uh[:, tok(2 * b + c)], ul[:, tok(2 * b + c)]).then_inc(q_full, 1)
                for t in range(4):
                    if t >= 2:
                        pe.wait_ge(kv_ready, 4 * b + t - 1)
                    for e in range(2):
                        i = TB * b + 2 * t + e
                        ins = mm3(bank[3 + t % 2][:, e * 256:(e + 1) * 256], uh[:, i * P:(i + 1) * P],
                                  ul[:, i * P:(i + 1) * P], wh[:, W_KV:W_KV + 2 * P], wl[:, W_KV:W_KV + 2 * P])
                    ins.then_inc(kv_full, 1)
                for i in range(TB):
                    pe.wait_ge(kv_ready, 4 * b + i // 2 + 1)
                    ins = pe.matmul(bank[5][:, 0:D + 1], kf[:, i, :], vx[:, i, :], start=(i == 0), stop=(i == TB - 1))
                ins.then_inc(s_full, 1)
                pe.wait_ge(kx_ready, b + 1)
                pe.wait_ge(qf_ready, 2 * b + 2)
                for t in range(4):
                    for e in range(2):
                        i = 2 * t + e
                        ins = pe.matmul(bank[1 + t][:, e * 256:e * 256 + P + H], qf[:, i * P:(i + 1) * P], kx[:, :],
                                        start=True, stop=True)
                    ins.then_inc(o_full, 1)
                for t in range(4):
                    pe.wait_ge(yt_ready, 4 * b + t + 1)
                    if t >= 2:
                        pe.wait_ge(mix_ready, 4 * b + t - 1)
                    for e in range(2):
                        ins = pe.transpose(bank[5 + t % 2][:, 256 + e * P:256 + (e + 1) * P], yt[:, t % 2, e, :],
                                           ident[:, :])
                    ins.then_inc(yt_full, 1)
                    if t >= 1:
                        project(b, t - 1)
                project(b, 3)
                if b == 1:
                    ln(8)

            def project(b, t):
                pe.wait_ge(mix_ready, 4 * b + t + 1)
                pe.wait_ge(a_loaded, 32)
                L = 4 * LIN + 2 * b + t // 2
                if t % 2 == 0:
                    acc_take(L)
                for e in range(2):
                    i = 2 * t + e
                    ins = pe.matmul(ACC[:, (i % 4) * P:(i % 4 + 1) * P], mix[:, i * P:(i + 1) * P], wp[:, 0, :],
                                    start=True, stop=True)
                if t % 2:
                    ins.then_inc(acc_ready, 1)

            def route(L, r):
                pe.wait_ge(split_ready, L + 1)
                t_take(lg_ready, r + 1)
                c = L % 4
                for t in range(CT):
                    i = c * CT + t
                    ins = mm3(T[:, t * 32:t * 32 + NR + 1], uh[:, i * P:(i + 1) * P], ul[:, i * P:(i + 1) * P],
                              wh[:, W_R:W_END], wl[:, W_R:W_END])
                ins.then_inc(lg_full, 1)

            def weights(r):
                pe.wait_ge(cs_ready, r + 1)
                t_take(cwt_ready, r + 1)
                tb = T[0:3 * NR, 0:CW // 2].bitcast(BF16)
                for t in range(CT):
                    ins = pe.transpose(tb[:, t * P:(t + 1) * P], cs[:, t, :, :].rearrange("p a n -> p (a n)"),
                                       identb[:, :])
                ins.then_inc(cw_full, 1)

            def moe(p):
                r0 = 4 if p == MOE1 else 0
                m0 = NC * NU if p == MOE1 else 0
                route(4 * p, r0)
                weights(r0)
                pe.wait_ge(x_ready, 4 * p)
                if p == MOE0:
                    pe.wait_ge(prep, 3)
                    pe.wait_ge(dw_loaded, 16)
                for n in range(NC * NU + 2):
                    if n < NC * NU:
                        c, u = divmod(n, NU)
                        m = m0 + n
                        L = 4 * p + c
                        if u == 0:
                            pe.wait_ge(split_ready, L + 1)
                            pe.wait_ge(cwt_ready, r0 + c + 1)
                        if n >= 2:
                            pe.wait_ge(hm_ready, m - 1)
                        f = slice(u * P, (u + 1) * P)
                        mm3(bank[1 + m % 2][:, :], gh[:, f], gl[:, f], uh[:, tok(c)], ul[:, tok(c)])
                        mm3(bank[3 + m % 2][:, :], vh[:, f], vl[:, f], uh[:, tok(c)], ul[:, tok(c)])
                        pe.matmul(bank[5 + m % 2][:, :], sel[:, u, :], cwt[:, (r0 + c) % 2, :], start=True, stop=True)\
                            .then_inc(g_full, 1)
                        if u == 1 and L + 1 < 24:
                            ln(L + 1)
                        if c < 3 and u == 4:
                            route(L + 1, r0 + c + 1)
                        if c < 3 and u == 8:
                            weights(r0 + c + 1)
                    if n >= 2:
                        c, u = divmod(n - 2, NU)
                        m = m0 + n - 2
                        if u == 0:
                            acc_take(4 * p + c)
                        pe.wait_ge(hm_ready, m + 1)
                        for t in range(CT):
                            ins = pe.matmul(ACC[:, t * P:(t + 1) * P], hbuf[:, m % 3, t * P:(t + 1) * P], dw[:, u, :],
                                            start=(u == 0 and t == 0), stop=(u == NU - 1), skip_group_check=True)
                        ins.then_inc(down_done, 1)

            def tile(b, i):
                n = TB * b + i
                t = n
                pe.wait_ge(split_ready, 4 * CAUSAL + t // CT + 1)
                if n >= 1:
                    pe.wait_ge(qkv_ready, n)
                mm3(bank[7][:, 0:3 * D], uh[:, t * P:(t + 1) * P], ul[:, t * P:(t + 1) * P],
                    wh[:, W_QKV:W_QKV + 3 * D], wl[:, W_QKV:W_QKV + 3 * D]).then_inc(qkv_full, 1)
                pe.wait_ge(stg_ready, n + 1)
                pe.wait_ge(stg_lo, n + 1)
                for which, first in enumerate((H, 0)):
                    t_take(kt_ready, 2 * n + which + 1)
                    for g in range(G):
                        ins = pe.transpose(T[:, g * P:(g + 1) * P].bitcast(F32R),
                                           stg[:, n % 2, first + g * GH:first + (g + 1) * GH, :]
                                           .rearrange("p h d -> p (h d)"), identr[:, :])
                    ins.then_inc(kt_full, 1)

            def maxima(s, half):
                n = 2 * s + half
                pe.wait_ge(stm_ready, n + 1)
                t_take(qtb_ready, n + 1)
                for t in range(CT):
                    ins = pe.transpose(T[:, t * P:(t + 1) * P].bitcast(F32R),
                                       stm[:, half, t, :, :].rearrange("p h d -> p (h d)"), identr[:, :])
                ins.then_inc(mx_full, 1)

            def sums(blk):
                s, k = divmod(blk, NBLK)
                c, j = B_BLOCKS[k]
                b, g = divmod(s, G)
                w = min(CW, CW * (c + 1) - j * P)
                pe.wait_ge(p_ready, GH * (blk + 1))
                pe.wait_ge(v_ready, TB * (b + 1))
                if j == 0 and 2 * s + c:
                    pe.wait_ge(ysb_ready, 2 * s + c)
                for h in range(GH):
                    ins = pe.matmul(bank[6][h * SL:h * SL + HD + 1, CW - w:CW], va[:, b, j, g * GH + h, :],
                                    pb[:, blk % 3, h, 0:w], start=(j == 0), stop=True,
                                    skip_group_check=True)
                ins.then_inc(pv_done, 1)

            def yout(s, c):
                n = 2 * s + c
                pe.wait_ge(ysb_ready, n + 1)
                t_take(y_norm, n + 1)
                for t in range(CT):
                    ins = pe.transpose(T[:, t * P:(t + 1) * P], ysb[:, n % 2, t * P:(t + 1) * P], ident[:, :])
                ins.then_inc(yo_full, 1)

            def final(b, c):
                f = 2 * b + c
                pe.wait_ge(y_norm, 2 * (G * b + G - 1) + c + 1)
                t_take(fin_ready, f + 1)
                for t in range(CT):
                    ins = pe.transpose(T[:, t * P:(t + 1) * P], ytok[:, c * CT + t, :], ident[:, :])
                ins.then_inc(fin_full, 1)
                acc_take(4 * CAUSAL + f)
                pe.wait_ge(fin_ready, f + 1)
                for t in range(CT):
                    ins = pe.matmul(ACC[:, t * P:(t + 1) * P], hbuf[:, 0, t * P:(t + 1) * P], wp[:, 1, :],
                                    start=True, stop=True)
                ins.then_inc(acc_ready, 1)

            def causal():
                ln(17)
                pe.wait_ge(x_ready, 4 * CAUSAL)
                for i in range(TB):
                    tile(0, i)
                for s in range(-1, STEPS):
                    for k, (c, j) in enumerate(B_BLOCKS):
                        i, half = A_BLOCKS[k]
                        for h in range(GH):
                            r = slice(h * SL, (h + 1) * SL)
                            if s >= 0:
                                b, g = divmod(s, G)
                                n = (s * NBLK + k) * GH + h
                                w = min(CW, CW * (c + 1) - j * P)
                                dst = bank[1 + n % 3]
                                if h == 0:
                                    pe.wait_ge(qtb_ready, 2 * s + c + 1)
                                if n >= 3:
                                    pe.wait_ge(p_ready, n - 2)
                                diag = j >= 4 * c
                                ins = pe.matmul(dst[:, 0:w], kt[r, b, g, j * P:(j + 1) * P],
                                                qtb[r, s % 2, (c + 1) * CW - w:(c + 1) * CW],
                                                start=True, stop=True)
                                if diag:
                                    ins = pe.matmul(dst[:, 0:P], identb[:, :], masks[:, 1, :], start=False, stop=True,
                                                    skip_group_check=True)
                                ins.then_inc(b_full, 1)
                            if s + 1 < STEPS:
                                b, g = divmod(s + 1, G)
                                n = ((s + 1) * NBLK + k) * GH + h
                                w = min(CW, (i + 1) * P - half * CW)
                                dst = bank[4 + n % 2]
                                if h == 0 and g == 0:
                                    pe.wait_ge(kt_ready, 2 * TB * (b + 1))
                                if n >= 2:
                                    pe.wait_ge(a_free, n - 1)
                                diag = i * P < half * CW + w
                                ins = pe.matmul(dst[:, 0:w], qta[r, b, g, i * P:(i + 1) * P],
                                                kt[r, b, g, half * CW:half * CW + w], start=True, stop=True)
                                if diag:
                                    ins = pe.matmul(dst[:, w - P:w], identb[:, :], masks[:, 0, :], start=False,
                                                    stop=True, skip_group_check=True)
                                ins.then_inc(a_full, 1)
                        if s >= 0 and s * NBLK + k >= 1:
                            sums(s * NBLK + k - 1)
                        for todo in extras(s, k):
                            if todo[0] == "ln":
                                ln(todo[1])
                            if todo[0] == "tile":
                                tile(*todo[1:])
                            if todo[0] == "max":
                                maxima(*todo[1:])
                            if todo[0] == "yout":
                                yout(*todo[1:])
                            if todo[0] == "final":
                                final(*todo[1:])
                sums(STEPS * NBLK - 1)
                yout(STEPS - 1, 1)
                final(1, 1)

            pe.wait_ge(consts, 1)
            ln(0)
            pe.wait_ge(w2_ready, 2)
            ffn(FFN0)
            pe.wait_ge(consts, 3)
            linear(0)
            linear(1)
            ffn(FFN1)
            moe(MOE0)
            causal()
            moe(MOE1)


def constants():
    import numpy as np
    c = np.zeros((P, C_END), np.float32)
    r = np.arange(P)
    c[:, C_ID:C_ID + P] = np.eye(P)
    c[:, C_MA:C_MA + P] = np.where(r[None, :] > r[:, None], -1e30, 0.0)
    c[:, C_MB:C_MB + P] = np.where(r[:, None] > r[None, :], -1e30, 0.0)
    c[:, C_BM:C_BM + P] = r[:, None] // HD == r[None, :] // HD
    c[:, C_HS:C_HS + H] = r[:, None] // HD == np.arange(H)[None, :]
    c[:, C_IO:C_IO + E_] = np.arange(E_)
    half = HD // 2
    theta = np.float32(1.0) / np.float32(10000.0) ** (np.arange(half, dtype=np.float32) / np.float32(half))
    freqs = np.arange(S, dtype=np.float32)[:, None] * theta[None, :].astype(np.float32)
    freqs = np.repeat(freqs, 2, axis=-1).astype(np.float64)
    sign = np.where(np.arange(HD) < half, -1.0, 1.0)
    c[:, C_COS:C_COS + TB * HD] = np.cos(freqs).reshape(TB, P, HD).transpose(1, 0, 2).reshape(P, -1)
    c[:, C_SIN:C_SIN + TB * HD] = (np.sin(freqs) * sign).reshape(TB, P, HD).transpose(1, 0, 2).reshape(P, -1)
    for u in range(NU):
        for f in range(P):
            e = 2 * u + f // FE if u < E_ // 2 else E_
            for part in range(3):
                c[part * NR + e, C_SEL + u * P + f] = 1.0
    return c


def kernel(**inputs):
    import numpy as np
    import concourse.bacc as bacc
    from concourse import mybir as mb
    from concourse.bass_utils import run_bass_kernel_spmd as run

    v = {n: np.asarray(a) for n, a in inputs.items()}
    cat = np.concatenate

    def blocks(a):
        k = a.shape[0] // P
        return a.reshape(k, P, -1).transpose(1, 0, 2).reshape(P, -1)

    def experts(w, shared):
        return cat([w.transpose(1, 0, 2).reshape(D, -1), shared], 1)

    f0 = "L0_ffn_"
    m = "L1_ffn_"
    arrays = {
        "x_in": v["L0_attn_x"].reshape(B * S, D),
        "wa_in": cat([v["L0_attn_Wq"].T, v["L0_attn_Wk"].T, v["L0_attn_Wv"].T, v["L1_attn_w_qkv"],
                      v[m + "router_w"].T, v[m + "shared_gate_w"], np.zeros((D, 1), np.float32)], 1),
        "wp_in": cat([v["L0_attn_Wp"].T, v["L1_attn_w_proj"]], 1),
        "gw_in": experts(v[m + "Wg"], v[m + "Sg"]),
        "uw_in": experts(v[m + "Wu"], v[m + "Su"]),
        "dw_in": blocks(cat([v[m + "Wd"].reshape(-1, D), v[m + "Sd"]], 0)),
        "q1_in": v[f0 + "fc1_q"],
        "q2_in": blocks(v[f0 + "fc2_q"]),
        "small_in": cat([v[f0 + "fc1_scales"].reshape(FB, P).T, v[f0 + "fc1_bias"].reshape(FB, P).T,
                         v[f0 + "ln_gamma"][:, None], v[f0 + "ln_beta"][:, None],
                         v["L0_attn_conv_w"], v["L0_attn_conv_b"][:, None]], 1),
        "rows_in": cat([v[f0 + "fc2_bias"], v["L0_attn_bp"], v[f0 + "fc2_scales"].reshape(-1)])[None, :],
        "const_in": constants(),
    }
    arrays = {n: np.ascontiguousarray(a) for n, a in arrays.items()}
    nc = bacc.Bacc("TRN2", target_bir_lowering=False, num_devices=1)
    args = [nc.dram_tensor(n, a.shape, mb.dt.from_np(a.dtype), kind="ExternalInput").ap() for n, a in arrays.items()]
    out = nc.dram_tensor("y_out", (B, S, D), mb.dt.float32, kind="ExternalOutput").ap()
    macaron(nc, *args, out)
    r = run(nc, [arrays], core_ids=[0])
    return r.results[0]["y_out"]
```

```python
import concourse.bass as bass
from concourse import mybir
from contextlib import ExitStack

F32 = mybir.dt.float32
F32R = mybir.dt.float32r
BF16 = mybir.dt.bfloat16
I32 = mybir.dt.int32
U32 = mybir.dt.uint32
ALU = mybir.AluOpType
ACT = mybir.ActivationFunctionType
AX = mybir.AxisListType

P = 128
D = 128
B, S = 2, 1024
TILES = B * S // P
CT = 4
CW = CT * P
NC = TILES // CT
H, HD = 16, 8
F = 512
FB = F // P
E_, FE, FS = 16, 64, 256
NU = E_ * FE // P + FS // P
NR = E_ + 1
EPS = 1e-5
TB = S // P
G, GH = 4, 4
SL = 32
SCALE = HD ** -0.5
FFN0, LIN, FFN1, MOE0, CAUSAL, MOE1 = range(6)
FFNS = (FFN0, FFN1)
MOES = (MOE0, MOE1)
W_Q, W_KV, W_QKV, W_R, W_END = 0, 128, 384, 768, 786
C_ID, C_MA, C_MB, C_BM, C_HS, C_IO, C_COS, C_SIN, C_SEL = 0, 128, 256, 384, 512, 528, 544, 608, 672
C_END = C_SEL + NU * P
S_S1, S_B1, S_GA, S_BE, S_CW, S_CB, S_END = 0, 4, 8, 9, 10, 13, 14
R_B2, R_BP, R_S2, R_END = 0, 128, 256, 768

B_BLOCKS = [(c, j) for c in range(2) for j in range(4 * c + 4)]
A_BLOCKS = [(3, 0), (2, 0), (1, 0), (0, 0), (4, 0), (5, 0), (6, 0), (7, 0), (7, 1), (6, 1), (5, 1), (4, 1)]
NBLK = len(B_BLOCKS)
STEPS = B * G


def schedule():
    at = {}

    def put(engine, s, k, stage, *args):
        s, k = s + k // NBLK, k % NBLK
        at.setdefault((engine, s, k), []).append((stage, *args))

    for t in range(TB + 1):
        for engine in ("pe", "act"):
            if t < TB:
                put(engine, 1, 3 * t, "qkv", 1, t)
            if t:
                put(engine, 1, 3 * t + 1, "parts", 1, t - 1, 0)
                put(engine, 1, 3 * t + 2, "parts", 1, t - 1, 1)
    for s in range(-1, STEPS + 1):
        if s + 1 < STEPS:
            for half, k in ((0, 4), (1, 12)):
                put("dve", s, k, "negate", s + 1, half)
                put("pe", s, k + 1, "max", s + 1, half)
                put("dve", s, k + 2, "add", s + 1, half)
        if 0 <= s < STEPS:
            for c, k in ((0, 5), (1, 13)):
                last = s == STEPS - 1 and c == 1
                if last:
                    continue
                put("act", s, k, "yraw", s, c)
                put("pe", s, k + 2, "yout", s, c)
                put("dve", s, k + 3, "yout", s, c)
                if s % G == G - 1:
                    put("pe", s, k + 4, "final", s // G, c)
                    put("act", s, k + 4, "final", s // G, c)
                    put("pe", s, k + 5, "project", s // G, c)
                    put("dve", s, k + 6, "update", 4 * CAUSAL + 2 * (s // G) + c)
    for L, k in ((18, 4), (19, 8)):
        for engine in ("pe", "act", "dve"):
            put(engine, -1, k, "ln", L)
    for t in range(TB):
        for engine in ("dve", "pool"):
            put(engine, 1, 3 * t + 1, "rope", 1, t)
    for s in range(2, STEPS):
        put("pool", s - 2, 7, "alone", s, 0)
        put("pool", s - 2, 15 if s == G else 11, "alone", s, 1)
    for L, k in ((20, 7), (21, 10)):
        put("dve", 4, k, "moments", L)
        put("pool", 4, k, "norm", L)
        put("dve", 4, k + 2, "norm", L)
    for engine in ("pe", "act", "dve"):
        put(engine, 7, 2, "ln", 20)
    put("pe", 7, 4, "route", 20)
    for engine in ("dve", "act"):
        put(engine, 7, 5, "route", 20)
    put("dve", 7, 6, "weigh", 20)
    for engine in ("pe", "act"):
        put(engine, 7, 9, "weights", 20)
    return at


HOOKS = schedule()


def macaron(nc, x_in, wa_in, wp_in, gw_in, uw_in, dw_in, q1_in, q2_in, small_in, rows_in, const_in, out):
    ctx = ExitStack()
    with ctx:
        def sb(name, shape, dt=F32):
            return ctx.enter_context(nc.sbuf_tensor(name, shape, dt))

        def sem(name):
            return ctx.enter_context(nc.semaphore(name))

        x = sb("x", [P, TILES, D])
        uh = sb("uh", [P, TILES * P], F32R)
        ul = sb("ul", [P, TILES * P], F32R)
        stats = sb("stats", [P, CT, 6])
        mv = sb("mv", [P, 2, CT, 2])
        rs = sb("rs", [P, 2, 3, CT])
        rtmp = sb("rtmp", [P, 2, CT])
        nhalf = sb("nhalf", [P, CT])
        hn = sb("hn", [P, 2, CT, D])
        ft = sb("ft", [P, CW])

        wh = sb("wh", [P, W_END], F32R)
        wl = sb("wl", [P, W_END], F32R)
        wp = sb("wp", [P, 2, P])
        late = sb("late", [P, 2 * 2 * H * SL], F32R)
        w1h, w1l = late[:, 0:F], late[:, F:2 * F]
        stg = late[:, :].rearrange("p (r h n) -> p r h n", r=2, h=2 * H)
        gh = sb("gh", [P, NU * P], F32R)
        gl = sb("gl", [P, NU * P], F32R)
        vh = sb("vh", [P, NU * P], F32R)
        vl = sb("vl", [P, NU * P], F32R)
        dw = sb("dw", [P, NU, D])
        small = sb("small", [P, S_END])
        bprow = sb("bprow", [P, D])
        b2q = sb("b2q", [P, D])
        identr = sb("identr", [P, P], F32R)
        ident = identr[:, :].bitcast(F32)
        identb = sb("identb", [P, P], BF16)
        mask_kq = sb("mask_kq", [P, P], BF16)
        mask_qk = sb("mask_qk", [P, CW], BF16)
        bmask = sb("bmask", [P, P + H])
        iota = sb("iota", [P, E_])
        rope = sb("rope", [P, 2, TB, HD])
        sel = sb("sel", [3 * NR, NU, P], BF16)

        VX = 2 * TB * H * (HD + 1)
        arena = sb("arena", [P, 2 * GH * CW + VX])
        work = sb("work", [P, 8 * CW])
        hbuf = work[:, 0:4 * CW].rearrange("p (r n) -> p r n", r=4)
        sg = work[:, 4 * CW:6 * CW].rearrange("p (r n) -> p r n", r=2)
        su = work[:, 6 * CW:8 * CW].rearrange("p (r n) -> p r n", r=2)
        ub = work[:, 4 * CW:5 * CW].rearrange("p (t d) -> p t d", t=CT)
        w2 = work[:, 5 * CW:6 * CW].rearrange("p (k d) -> p k d", k=FB)
        o = CW
        qkv = work[:, o:o + 6 * D].rearrange("p (r n) -> p r n", r=2); o += 6 * D
        ysb = work[:, o:o + 2 * CW].rearrange("p (r n) -> p r n", r=2); o += 2 * CW
        ytok = work[:, o:o + TB * D].rearrange("p (t d) -> p t d", t=TB); o += TB * D
        ra = work[:, o:o + 2 * D].rearrange("p (h d) -> p h d", d=HD); o += 2 * D
        rb = work[:, o:o + 2 * D].rearrange("p (h d) -> p h d", d=HD); o += 2 * D
        mx = work[:, o:o + 2 * TB * GH].rearrange("p (t h a) -> p t h a", t=TB, h=GH); o += 2 * TB * GH
        mm8 = work[:, o:o + CT * GH].rearrange("p (t h) -> p t h", t=CT); o += CT * GH
        yrec = work[:, o:o + CT * GH].rearrange("p (t h) -> p t h", t=CT); o += CT * GH
        assert o <= 8 * CW

        lg = sb("lg", [P, CT, NR + 1])
        m8 = sb("m8", [P, CT, 8])
        ix = sb("ix", [P, CT, 8], U32)
        ixf = sb("ixf", [P, CT, 2])
        dd = sb("dd", [P, 2, CT])
        th = sb("th", [P, 2, CT])
        tw = sb("tw", [P, 3, CT])
        oh = sb("oh", [P, 2, CT, E_])
        cw = sb("cw", [P, CT, NR])
        cr = sb("cr", [P, 2, CT, NR])
        cs = sb("cs", [P, CT, 3, NR], BF16)
        cwt = sb("cwt", [3 * NR, 2, CW], BF16)

        qta = sb("qta", [P, G + 2, S], F32R)
        kt = sb("kt", [P, G + 2, S], F32R)
        kza = [sb(f"kza{i}", [P, GH, CW], F32R) for i in range(3)]
        qtb = sb("qtb", [P, 2, S], F32R)
        stm = sb("stm", [P, 2, CT, GH, SL], F32R)

        raw_a = arena[:, 0:W_END]
        raw_c = arena[:, 1024:1024 + C_END]
        raw_g = arena[:, 3072:3072 + NU * P]
        raw_u = arena[:, 4352:4352 + NU * P]
        rows = arena[:, 5632:5632 + R_END]
        raw_q = work[:, 0:2 * F].bitcast(I32).rearrange("p (a n) -> p a n", a=2)
        w1f = work[:, 2 * F:3 * F]
        PADS = S + 2
        uf = arena[:, 0:2 * PADS].rearrange("p (b t) -> p b t", b=B)
        o = 2 * PADS
        qf = arena[:, o:o + S]; o += S
        kf = arena[:, o:o + S].rearrange("p (t d) -> p t d", t=TB); o += S
        vx = arena[:, o:o + TB * (D + 1)].rearrange("p (t d) -> p t d", t=TB); o += TB * (D + 1)
        relu = arena[:, o:o + 2 * CW].rearrange("p (r n) -> p r n", r=2); o += 2 * CW
        assert o <= 2 * GH * CW + VX
        loc = work[:, 6 * CW:6 * CW + S]
        yt = work[:, 0:4 * D].rearrange("p (r t d) -> p r t d", r=2, t=2)
        mix = loc
        expo = work[:, CW:3 * CW].rearrange("p (r n) -> p r n", r=2)
        o = CW + S
        kx = work[:, o:o + P + H]; o += P + H
        den = work[:, o:o + 4 * H].rearrange("p (r e h) -> p r e h", r=2, e=2); o += 4 * H
        rden = work[:, o:o + 4 * H].rearrange("p (r e h) -> p r e h", r=2, e=2)
        pb = arena[:, 0:2 * GH * CW].rearrange("p (r h n) -> p r h n", r=2, h=GH)
        va = arena[:, 2 * GH * CW:].rearrange("p (b t h d) -> p b t h d", b=B, t=TB, h=H)

        bank = [ctx.enter_context(nc.psum_tensor(f"bank{i}", [P, CW], F32)) for i in range(8)]
        T, ACC = bank[0], bank[7]

        x_loaded = [sem(f"x_loaded{c}") for c in range(NC)]
        q_loaded, small_loaded, a_loaded = sem("q_loaded"), sem("small_loaded"), sem("a_loaded")
        c_loaded, g_loaded = sem("c_loaded"), sem("g_loaded")
        dw_loaded, stored = sem("dw_loaded"), sem("stored")
        consts, w1_ready, w1_hi, w2_ready, prep = (
            sem("consts"), sem("w1_ready"), sem("w1_hi"), sem("w2_ready"), sem("prep"))
        hi_ready = sem("hi_ready")
        stats_ready, rstd_ready, norm_ready, xadd_ready = (
            sem("stats_ready"), sem("rstd_ready"), sem("norm_ready"), sem("xadd_ready"))
        ub_ready = sem("ub_ready")
        ln_t, ft_ready, split_ready = sem("ln_t"), sem("ft_ready"), sem("split_ready")
        lg_ready = sem("lg_ready")
        x_ready, acc_ready = sem("x_ready"), sem("acc_ready")
        dch, pch, ach = sem("dve_chain"), sem("pool_chain"), sem("act_chain")
        y_full, h_ready = sem("y_full"), sem("h_ready")
        g_full, sg_ready, hm_ready = sem("g_full"), sem("sg_ready"), sem("hm_ready")
        down_done = sem("down_done")
        lg_full, dd_ready, th_ready, cs_ready, cw_full, cwt_ready = (
            sem("lg_full"), sem("dd_ready"), sem("th_ready"), sem("cs_ready"), sem("cw_full"), sem("cwt_ready"))
        q_full, eq_ready, qf_ready = sem("q_full"), sem("eq_ready"), sem("qf_ready")
        kv_full, ek_ready, kv_ready = sem("kv_full"), sem("ek_ready"), sem("kv_ready")
        s_full, kx_ready, o_full, yt_ready, yt_full, mix_ready = (
            sem("s_full"), sem("kx_ready"), sem("o_full"), sem("yt_ready"), sem("yt_full"), sem("mix_ready"))
        qkv_full, qkv_ready, stg_hi, stg_lo, v_ready = (
            sem("qkv_full"), sem("qkv_ready"), sem("stg_hi"), sem("stg_lo"), sem("v_ready"))
        stg_clear, kz_clear, kz_ready = sem("stg_clear"), sem("kz_clear"), sem("kz_ready")
        kt_full, kt_ready = sem("kt_full"), sem("kt_ready")
        a_full, a_free = sem("a_full"), sem("a_free")
        stm_ready, mx_full, qtb_ready = sem("stm_ready"), sem("mx_full"), sem("qtb_ready")
        b_full, p_ready, pv_done = sem("b_full"), sem("p_ready"), sem("pv_done")
        ysb_ready, yo_full, y_norm = sem("ysb_ready"), sem("yo_full"), sem("y_norm")
        fin_full, fin_ready = sem("fin_full"), sem("fin_ready")

        block = ctx.enter_context(nc.Block())

        def acc_done(L):
            p, c = divmod(L, 4)
            if p in FFNS:
                return down_done, FB * (L - 4 * p + 1) + (NC * FB if p == FFN1 else 0)
            if p in MOES:
                return down_done, 2 * NC * FB + NU * (c + 1) + (NC * NU if p == MOE1 else 0)
            return acc_ready, c + 1 + (NC if p == CAUSAL else 0)

        def slot(b, g):
            return (g + 2) % G if b == 0 else g + 2

        def kz(s, h, half):
            if s % 2 == 0 and half:
                return (uh, ul)[h // 2][:, h % 2 * CW:(h % 2 + 1) * CW]
            return kza[0 if s % 2 == 0 else 1 + half][:, h, :]

        def tok(c):
            return slice(c * CW, (c + 1) * CW)

        @block.sync
        def _(sp):
            xv = x_in.rearrange("(t p) d -> p t d", p=P)
            ov = out.rearrange("b (t p) d -> p b t d", p=P)
            for c in range(NC):
                sp.dma_start(x[:, c * CT:(c + 1) * CT, :], xv[:, c * CT:(c + 1) * CT, :]).then_inc(x_loaded[c], 16)
                if c == 0:
                    sp.dma_start(raw_q[:, 0, :], q1_in).then_inc(q_loaded, 16)
                    sp.dma_start(raw_q[:, 1, :], q2_in).then_inc(q_loaded, 16)
            sp.dma_start(raw_g, gw_in).then_inc(g_loaded, 16)
            sp.dma_start(raw_u, uw_in).then_inc(g_loaded, 16)
            sp.dma_start(dw[:, :, :].rearrange("p u d -> p (u d)"), dw_in).then_inc(dw_loaded, 16)
            for c in range(NC):
                sp.wait_ge(x_ready, 4 * MOE1 + c + 1)
                sp.dma_start(ov[:, c // 2, (c % 2) * CT:(c % 2 + 1) * CT, :],
                             x[:, c * CT:(c + 1) * CT, :]).then_inc(stored, 16)
            sp.wait_ge(stored, 16 * NC)

        @block.gpsimd
        def _(pool):
            chain = [0]

            def link(ins):
                chain[0] += 1
                ins.then_inc(pch, 1)
                pool.wait_ge(pch, chain[0])

            def rstd(L):
                r = L % 2
                pool.wait_ge(stats_ready, L + 1)
                var = mv[:, r, :, 1]
                r1, r2, r3 = (rs[:, r, n, :] for n in range(3))
                t = rtmp[:, r, :]
                link(pool.tensor_scalar(t, var, EPS, None, ALU.add))
                p = pool.tensor_tensor(r1, t, nhalf[:, :], ALU.pow)
                if L // 4 not in FFNS:
                    p.then_inc(rstd_ready, 1)
                    if L // 4 == LIN:
                        xadd(L, bprow[:, :])
                    return
                link(p)
                link(pool.tensor_tensor(t, r1, r1, ALU.mult))
                link(pool.tensor_tensor(t, t, var, ALU.mult))
                link(pool.tensor_scalar(t, t, EPS, None, ALU.add))
                link(pool.tensor_tensor(r2, t, nhalf[:, :], ALU.pow))
                pool.tensor_tensor(r3, r1, r2, ALU.mult).then_inc(rstd_ready, 1)
                xadd(L, b2q[:, :])

            def xadd(L, row):
                c = L % 4
                pool.wait_ge(norm_ready, L + 1)
                if L // 4 in FFNS:
                    pool.wait_ge(ub_ready, L % 4 + 1 + (4 if L // 4 == FFN1 else 0))
                xc = x[:, c * CT:(c + 1) * CT, :]
                pool.tensor_tensor(xc, xc, row.unsqueeze(1).to_broadcast([P, CT, D]), ALU.add).then_inc(xadd_ready, 1)

            def tile(b, i):
                n = TB * b + i
                pool.wait_ge(qkv_ready, n + 1)
                pool.tensor_copy(va[:, b, i, :, 0:HD],
                                 qkv[:, n % 2, 2 * D:].rearrange("p (h d) -> p h d", h=H)).then_inc(v_ready, 1)
                pool.wait_ge(v_ready, n + 1)

            def alone(s, half):
                b, g = divmod(s, G)
                n = GH * (2 * s + half)
                pool.wait_ge(kt_ready, 2 * (TB * b + CT * (half + 1)))
                pool.wait_ge(v_ready, TB)
                pool.wait_ge(kz_ready, n)
                if s >= 2:
                    pool.wait_ge(b_full, ((s - 2) * NBLK + (12 if half else 8)) * GH)
                for h in range(GH):
                    r = slice(h * SL, (h + 1) * SL)
                    pool.tensor_copy(kz(s, h, half)[r, :], kt[r, slot(b, g), tok(half)].bitcast(F32))\
                        .then_inc(kz_ready, 1)
                    pool.wait_ge(kz_ready, n + h + 1)

            pool.memset(nhalf[:, :], -0.5)
            pool.memset(stm[:, :, :, :, :].bitcast(F32), 0.0)
            for z in kza:
                pool.memset(z[:, :, :].bitcast(F32), 0.0)
            pool.wait_ge(c_loaded, 16)
            pool.tensor_copy(identr[:, :], raw_c[:, C_ID:C_ID + P]).then_inc(consts, 1)
            pool.wait_ge(small_loaded, 32)
            pool.tensor_scalar(b2q[:, :], rows[:, R_B2:R_B2 + D], 0.25, None, ALU.mult)
            pool.tensor_copy(bprow[:, :], rows[:, R_BP:R_BP + D]).then_inc(consts, 1)
            rstd(0)
            rstd(1)
            pool.tensor_copy(identb[:, :], raw_c[:, C_ID:C_ID + P])
            pool.memset(mask_qk[:, 0:CW - P], 0.0)
            pool.tensor_copy(mask_qk[:, CW - P:], raw_c[:, C_MA:C_MA + P])
            pool.tensor_copy(mask_kq[:, :], raw_c[:, C_MB:C_MB + P])
            pool.tensor_copy(bmask[:, :], raw_c[:, C_BM:C_BM + P + H])
            pool.tensor_copy(iota[:, :], raw_c[:, C_IO:C_IO + E_])
            pool.tensor_copy(rope[:, :, :, :], raw_c[:, C_COS:C_COS + 2 * TB * HD]
                             .rearrange("p (a t d) -> p a t d", a=2, t=TB))
            pool.tensor_copy(sel[:, :, :], raw_c[0:3 * NR, C_SEL:C_END].rearrange("p (u n) -> p u n", u=NU))\
                .then_inc(consts, 1)

            def low(part, hi, lo, raw, last=False):
                pool.wait_ge(hi_ready, part)
                pool.tensor_tensor(lo, raw, hi.bitcast(F32), ALU.subtract).then_inc(prep, 1)

            low(1, wh[:, :], wl[:, :], raw_a)
            rstd(2)
            low(2, gh[:, :], gl[:, :], raw_g)
            rstd(3)
            low(3, vh[:, :], vl[:, :], raw_u)
            for L in range(4, 20):
                if L == 16:
                    pool.wait_ge(x_ready, 4 * LIN + 4)
                    pool.memset(va[:, :, :, :, HD:HD + 1], 1.0)
                    pool.wait_ge(x_ready, 4 * FFN1 + 4)
                    link(pool.memset(stg[:, :, :, :].bitcast(F32), 0.0))
                    pool.memset(stg[:, :, H:, 3 * HD:3 * HD + 2].bitcast(F32), 1.0).then_inc(stg_clear, 1)
                if L < 18:
                    rstd(L)
            rstd(18)
            for i in range(TB):
                tile(0, i)
                if i == 1:
                    rstd(19)
            alone(1, 0)
            alone(1, 1)
            for s in range(-1, STEPS):
                for k in range(NBLK):
                    for todo in HOOKS.get(("pool", s, k), []):
                        if todo[0] == "rope":
                            tile(*todo[1:])
                        if todo[0] == "alone":
                            alone(*todo[1:])
                        if todo[0] == "norm":
                            rstd(todo[1])
                            pool.wait_ge(rstd_ready, todo[1] + 1)
            rstd(22)
            rstd(23)

        @block.scalar
        def _(act):
            chain = [0]

            def link(ins):
                chain[0] += 1
                ins.then_inc(ach, 1)
                act.wait_ge(ach, chain[0])

            act.dma_start(small[:, :], small_in).then_inc(small_loaded, 16)
            act.dma_start(rows, rows_in.to_broadcast([P, R_END])).then_inc(small_loaded, 16)
            act.dma_start(raw_c, const_in).then_inc(c_loaded, 16)
            act.dma_start(raw_a, wa_in).then_inc(a_loaded, 16)
            act.dma_start(wp[:, :, :].rearrange("p a n -> p (a n)"), wp_in).then_inc(a_loaded, 16)

            def ln(L):
                p, c = divmod(L, 4)
                act.wait_ge(ln_t, L + 1)
                if L >= 1:
                    act.wait_ge(split_ready, L)
                dst = ft[:, :]
                if p == LIN:
                    dst = uf[:, c // 2, 1 + (c % 2) * CW:1 + (c % 2 + 1) * CW]
                    act.wait_ge(prep, 3)
                    act.wait_ge(consts, 3)
                    act.wait_ge(w2_ready, 2)
                if p in FFNS:
                    ins = act.activation(dst, T[:, :], ACT.Identity, bias=small[:, S_BE:S_BE + 1],
                                         scale=small[:, S_GA:S_GA + 1])
                else:
                    ins = act.activation(dst, T[:, :], ACT.Copy)
                ins.then_inc(ft_ready, 1)

            def ffn(p):
                for n in range(NC * FB):
                    k, m = n % FB, n + (16 if p == FFN1 else 0)
                    act.wait_ge(y_full, m + 1)
                    if m >= 4:
                        act.wait_ge(down_done, m - 3)
                    act.activation(hbuf[:, m % 4, :], bank[1 + m % 4][:, :], ACT.Silu,
                                   bias=small[:, S_B1 + k:S_B1 + k + 1],
                                   scale=small[:, S_S1 + k:S_S1 + k + 1]).then_inc(h_ready, 1)
                    if k == 1:
                        ln(4 * p + n // FB + 1)
                if p == FFN1:
                    route(0)

            def linear(b):
                if b == 1:
                    ln(4 * LIN + 2)
                ln(4 * LIN + 2 * b + 1)
                for c in range(2):
                    n = 2 * b + c
                    act.wait_ge(q_full, n + 1)
                    if b:
                        act.wait_ge(kv_ready, 4)
                    act.activation(relu[:, c, :], bank[1 + c][:, :], ACT.Relu)
                    act.activation(expo[:, c, :], bank[1 + c][:, :], ACT.Exp).then_inc(eq_ready, 1)
                for t in range(4):
                    n = 4 * b + t
                    act.wait_ge(kv_full, n + 1)
                    act.wait_ge(qf_ready, 2 * b + t + 1) if t < 2 else act.wait_ge(kv_ready, n - 1)
                    kp = bank[3 + t][:, :].rearrange("p (t n) -> p t n", t=2)[:, :, 0:D]
                    n0 = relu[:, t % 2, 0:2 * D].rearrange("p (t n) -> p t n", t=2)
                    n1 = expo[:, t % 2, 0:2 * D].rearrange("p (t n) -> p t n", t=2)
                    act.activation(n0, kp, ACT.Relu)
                    act.activation(n1, kp, ACT.Exp).then_inc(ek_ready, 1)

            def route(r):
                act.wait_ge(dd_ready, r + 1)
                act.activation(th[:, :, :], dd[:, :, :], ACT.Tanh, scale=0.5).then_inc(th_ready, 1)

            def weights(r):
                act.wait_ge(cw_full, r + 1)
                act.activation(cwt[:, r % 2, :], T[0:3 * NR, 0:CW // 2].bitcast(BF16), ACT.Copy)\
                    .then_inc(cwt_ready, 1)

            def moe(p):
                r0 = 4 if p == MOE1 else 0
                if p == MOE0:
                    weights(r0)
                for n in range(NC * NU):
                    c, u = divmod(n, NU)
                    m = n + (NC * NU if p == MOE1 else 0)
                    act.wait_ge(g_full, m + 1)
                    if m >= 2:
                        act.wait_ge(hm_ready, m - 1)
                    act.activation(sg[:, m % 2, :], bank[1 + m % 2][:, :], ACT.Silu).then_inc(sg_ready, 1)
                    L = 4 * p + c + 1
                    if u == 1 and L < 24:
                        ln(L)
                    if c < 3 and u == 5:
                        route(r0 + c + 1)
                    if c < 3 and u == 8:
                        weights(r0 + c + 1)

            def qkv_out(b, i):
                n = TB * b + i
                act.wait_ge(qkv_full, n + 1)
                if n >= 2:
                    act.wait_ge(stg_lo, n - 1)
                    act.wait_ge(v_ready, n - 1)
                src = bank[6 + n % 2] if b == 0 else T
                act.activation(qkv[:, n % 2, :], src[:, 0:3 * D], ACT.Copy).then_inc(qkv_ready, 1)

            def parts(b, i, which):
                n = 2 * (TB * b + i) + which
                act.wait_ge(kt_full, n + 1)
                src = bank[3] if b == 0 and which else T
                act.activation((kt, qta)[which][:, 2 * b:2 * b + G, i * P:(i + 1) * P],
                               src[:, :].rearrange("p (g t) -> p g t", g=G), ACT.Copy).then_inc(kt_ready, 1)

            def alone(half):
                act.wait_ge(kt_ready, 2 * CT * (half + 1))
                if half:
                    act.wait_ge(kz_clear, 1)
                for h in range(GH):
                    r = slice(h * SL, (h + 1) * SL)
                    act.activation(kz(0, h, half)[r, :], kt[r, slot(0, 0), tok(half)].bitcast(F32), ACT.Copy)\
                        .then_inc(kz_ready, 1)

            def causal():
                ln(17)
                for i in range(TB + 1):
                    if i < TB:
                        qkv_out(0, i)
                    if i >= 1:
                        parts(0, i - 1, 0)
                        parts(0, i - 1, 1)
                    if i == CT:
                        alone(0)
                alone(1)
                for s in range(-1, STEPS):
                    for k, (c, j) in enumerate(B_BLOCKS):
                        if s >= 0:
                            blk = s * NBLK + k
                            w = min(CW, CW * (c + 1) - j * P)
                            for h in range(GH):
                                n = blk * GH + h
                                act.wait_ge(b_full, n + 1)
                                if h == 0 and blk >= 2:
                                    act.wait_ge(pv_done, blk - 1)
                                act.activation(pb[:, blk % 2, h, 0:w], bank[1 + n % 3][:, 0:w], ACT.Exp,
                                               scale=SCALE).then_inc(p_ready, 1)
                        for todo in HOOKS.get(("act", s, k), []):
                            if todo[0] == "ln":
                                ln(todo[1])
                            if todo[0] == "qkv":
                                qkv_out(*todo[1:])
                            if todo[0] == "parts":
                                parts(*todo[1:])
                            if todo[0] == "yraw":
                                yraw(*todo[1:])
                            if todo[0] == "final":
                                final(*todo[1:])
                            if todo[0] == "route":
                                route(4)
                            if todo[0] == "weights":
                                weights(4)
                yraw(STEPS - 1, 1)
                final(1, 1)

            def yraw(s, c):
                n = 2 * s + c
                act.wait_ge(pv_done, s * NBLK + (4 if c == 0 else 12))
                if n >= 2:
                    act.wait_ge(yo_full, n - 1)
                act.activation(ysb[:, n % 2, :], bank[6 + n % 2][:, :], ACT.Copy).then_inc(ysb_ready, 1)

            def final(b, c):
                f = 2 * b + c
                act.wait_ge(fin_full, f + 1)
                if f >= 1:
                    act.wait_ge(*acc_done(4 * CAUSAL + f - 1))
                act.activation(hbuf[:, 0, :], T[:, :], ACT.Copy).then_inc(fin_ready, 1)

            act.wait_ge(w1_ready, 1)
            act.activation(w1h[:, :], w1f[:, :], ACT.Copy).then_inc(w1_hi, 1)
            ln(0)
            act.wait_ge(a_loaded, 32)
            act.activation(wh[:, :], raw_a, ACT.Copy).then_inc(hi_ready, 1)
            act.wait_ge(g_loaded, 32)
            act.activation(gh[:, :], raw_g, ACT.Copy).then_inc(hi_ready, 1)
            act.activation(vh[:, :], raw_u, ACT.Copy).then_inc(hi_ready, 1)
            ffn(FFN0)
            linear(0)
            linear(1)
            ln(8)
            ffn(FFN1)
            moe(MOE0)
            causal()
            moe(MOE1)

        @block.vector
        def _(dve):
            chain = [0]

            def link(ins):
                chain[0] += 1
                ins.then_inc(dch, 1)
                dve.wait_ge(dch, chain[0])

            def moments(L):
                p, c = divmod(L, 4)
                r = L % 2
                if p == 0:
                    dve.wait_ge(x_loaded[c], 16)
                else:
                    dve.wait_ge(x_ready, L - 3)
                for t in range(CT):
                    ins = dve.bn_stats(stats[:, t, :], x[:, c * CT + t, :])
                link(ins)
                for t in range(CT):
                    ins = dve.bn_aggr(mv[:, r, t, :], stats[:, t, :])
                ins.then_inc(stats_ready, 1)

            def norm(L):
                p, c = divmod(L, 4)
                r = L % 2
                dve.wait_ge(rstd_ready, L + 1)
                dve.wait_ge(stats_ready, L + 1)
                if L >= 2:
                    dve.wait_ge(ln_t, L - 1)
                for t in range(CT):
                    ins = dve.tensor_scalar(hn[:, r, t, :], x[:, c * CT + t, :], mv[:, r, t, 0:1],
                                            rs[:, r, 2 if p in FFNS else 0, t:t + 1], ALU.subtract, ALU.mult)
                ins.then_inc(norm_ready, 1)
                if p in FFNS:
                    for t in range(CT):
                        ins = dve.tensor_scalar(ub[:, t, :], x[:, c * CT + t, :], mv[:, r, t, 0:1],
                                                rs[:, r, 0, t:t + 1], ALU.subtract, ALU.mult)
                    link(ins)
                    xc = x[:, c * CT:(c + 1) * CT, :]
                    dve.scalar_tensor_tensor(out=xc, in0=ub[:, :, :], scalar=0.5, in1=xc,
                                             op0=ALU.mult, op1=ALU.add).then_inc(ub_ready, 1)

            def split(L):
                p, c = divmod(L, 4)
                dve.wait_ge(ft_ready, L + 1)
                src = ft[:, :]
                if p == LIN:
                    src = uf[:, c // 2, 1 + (c % 2) * CW:1 + (c % 2 + 1) * CW]
                if L in (20, 21):
                    dve.wait_ge(b_full, 7 * NBLK * GH)
                link(dve.tensor_copy(uh[:, tok(c)], src))
                dve.tensor_tensor(ul[:, tok(c)], src, uh[:, tok(c)].bitcast(F32), ALU.subtract)\
                    .then_inc(split_ready, 1)

            def update(L, scale, acc=ACC):
                c = L % 4
                dve.wait_ge(*acc_done(L))
                if L < 12:
                    dve.wait_ge(xadd_ready, L + 1)
                xc = x[:, c * CT:(c + 1) * CT, :]
                dve.scalar_tensor_tensor(out=xc, in0=acc[:, :].rearrange("p (t d) -> p t d", t=CT), scalar=scale,
                                         in1=xc, op0=ALU.mult, op1=ALU.add).then_inc(x_ready, 1)

            def ffn(p):
                for c in range(NC):
                    L = 4 * p + c
                    split(L + 1)
                    norm(L + 2)
                    if L + 1 == 4 * MOE0:
                        route(0)
                    update(L, 0.25)
                    if L + 1 == 4 * MOE0:
                        weigh(0)
                    moments(L + 3)

            def linear(b):
                if b == 1:
                    split(4 * LIN + 2)
                split(4 * LIN + 2 * b + 1)
                norm(4 * LIN + 2 * b + 2)
                for c in range(2):
                    n = 2 * b + c
                    dve.wait_ge(eq_ready, n + 1)
                    dve.scalar_tensor_tensor(out=qf[:, tok(c)], in0=expo[:, c, :], scalar=1.0, in1=relu[:, c, :],
                                             op0=ALU.min, op1=ALU.add).then_inc(qf_ready, 1)
                moments(4 * LIN + 2 * b + 3)
                for t in range(4):
                    n = 4 * b + t
                    dve.wait_ge(ek_ready, n + 1)
                    kvp = bank[3 + t][:, :].rearrange("p (t n) -> p t n", t=2)
                    n0 = relu[:, t % 2, 0:2 * D].rearrange("p (t n) -> p t n", t=2)
                    n1 = expo[:, t % 2, 0:2 * D].rearrange("p (t n) -> p t n", t=2)
                    dve.scalar_tensor_tensor(out=kf[:, 2 * t:2 * t + 2, :], in0=n1, scalar=1.0, in1=n0,
                                             op0=ALU.min, op1=ALU.add)
                    dve.tensor_copy(vx[:, 2 * t:2 * t + 2, 0:D], kvp[:, :, D:2 * D]).then_inc(kv_ready, 1)
                u = uf[:, b, :]
                link(dve.tensor_scalar(loc, u[:, 0:S], small[:, S_CW:S_CW + 1], small[:, S_CB:S_CB + 1],
                                       ALU.mult, ALU.add))
                for w in range(1, 3):
                    link(dve.scalar_tensor_tensor(out=loc, in0=u[:, w:w + S],
                                                  scalar=small[:, S_CW + w:S_CW + w + 1], in1=loc,
                                                  op0=ALU.mult, op1=ALU.add))
                dve.wait_ge(s_full, b + 1)
                sv = bank[1]
                dve.tensor_tensor(kx[:, 0:P], sv[:, 0:P], bmask[:, 0:P], ALU.mult)
                dve.tensor_scalar(kx[:, P:P + H], bmask[:, P:P + H], sv[:, P:P + 1], None, ALU.mult)\
                    .then_inc(kx_ready, 1)
                norm(4 * LIN + 2 * b + 3)
                for t in range(4):
                    n = 4 * b + t
                    dve.wait_ge(o_full, n + 1)
                    ov = bank[2 + t][:, :].rearrange("p (t n) -> p t n", t=2)
                    link(dve.tensor_scalar(den[:, t % 2, :, :], ov[:, :, P:P + H], 1e-6, None, ALU.max))
                    link(dve.reciprocal(rden[:, t % 2, :, :], den[:, t % 2, :, :]))
                    if t >= 2:
                        dve.wait_ge(yt_full, n - 1)
                    for e in range(2):
                        ins = dve.tensor_tensor(
                            yt[:, t % 2, e, :].rearrange("p (h d) -> p h d", h=H),
                            ov[:, e, 0:P].rearrange("p (h d) -> p h d", h=H),
                            rden[:, t % 2, e, :].unsqueeze(2).to_broadcast([P, H, HD]), ALU.mult)
                    ins.then_inc(yt_ready, 1)
                    if t >= 1:
                        add_local(b, t - 1)
                add_local(b, 3)
                moments(4 * LIN + 2 * b + 4)
                if b == 1:
                    split(8)

            def add_local(b, t):
                n = 4 * b + t
                dve.wait_ge(yt_full, n + 1)
                cols = slice(t * 2 * P, (t + 1) * 2 * P)
                dve.tensor_tensor(mix[:, cols], bank[(6, 1)[t % 2]][:, 0:256], loc[:, cols], ALU.add)\
                    .then_inc(mix_ready, 1)
                if t % 2:
                    update(4 * LIN + 2 * b + t // 2, 1.0)

            def route(r):
                dve.wait_ge(lg_full, r + 1)
                if r >= 1:
                    dve.wait_ge(cs_ready, r)
                lv = T[:, 0:CT * 32].rearrange("p (t n) -> p t n", t=CT)
                dve.tensor_copy(dd[:, 1, :], lv[:, :, E_])
                dve.tensor_copy(lg[:, :, :], lv[:, :, 0:NR + 1]).then_inc(lg_ready, 1)
                dve.wait_ge(lg_ready, r + 1)
                for t in range(CT):
                    ins = dve.max(m8[:, t, :], lg[:, t, 0:E_])
                link(ins)
                for t in range(CT):
                    dve.max_index(ix[:, t, :], m8[:, t, :], lg[:, t, 0:E_])
                dve.tensor_tensor(dd[:, 0, :], m8[:, :, 0], m8[:, :, 1], ALU.subtract).then_inc(dd_ready, 1)

            def weigh(r):
                dve.wait_ge(dd_ready, r + 1)
                dve.tensor_copy(ixf[:, :, :], ix[:, :, 0:2])
                dve.wait_ge(th_ready, r + 1)
                dve.tensor_scalar(tw[:, 0, :], th[:, 0, :], 0.5, 0.5, ALU.mult, ALU.add)
                dve.tensor_scalar(cw[:, :, E_], th[:, 1, :], 0.5, 0.5, ALU.mult, ALU.add)
                link(dve.tensor_scalar(tw[:, 1, :], th[:, 0, :], -0.5, 0.5, ALU.mult, ALU.add))
                io = iota[:, :].unsqueeze(1).to_broadcast([P, CT, E_])
                for a in range(2):
                    ins = dve.tensor_tensor(oh[:, a, :, :], io, ixf[:, :, a].unsqueeze(2).to_broadcast([P, CT, E_]),
                                            ALU.is_equal)
                link(ins)
                for a in range(2):
                    ins = dve.tensor_tensor(oh[:, a, :, :], oh[:, a, :, :],
                                            tw[:, a, :].unsqueeze(2).to_broadcast([P, CT, E_]), ALU.mult)
                link(ins)
                link(dve.tensor_tensor(cw[:, :, 0:E_], oh[:, 0, :, :], oh[:, 1, :, :], ALU.add))
                link(dve.tensor_copy(cs[:, :, 0, :], cw[:, :, :]))
                link(dve.tensor_tensor(cr[:, 0, :, :], cw[:, :, :], cs[:, :, 0, :], ALU.subtract))
                link(dve.tensor_copy(cs[:, :, 1, :], cr[:, 0, :, :]))
                dve.tensor_tensor(cs[:, :, 2, :], cr[:, 0, :, :], cs[:, :, 1, :], ALU.subtract).then_inc(cs_ready, 1)

            def moe(p):
                r0 = 4 if p == MOE1 else 0
                for n in range(NC * NU):
                    c, u = divmod(n, NU)
                    m = n + (NC * NU if p == MOE1 else 0)
                    L = 4 * p + c
                    dve.wait_ge(sg_ready, m + 1)
                    link(dve.tensor_tensor(su[:, m % 2, :], sg[:, m % 2, :], bank[3 + m % 2][:, :], ALU.mult))
                    if m >= 3:
                        dve.wait_ge(down_done, 32 + m - 2)
                    dve.tensor_tensor(hbuf[:, m % 3, :], su[:, m % 2, :], bank[5 + m % 2][:, :], ALU.mult)\
                        .then_inc(hm_ready, 1)
                    if u == 1 and c > 0:
                        update(L - 1, 0.5)
                    if u == 1 and L + 1 < 24:
                        split(L + 1)
                    if u == 2 and L + 2 < 24:
                        norm(L + 2)
                    if u == 3 and L + 3 < 24:
                        moments(L + 3)
                    if c < 3 and u == 4:
                        route(r0 + c + 1)
                    if c < 3 and u == 5:
                        weigh(r0 + c + 1)
                update(4 * p + 3, 0.5)

            def tile(b, i):
                n = TB * b + i
                dve.wait_ge(qkv_ready, n + 1)
                dve.wait_ge(stg_clear, 1)
                if n >= 1:
                    dve.wait_ge(stg_lo, n)
                s = stg[:, n % 2, :, :]
                qk = qkv[:, n % 2, 0:2 * D].rearrange("p (h d) -> p h d", d=HD)
                cos = rope[:, 0, i, :].unsqueeze(1).to_broadcast([P, 2 * H, HD])
                dve.tensor_tensor(ra[:, :, :], qk, cos, ALU.mult)
                hh = HD // 2
                for a in range(2):
                    src = slice((1 - a) * hh, (2 - a) * hh)
                    dst = slice(a * hh, (a + 1) * hh)
                    sin = rope[:, 1, i, dst].unsqueeze(1).to_broadcast([P, 2 * H, hh])
                    ins = dve.tensor_tensor(rb[:, :, dst], qk[:, :, src], sin, ALU.mult)
                link(ins)
                link(dve.tensor_tensor(ra[:, :, :], ra[:, :, :], rb[:, :, :], ALU.add))
                if n >= 2:
                    dve.wait_ge(kt_full, 2 * n - 2)
                dve.tensor_copy(s[:, 0:H, 0:2 * HD].rearrange("p h (a d) -> p h a d", a=2),
                                ra[:, 0:H, :].unsqueeze(2).to_broadcast([P, H, 2, HD]))
                dve.tensor_copy(s[:, H:, 0:3 * HD].rearrange("p h (a d) -> p h a d", a=3)[:, :, 0:3:2, :],
                                ra[:, H:, :].unsqueeze(2).to_broadcast([P, H, 2, HD])).then_inc(stg_hi, 1)
                dve.wait_ge(stg_hi, n + 1)
                sf = s.bitcast(F32)
                dve.tensor_tensor(s[:, 0:H, 2 * HD:3 * HD], ra[:, 0:H, :], sf[:, 0:H, 0:HD], ALU.subtract)
                dve.tensor_tensor(s[:, H:, HD:2 * HD], ra[:, H:, :], sf[:, H:, 0:HD], ALU.subtract)\
                    .then_inc(stg_lo, 1)

            def maxima(s, k):
                i, half = A_BLOCKS[k]
                w = min(CW, (i + 1) * P - half * CW)
                for h in range(GH):
                    n = (s * NBLK + k) * GH + h
                    dve.wait_ge(a_full, n + 1)
                    src = bank[4 + n % 2][:, 0:w]
                    dst = mx[:, i, h, half:half + 1]
                    if i * P < half * CW + w:
                        ins = dve.tensor_tensor_reduce(out=src, in0=src, in1=mask_qk[:, CW - w:], scale=1.0,
                                                       scalar=-3e38, op0=ALU.add, op1=ALU.max, accum_out=dst)
                    else:
                        ins = dve.tensor_reduce(dst, src, AX.X, ALU.max)
                    ins.then_inc(a_free, 1)
                    if h == 1:
                        drains(s - 1, k)

            def drains(s, k):
                for todo in HOOKS.get(("dve", s, k), []):
                    if todo[0] == "add":
                        add_max(*todo[1:])
                    if todo[0] == "yout":
                        yout(*todo[1:])
                    if todo[0] == "update":
                        update(todo[1], 1.0, T)
                    if todo[0] == "route":
                        route(4)
                    if todo[0] == "weigh":
                        weigh(4)

            def negate(s, half):
                n = 2 * s + half
                b, g = divmod(s, G)
                t0 = half * CT
                dve.wait_ge(a_free, s * NBLK * GH + (4 if half == 0 else NBLK) * GH)
                m = mx[:, t0:t0 + CT, :, 0]
                if half:
                    link(dve.tensor_tensor(mm8, m, mx[:, t0:t0 + CT, :, 1], ALU.max))
                    m = mm8
                if n >= 2:
                    dve.wait_ge(mx_full, n - 1)
                    dve.wait_ge(stm_ready, n - 1)
                st = stm[:, half, :, :, :]
                link(dve.tensor_scalar(st[:, :, :, 3 * HD], m, -1.0, None, ALU.mult))
                dve.scalar_tensor_tensor(out=st[:, :, :, 3 * HD + 1], in0=m, scalar=-1.0,
                                         in1=st[:, :, :, 3 * HD].bitcast(F32), op0=ALU.mult, op1=ALU.subtract)\
                    .then_inc(stm_ready, 1)

            def add_max(s, half):
                n = 2 * s + half
                b, g = divmod(s, G)
                dve.wait_ge(mx_full, n + 1)
                dve.tensor_tensor(qtb[:, s % 2, tok(half)], T[:, :], qta[:, slot(b, g), tok(half)].bitcast(F32), ALU.add)\
                    .then_inc(qtb_ready, 1)

            def yout(s, c):
                n = 2 * s + c
                b, g = divmod(s, G)
                dve.wait_ge(yo_full, n + 1)
                if n >= 1:
                    dve.wait_ge(y_norm, n)
                v = T[:, :].rearrange("p (t h d) -> p t h d", t=CT, h=GH)
                if b:
                    dve.wait_ge(fin_full, c + 1)
                link(dve.reciprocal(yrec, v[:, :, :, HD]))
                dst = ytok[:, c * CT:(c + 1) * CT, g * GH * HD:(g + 1) * GH * HD]
                dve.tensor_tensor(dst.rearrange("p t (h d) -> p t h d", h=GH), v[:, :, :, 0:HD],
                                  yrec.unsqueeze(3).to_broadcast([P, CT, GH, HD]), ALU.mult)\
                    .then_inc(y_norm, 1)

            def causal():
                split(17)
                norm(18)
                for i in range(TB):
                    tile(0, i)
                    if i == 1:
                        moments(19)
                    if i == 3:
                        norm(19)
                    if i > CT:
                        maxima(0, i - CT - 1)
                maxima(0, CT - 1)
                dve.wait_ge(qkv_full, TB)
                dve.memset(uh[:, 0:2 * CW].bitcast(F32), 0.0)
                dve.memset(ul[:, 0:2 * CW].bitcast(F32), 0.0).then_inc(kz_clear, 1)
                for s in range(-1, STEPS):
                    for k in range(CT if s < 0 else 0, NBLK):
                        if s + 1 < STEPS:
                            maxima(s + 1, k)
                        else:
                            drains(s, k)
                        for todo in HOOKS.get(("dve", s, k), []):
                            if todo[0] == "ln":
                                split(todo[1])
                            if todo[0] == "moments":
                                moments(todo[1])
                            if todo[0] == "norm":
                                norm(todo[1])
                            if todo[0] == "rope":
                                tile(*todo[1:])
                            if todo[0] == "negate":
                                negate(*todo[1:])
                yout(STEPS - 1, 1)
                update(4 * CAUSAL + 3, 1.0, T)
                moments(22)

            dve.wait_ge(q_loaded, 32)
            dve.tensor_scalar(w1f[:, :], raw_q[:, 0, :], -128.0, None, ALU.add).then_inc(w1_ready, 1)
            moments(0)
            norm(0)
            moments(1)
            dve.wait_ge(w1_hi, 1)
            dve.tensor_tensor(w1l[:, :], w1f[:, :], w1h[:, :].bitcast(F32), ALU.subtract).then_inc(w2_ready, 1)
            dve.wait_ge(small_loaded, 32)
            dve.scalar_tensor_tensor(out=w2[:, :, :].rearrange("p k n -> p (k n)"), in0=raw_q[:, 1, :], scalar=-128.0,
                                     in1=rows[:, R_S2:R_S2 + F], op0=ALU.add, op1=ALU.mult).then_inc(w2_ready, 1)
            split(0)
            norm(1)
            moments(2)
            ffn(FFN0)
            dve.wait_ge(prep, 3)
            dve.wait_ge(consts, 3)
            dve.memset(uf[:, :, 0:1], 0.0)
            dve.memset(uf[:, :, S + 1:S + 2], 0.0)
            link(dve.memset(vx[:, :, D:D + 1], 1.0))
            linear(0)
            linear(1)
            ffn(FFN1)
            moe(MOE0)
            causal()
            moe(MOE1)

        @block.tensor
        def _(pe):
            drain = [None]

            def t_take(drained, value):
                if drain[0]:
                    pe.wait_ge(*drain[0])
                drain[0] = (drained, value)

            def mm3(dst, ah, al, bh, bl, start=True, stop=True):
                pe.matmul(dst, ah, bl, start=start, stop=False)
                pe.matmul(dst, al, bh, start=False, stop=False)
                return pe.matmul(dst, ah, bh, start=False, stop=stop)

            def ln(L):
                pe.wait_ge(norm_ready, L + 1)
                t_take(ft_ready, L + 1)
                for t in range(CT):
                    ins = pe.transpose(T[:, t * P:(t + 1) * P], hn[:, L % 2, t, :], ident[:, :])
                ins.then_inc(ln_t, 1)

            def acc_take(L):
                if L:
                    pe.wait_ge(x_ready, L)

            def ffn(p):
                if p:
                    pe.wait_ge(mix_ready, 8)
                for n in range(NC * FB + 2):
                    if n < NC * FB:
                        c, k = divmod(n, FB)
                        m = n + (16 if p == FFN1 else 0)
                        if k == 0:
                            pe.wait_ge(split_ready, 4 * p + c + 1)
                        if n >= 4:
                            pe.wait_ge(h_ready, m - 3)
                        f = slice(k * P, (k + 1) * P)
                        mm3(bank[1 + m % 4][:, :], w1h[:, f], w1l[:, f], uh[:, tok(c)], ul[:, tok(c)])\
                            .then_inc(y_full, 1)
                        if k == 1:
                            ln(4 * p + c + 1)
                        if n == NC * FB - 1 and p == FFN1:
                            route(4 * MOE0, 0)
                    if n >= 2:
                        c, k = divmod(n - 2, FB)
                        m = n - 2 + (16 if p == FFN1 else 0)
                        if k == 0:
                            acc_take(4 * p + c)
                        pe.wait_ge(h_ready, m + 1)
                        for t in range(CT):
                            ins = pe.matmul(ACC[:, t * P:(t + 1) * P], hbuf[:, m % 4, t * P:(t + 1) * P], w2[:, k, :],
                                            start=(k == 0 and t == 0), stop=(k == FB - 1), skip_group_check=True)
                        ins.then_inc(down_done, 1)

            def linear(b):
                if b == 1:
                    ln(4 * LIN + 2)
                ln(4 * LIN + 2 * b + 1)
                pe.wait_ge(mix_ready, 4) if b else pe.wait_ge(h_ready, NC * FB)
                pe.wait_ge(split_ready, 4 * LIN + 2 * b + 2)
                pe.wait_ge(prep, 1)
                for c in range(2):
                    mm3(bank[1 + c][:, :], wh[:, W_Q:W_Q + P], wl[:, W_Q:W_Q + P],
                        uh[:, tok(2 * b + c)], ul[:, tok(2 * b + c)]).then_inc(q_full, 1)
                for t in range(4):
                    for e in range(2):
                        i = TB * b + 2 * t + e
                        ins = mm3(bank[3 + t][:, e * 256:(e + 1) * 256], uh[:, i * P:(i + 1) * P],
                                  ul[:, i * P:(i + 1) * P], wh[:, W_KV:W_KV + 2 * P], wl[:, W_KV:W_KV + 2 * P])
                    ins.then_inc(kv_full, 1)
                pe.wait_ge(qf_ready, 2 * b + 1)
                pe.wait_ge(eq_ready, 2 * b + 1)
                for i in range(TB):
                    pe.wait_ge(kv_ready, 4 * b + i // 2 + 1)
                    ins = pe.matmul(bank[1][:, 0:D + 1], kf[:, i, :], vx[:, i, :], start=(i == 0), stop=(i == TB - 1))
                ins.then_inc(s_full, 1)
                pe.wait_ge(kx_ready, b + 1)
                pe.wait_ge(qf_ready, 2 * b + 2)
                for t in range(4):
                    for e in range(2):
                        i = 2 * t + e
                        ins = pe.matmul(bank[2 + t][:, e * 256:e * 256 + P + H], qf[:, i * P:(i + 1) * P], kx[:, :],
                                        start=True, stop=True)
                    ins.then_inc(o_full, 1)
                for t in range(4):
                    pe.wait_ge(yt_ready, 4 * b + t + 1)
                    if t >= 2:
                        pe.wait_ge(mix_ready, 4 * b + t - 1)
                    for e in range(2):
                        ins = pe.transpose(bank[(6, 1)[t % 2]][:, e * P:(e + 1) * P], yt[:, t % 2, e, :],
                                           ident[:, :])
                    ins.then_inc(yt_full, 1)
                    if t >= 1:
                        project(b, t - 1)
                project(b, 3)
                if b == 1:
                    ln(8)

            def project(b, t):
                pe.wait_ge(mix_ready, 4 * b + t + 1)
                pe.wait_ge(a_loaded, 32)
                L = 4 * LIN + 2 * b + t // 2
                if t % 2 == 0:
                    acc_take(L)
                for e in range(2):
                    i = 2 * t + e
                    ins = pe.matmul(ACC[:, (i % 4) * P:(i % 4 + 1) * P], mix[:, i * P:(i + 1) * P], wp[:, 0, :],
                                    start=True, stop=True)
                if t % 2:
                    ins.then_inc(acc_ready, 1)

            def route(L, r):
                pe.wait_ge(split_ready, L + 1)
                t_take(lg_ready, r + 1)
                c = L % 4
                for t in range(CT):
                    i = c * CT + t
                    ins = mm3(T[:, t * 32:t * 32 + NR + 1], uh[:, i * P:(i + 1) * P], ul[:, i * P:(i + 1) * P],
                              wh[:, W_R:W_END], wl[:, W_R:W_END])
                ins.then_inc(lg_full, 1)

            def weights(r):
                pe.wait_ge(cs_ready, r + 1)
                t_take(cwt_ready, r + 1)
                tb = T[0:3 * NR, 0:CW // 2].bitcast(BF16)
                for t in range(CT):
                    ins = pe.transpose(tb[:, t * P:(t + 1) * P], cs[:, t, :, :].rearrange("p a n -> p (a n)"),
                                       identb[:, :])
                ins.then_inc(cw_full, 1)

            def moe(p):
                r0 = 4 if p == MOE1 else 0
                m0 = NC * NU if p == MOE1 else 0
                if p == MOE1:
                    pe.wait_ge(p_ready, STEPS * NBLK * GH)
                    pe.wait_ge(ysb_ready, 2 * STEPS)
                    pe.wait_ge(a_free, STEPS * NBLK * GH)
                if p == MOE0:
                    weights(r0)
                    pe.wait_ge(h_ready, 2 * NC * FB)
                    pe.wait_ge(prep, 3)
                    pe.wait_ge(dw_loaded, 16)
                for n in range(NC * NU + 2):
                    if n < NC * NU:
                        c, u = divmod(n, NU)
                        m = m0 + n
                        L = 4 * p + c
                        if u == 0:
                            pe.wait_ge(split_ready, L + 1)
                            pe.wait_ge(cwt_ready, r0 + c + 1)
                        if n >= 2:
                            pe.wait_ge(hm_ready, m - 1)
                        f = slice(u * P, (u + 1) * P)
                        mm3(bank[1 + m % 2][:, :], gh[:, f], gl[:, f], uh[:, tok(c)], ul[:, tok(c)])
                        mm3(bank[3 + m % 2][:, :], vh[:, f], vl[:, f], uh[:, tok(c)], ul[:, tok(c)])
                        pe.matmul(bank[5 + m % 2][:, :], sel[:, u, :], cwt[:, (r0 + c) % 2, :], start=True, stop=True)\
                            .then_inc(g_full, 1)
                        if u == 1 and L + 1 < 24:
                            ln(L + 1)
                        if c < 3 and u == 4:
                            route(L + 1, r0 + c + 1)
                        if c < 3 and u == 8:
                            weights(r0 + c + 1)
                    if n >= 2:
                        c, u = divmod(n - 2, NU)
                        m = m0 + n - 2
                        if u == 0:
                            acc_take(4 * p + c)
                        pe.wait_ge(hm_ready, m + 1)
                        for t in range(CT):
                            ins = pe.matmul(ACC[:, t * P:(t + 1) * P], hbuf[:, m % 3, t * P:(t + 1) * P], dw[:, u, :],
                                            start=(u == 0 and t == 0), stop=(u == NU - 1), skip_group_check=True)
                        ins.then_inc(down_done, 1)

            def make_qkv(b, i):
                n = TB * b + i
                pe.wait_ge(split_ready, 4 * CAUSAL + n // CT + 1)
                if b == 0:
                    dst = bank[6 + n % 2]
                    if n >= 2:
                        pe.wait_ge(qkv_ready, n - 1)
                else:
                    t_take(qkv_ready, n + 1)
                    dst = T
                mm3(dst[:, 0:3 * D], uh[:, n * P:(n + 1) * P], ul[:, n * P:(n + 1) * P],
                    wh[:, W_QKV:W_QKV + 3 * D], wl[:, W_QKV:W_QKV + 3 * D]).then_inc(qkv_full, 1)

            def parts(b, i, which):
                n = TB * b + i
                pe.wait_ge(stg_lo, n + 1)
                if b == 0 and which:
                    dst = bank[3]
                    if i >= 1:
                        pe.wait_ge(kt_ready, 2 * n)
                else:
                    dst = T
                    t_take(kt_ready, 2 * n + which + 1)
                first = 0 if which else H
                for g in range(G):
                    o = slot(b, g) - 2 * b
                    ins = pe.transpose(dst[:, o * P:(o + 1) * P].bitcast(F32R),
                                       stg[:, n % 2, first + g * GH:first + (g + 1) * GH, :]
                                       .rearrange("p h d -> p (h d)"), identr[:, :])
                ins.then_inc(kt_full, 1)

            def maxima(s, half):
                n = 2 * s + half
                pe.wait_ge(stm_ready, n + 1)
                t_take(qtb_ready, n + 1)
                for t in range(CT):
                    ins = pe.transpose(T[:, t * P:(t + 1) * P].bitcast(F32R),
                                       stm[:, half, t, :, :].rearrange("p h d -> p (h d)"), identr[:, :])
                ins.then_inc(mx_full, 1)

            def sums(blk):
                s, k = divmod(blk, NBLK)
                c, j = B_BLOCKS[k]
                b, g = divmod(s, G)
                w = min(CW, CW * (c + 1) - j * P)
                pe.wait_ge(p_ready, GH * (blk + 1))
                pe.wait_ge(v_ready, TB * (b + 1))
                y = 2 * s + c
                if j == 0 and y >= 2:
                    pe.wait_ge(ysb_ready, y - 1)
                for h in range(GH):
                    ins = pe.matmul(bank[6 + y % 2][h * SL:h * SL + HD + 1, CW - w:CW], va[:, b, j, g * GH + h, :],
                                    pb[:, blk % 2, h, 0:w], start=(j == 0), stop=True,
                                    skip_group_check=True)
                ins.then_inc(pv_done, 1)

            def yout(s, c):
                n = 2 * s + c
                pe.wait_ge(ysb_ready, n + 1)
                t_take(y_norm, n + 1)
                for t in range(CT):
                    ins = pe.transpose(T[:, t * P:(t + 1) * P], ysb[:, n % 2, t * P:(t + 1) * P], ident[:, :])
                ins.then_inc(yo_full, 1)

            def final(b, c):
                f = 2 * b + c
                pe.wait_ge(y_norm, 2 * (G * b + G - 1) + c + 1)
                t_take(fin_ready, f + 1)
                for t in range(CT):
                    ins = pe.transpose(T[:, t * P:(t + 1) * P], ytok[:, c * CT + t, :], ident[:, :])
                ins.then_inc(fin_full, 1)

            def project_out(b, c):
                f = 2 * b + c
                t_take(x_ready, 4 * CAUSAL + f + 1)
                for t in range(CT):
                    ins = pe.matmul(T[:, t * P:(t + 1) * P], hbuf[:, 0, t * P:(t + 1) * P], wp[:, 1, :],
                                    start=True, stop=True)
                ins.then_inc(acc_ready, 1)

            def causal():
                def score(s, k, h):
                    c, j = B_BLOCKS[k]
                    b, g = divmod(s, G)
                    n = (s * NBLK + k) * GH + h
                    w = min(CW, CW * (c + 1) - j * P)
                    if n == 0:
                        pe.wait_ge(kt_ready, 2 * TB)
                    if h == 0:
                        pe.wait_ge(qtb_ready, 2 * s + c + 1)
                    if n >= 3:
                        pe.wait_ge(p_ready, n - 2)
                    ins = pe.matmul(bank[1 + n % 3][:, 0:w], kz(s, h, j // CT)[:, j % CT * P:(j % CT + 1) * P],
                                    qtb[:, s % 2, (c + 1) * CW - w:(c + 1) * CW], start=True, stop=True)
                    if j < 4 * c:
                        ins.then_inc(b_full, 1)

                def mask(s, k, h):
                    c, j = B_BLOCKS[k]
                    n = (s * NBLK + k) * GH + h
                    if j >= 4 * c:
                        pe.matmul(bank[1 + n % 3][:, 0:P], identb[:, :], mask_kq[:, :], start=False, stop=True,
                                  skip_group_check=True).then_inc(b_full, 1)

                def score_max(s, k, h):
                    i, half = A_BLOCKS[k]
                    b, g = divmod(s, G)
                    n = (s * NBLK + k) * GH + h
                    w = min(CW, (i + 1) * P - half * CW)
                    if h == 0 and g == 0:
                        pe.wait_ge(kt_ready, 2 * (TB * b + i + 1))
                    if h == 0 and k in (0, 8):
                        pe.wait_ge(kz_ready, GH * (2 * s + 1 + half))
                    if n >= 2:
                        pe.wait_ge(a_free, n - 1)
                    pe.matmul(bank[4 + n % 2][:, 0:w], qta[:, slot(b, g), i * P:(i + 1) * P],
                              kz(s, h, half)[:, 0:w], start=True, stop=True).then_inc(a_full, 1)

                ln(17)
                pe.wait_ge(x_ready, 4 * CAUSAL)
                for i in range(TB + 1):
                    if i < TB:
                        make_qkv(0, i)
                    if i >= 1:
                        parts(0, i - 1, 0)
                        parts(0, i - 1, 1)
                    if i > CT:
                        for h in range(GH):
                            score_max(0, i - CT - 1, h)
                for s in range(-1, STEPS):
                    for k in range(CT if s < 0 else 0, NBLK):
                        now, ahead = s >= 0, s + 1 < STEPS
                        for h in (0, 2):
                            if ahead and h == 2:
                                score_max(s + 1, k, h)
                            if now:
                                score(s, k, h)
                            if ahead and h == 0:
                                score_max(s + 1, k, h)
                            if now:
                                score(s, k, h + 1)
                                mask(s, k, h)
                                mask(s, k, h + 1)
                            if ahead:
                                score_max(s + 1, k, h + 1)
                            if now and h == 0 and s * NBLK + k >= 1:
                                sums(s * NBLK + k - 1)
                        for todo in HOOKS.get(("pe", s, k), []):
                            if todo[0] == "ln":
                                ln(todo[1])
                            if todo[0] == "qkv":
                                make_qkv(*todo[1:])
                            if todo[0] == "parts":
                                parts(*todo[1:])
                            if todo[0] == "max":
                                maxima(*todo[1:])
                            if todo[0] == "yout":
                                yout(*todo[1:])
                            if todo[0] == "final":
                                final(*todo[1:])
                            if todo[0] == "project":
                                project_out(*todo[1:])
                            if todo[0] == "route":
                                route(todo[1], 4)
                            if todo[0] == "weights":
                                weights(4)
                sums(STEPS * NBLK - 1)
                yout(STEPS - 1, 1)
                final(1, 1)
                project_out(1, 1)

            pe.wait_ge(consts, 1)
            ln(0)
            pe.wait_ge(w2_ready, 2)
            ffn(FFN0)
            pe.wait_ge(consts, 3)
            linear(0)
            linear(1)
            ffn(FFN1)
            moe(MOE0)
            causal()
            moe(MOE1)


def constants():
    import numpy as np
    c = np.zeros((P, C_END), np.float32)
    r = np.arange(P)
    c[:, C_ID:C_ID + P] = np.eye(P)
    c[:, C_MA:C_MA + P] = np.where(r[None, :] > r[:, None], -1e30, 0.0)
    c[:, C_MB:C_MB + P] = np.where(r[:, None] > r[None, :], -1e30, 0.0)
    c[:, C_BM:C_BM + P] = r[:, None] // HD == r[None, :] // HD
    c[:, C_HS:C_HS + H] = r[:, None] // HD == np.arange(H)[None, :]
    c[:, C_IO:C_IO + E_] = np.arange(E_)
    half = HD // 2
    theta = np.float32(1.0) / np.float32(10000.0) ** (np.arange(half, dtype=np.float32) / np.float32(half))
    freqs = np.arange(S, dtype=np.float32)[:, None] * theta[None, :].astype(np.float32)
    freqs = np.repeat(freqs, 2, axis=-1).astype(np.float64)
    sign = np.where(np.arange(HD) < half, -1.0, 1.0)
    c[:, C_COS:C_COS + TB * HD] = np.cos(freqs).reshape(TB, P, HD).transpose(1, 0, 2).reshape(P, -1)
    c[:, C_SIN:C_SIN + TB * HD] = (np.sin(freqs) * sign).reshape(TB, P, HD).transpose(1, 0, 2).reshape(P, -1)
    for u in range(NU):
        for f in range(P):
            e = 2 * u + f // FE if u < E_ // 2 else E_
            for part in range(3):
                c[part * NR + e, C_SEL + u * P + f] = 1.0
    return c


def kernel(**inputs):
    import numpy as np
    import concourse.bacc as bacc
    from concourse import mybir as mb
    from concourse.bass_utils import run_bass_kernel_spmd as run

    v = {n: np.asarray(a) for n, a in inputs.items()}
    cat = np.concatenate

    def blocks(a):
        k = a.shape[0] // P
        return a.reshape(k, P, -1).transpose(1, 0, 2).reshape(P, -1)

    def experts(w, shared):
        return cat([w.transpose(1, 0, 2).reshape(D, -1), shared], 1)

    f0 = "L0_ffn_"
    m = "L1_ffn_"
    arrays = {
        "x_in": v["L0_attn_x"].reshape(B * S, D),
        "wa_in": cat([v["L0_attn_Wq"].T, v["L0_attn_Wk"].T, v["L0_attn_Wv"].T, v["L1_attn_w_qkv"],
                      v[m + "router_w"].T, v[m + "shared_gate_w"], np.zeros((D, 1), np.float32)], 1),
        "wp_in": cat([v["L0_attn_Wp"].T, v["L1_attn_w_proj"]], 1),
        "gw_in": experts(v[m + "Wg"], v[m + "Sg"]),
        "uw_in": experts(v[m + "Wu"], v[m + "Su"]),
        "dw_in": blocks(cat([v[m + "Wd"].reshape(-1, D), v[m + "Sd"]], 0)),
        "q1_in": v[f0 + "fc1_q"],
        "q2_in": blocks(v[f0 + "fc2_q"]),
        "small_in": cat([v[f0 + "fc1_scales"].reshape(FB, P).T, v[f0 + "fc1_bias"].reshape(FB, P).T,
                         v[f0 + "ln_gamma"][:, None], v[f0 + "ln_beta"][:, None],
                         v["L0_attn_conv_w"], v["L0_attn_conv_b"][:, None]], 1),
        "rows_in": cat([v[f0 + "fc2_bias"], v["L0_attn_bp"], v[f0 + "fc2_scales"].reshape(-1)])[None, :],
        "const_in": constants(),
    }
    arrays = {n: np.ascontiguousarray(a) for n, a in arrays.items()}
    nc = bacc.Bacc("TRN2", target_bir_lowering=False, num_devices=1)
    args = [nc.dram_tensor(n, a.shape, mb.dt.from_np(a.dtype), kind="ExternalInput").ap() for n, a in arrays.items()]
    out = nc.dram_tensor("y_out", (B, S, D), mb.dt.float32, kind="ExternalOutput").ap()
    macaron(nc, *args, out)
    r = run(nc, [arrays], core_ids=[0])
    return r.results[0]["y_out"]
```

```python
import concourse.bass as bass
from concourse import mybir
from contextlib import ExitStack

F32 = mybir.dt.float32
F32R = mybir.dt.float32r
BF16 = mybir.dt.bfloat16
I32 = mybir.dt.int32
U32 = mybir.dt.uint32
ALU = mybir.AluOpType
ACT = mybir.ActivationFunctionType
AX = mybir.AxisListType

P = 128
D = 128
B, S = 2, 1024
TILES = B * S // P
CT = 4
CW = CT * P
NC = TILES // CT
H, HD = 16, 8
F = 512
FB = F // P
E_, FE, FS = 16, 64, 256
NU = E_ * FE // P + FS // P
NR = E_ + 1
EPS = 1e-5
TB = S // P
G, GH = 4, 4
SL = 32
SCALE = HD ** -0.5
FFN0, LIN, FFN1, MOE0, CAUSAL, MOE1 = range(6)
FFNS = (FFN0, FFN1)
MOES = (MOE0, MOE1)
W_Q, W_KV, W_QKV, W_R, W_END = 0, 128, 384, 768, 786
C_ID, C_MA, C_MB, C_BM, C_HS, C_IO, C_COS, C_SIN, C_SEL = 0, 128, 256, 384, 512, 528, 544, 608, 672
C_END = C_SEL + NU * P
S_S1, S_B1, S_GA, S_BE, S_CW, S_CB, S_END = 0, 4, 8, 9, 10, 13, 14
R_B2, R_BP, R_S2, R_END = 0, 128, 256, 768

B_BLOCKS = [(c, j) for c in range(2) for j in range(4 * c + 4)]
A_BLOCKS = [(3, 0), (2, 0), (1, 0), (0, 0), (4, 0), (5, 0), (6, 0), (7, 0), (7, 1), (6, 1), (5, 1), (4, 1)]
NBLK = len(B_BLOCKS)
BLOCK_ORDER = (("score", 0), ("max", 0), ("score", 1), ("mask", 0), ("mask", 1), ("max", 1), ("score", 2),
               ("mask", 2), ("max", 2), ("sums", None), ("score", 3), ("mask", 3), ("max", 3))
S_DEEP, A_DEEP = 3, 3
STEPS = B * G


def schedule():
    at = {}

    def put(engine, s, k, stage, *args):
        s, k = s + k // NBLK, k % NBLK
        at.setdefault((engine, s, k), []).append((stage, *args))

    for t in range(TB + 1):
        for engine in ("pe", "act"):
            if t < TB:
                put(engine, 1, 3 * t, "qkv", 1, t)
            if t:
                put(engine, 1, 3 * t + 1, "parts", 1, t - 1, 0)
                put(engine, 1, 3 * t + 2, "parts", 1, t - 1, 1)
    for s in range(-1, STEPS + 1):
        if s + 1 < STEPS:
            for half, k in ((0, 4), (1, 12)):
                put("dve", s, k, "negate", s + 1, half)
                put("pe", s, k + 1, "max", s + 1, half)
                put("act", s, k + 1, "max", s + 1, half)
        if 0 <= s < STEPS:
            for c, k in ((0, 4), (1, 12)):
                last = s == STEPS - 1 and c == 1
                if last:
                    continue
                put("act", s, k, "yraw", s, c)
                put("pe", s, k + 3, "yout", s, c)
                put("dve", s, k + 4, "yout", s, c)
                if s % G == G - 1:
                    put("pe", s, k + 5, "final", s // G, c)
                    put("act", s, k + 5, "final", s // G, c)
                    put("pe", s, k + 6, "project", s // G, c)
                    put("dve", s, k + 7, "update", 4 * CAUSAL + 2 * (s // G) + c)
    put("dve", -1, 5, "norm", 19)
    for L, k in ((18, 2), (19, 8)):
        for engine in ("pe", "act", "dve"):
            put(engine, -1, k, "ln", L)
    for t in range(TB):
        put("pool", 1, 3 * t, "rope", 1, t)
    for s in range(2, STEPS):
        if s in (3, 4):
            for h in range(GH):
                put("act", s - 2, 8 + h, "alone", s, 0, h)
                put("act", s - 2, (15 if s == G else 12) + h, "alone", s, 1, h)
        else:
            put("pool", s - 2, 7, "alone", s, 0)
            put("pool", s - 2, 11, "alone", s, 1)
    for L, k in ((20, 7), (21, 10)):
        put("dve", 4, k, "moments", L)
        put("pool", 4, k, "norm", L)
        put("dve", 4, k + 2, "norm", L)
    for engine in ("pe", "act", "dve"):
        put(engine, 7, 2, "ln", 20)
    put("pe", 7, 4, "route", 20)
    for engine in ("dve", "act"):
        put(engine, 7, 5, "route", 20)
    put("dve", 7, 6, "weigh", 20)
    for engine in ("pe", "act"):
        put(engine, 7, 9, "weights", 20)
    return at


HOOKS = schedule()


def early():
    at = {}

    def put(engine, n, stage, *args):
        at.setdefault((engine, n), []).append((stage, *args))

    c2 = 2 * NU
    put("dve", c2 + 2, "norm", 16)
    put("dve", c2 + 3, "moments", 17)
    put("dve", c2 + 6, "norm", 17)
    for engine in ("pe", "act", "dve"):
        put(engine, c2 + 3, "ln", 16)
        put(engine, c2 + 7, "ln", 17)
    for i in range(TB):
        n = c2 + 5 + 2 * i
        for engine in ("pe", "act"):
            put(engine, n, "qkv", 0, i)
        put("dve", n + 1, "rope", 0, i)
        for which in range(2):
            for engine in ("pe first", "act first") if which else ("pe", "act"):
                put(engine, n + 3 + which, "parts", 0, i, which)
    for h in range(GH):
        put("act", c2 + 16, "alone", 0, 0, h)
        put("act", c2 + 18, "alone", 1, 0, h)
    return at


EARLY = early()


def macaron(nc, x_in, wa_in, wp_in, gw_in, uw_in, dw_in, q1_in, q2_in, small_in, rows_in, const_in, out):
    ctx = ExitStack()
    with ctx:
        def sb(name, shape, dt=F32):
            return ctx.enter_context(nc.sbuf_tensor(name, shape, dt))

        def sem(name):
            return ctx.enter_context(nc.semaphore(name))

        x = sb("x", [P, TILES, D])
        uh = sb("uh", [P, TILES * P], F32R)
        ul = sb("ul", [P, TILES * P], F32R)
        stats = sb("stats", [P, CT, 6])
        mv = sb("mv", [P, 2, CT, 2])
        rs = sb("rs", [P, 2, 3, CT])
        rtmp = sb("rtmp", [P, 2, CT])
        nhalf = sb("nhalf", [P, CT])
        hn = sb("hn", [P, 2, CT, D])
        ft = sb("ft", [P, CW])

        wh = sb("wh", [P, W_END], F32R)
        wl = sb("wl", [P, W_END], F32R)
        wp = sb("wp", [P, 2, P])
        late = sb("late", [P, 2 * 2 * H * SL], F32R)
        w1h, w1l = late[:, 0:F], late[:, F:2 * F]
        stg = late[:, :].rearrange("p (r h n) -> p r h n", r=2, h=2 * H)
        gh = sb("gh", [P, NU * P], F32R)
        gl = sb("gl", [P, NU * P], F32R)
        vh = sb("vh", [P, NU * P], F32R)
        vl = sb("vl", [P, NU * P], F32R)
        dw = sb("dw", [P, NU, D])
        small = sb("small", [P, S_END])
        bprow = sb("bprow", [P, D])
        own = sb("own", [P, 2, 2, CT])
        b2q = sb("b2q", [P, D])
        identr = sb("identr", [P, P], F32R)
        ident = identr[:, :].bitcast(F32)
        identb = sb("identb", [P, P], BF16)
        mask_kq = sb("mask_kq", [P, P], BF16)
        mask_qk = sb("mask_qk", [P, CW], BF16)
        bmask = sb("bmask", [P, P + H])
        iota = sb("iota", [P, E_])
        rope = sb("rope", [P, 2, TB, HD])
        sel = sb("sel", [3 * NR, NU, P], BF16)

        VX = 2 * TB * H * (HD + 1)
        arena = sb("arena", [P, 2 * GH * CW + VX])
        work = sb("work", [P, 8 * CW])
        hbuf = work[:, 0:4 * CW].rearrange("p (r n) -> p r n", r=4)
        sg = work[:, 4 * CW:6 * CW].rearrange("p (r n) -> p r n", r=2)
        su = work[:, 6 * CW:8 * CW].rearrange("p (r n) -> p r n", r=2)
        w2 = work[:, 5 * CW:6 * CW].rearrange("p (k d) -> p k d", k=FB)
        o = CW
        qkv1 = work[:, o:o + 6 * D].rearrange("p (r n) -> p r n", r=2); o += 6 * D
        ysb = work[:, o:o + 2 * CW].rearrange("p (r n) -> p r n", r=2); o += 2 * CW
        ytok = work[:, o:o + TB * D].rearrange("p (t d) -> p t d", t=TB); o += TB * D
        ra = work[:, o:o + 2 * D].rearrange("p (h d) -> p h d", d=HD); o += 2 * D
        rb = work[:, o:o + 2 * D].rearrange("p (h d) -> p h d", d=HD); o += 2 * D
        mx = work[:, o:o + 2 * TB * GH].rearrange("p (t h a) -> p t h a", t=TB, h=GH); o += 2 * TB * GH
        mm8 = work[:, o:o + CT * GH].rearrange("p (t h) -> p t h", t=CT); o += CT * GH
        yrec = work[:, o:o + CT * GH].rearrange("p (t h) -> p t h", t=CT); o += CT * GH
        assert o <= 8 * CW

        lg = sb("lg", [P, CT, NR + 1])
        m8 = sb("m8", [P, CT, 8])
        ix = sb("ix", [P, CT, 8], U32)
        ixf = sb("ixf", [P, CT, 2])
        dd = sb("dd", [P, 2, CT])
        th = sb("th", [P, 2, CT])
        tw = sb("tw", [P, 3, CT])
        oh = sb("oh", [P, 2, CT, E_])
        cw = sb("cw", [P, CT, NR])
        cr = sb("cr", [P, 2, CT, NR])
        cs = sb("cs", [P, CT, 3, NR], BF16)
        cwt = sb("cwt", [3 * NR, 2, CW], BF16)

        qta = sb("qta", [P, G + 2, S], F32R)
        kt = sb("kt", [P, G + 2, S], F32R)
        kza = [sb(f"kza{i}", [P, GH, CW], F32R) for i in range(3)]
        qtb = sb("qtb", [P, 2, S], F32R)
        stm = sb("stm", [P, 2, CT, GH, SL], F32R)

        raw_a = arena[:, 0:W_END]
        raw_c = arena[:, 1024:1024 + C_END]
        raw_g = arena[:, 3072:3072 + NU * P]
        raw_u = arena[:, 4352:4352 + NU * P]
        rows = arena[:, 5632:5632 + R_END]
        raw_q = work[:, 0:2 * F].bitcast(I32).rearrange("p (a n) -> p a n", a=2)
        w1f = work[:, 2 * F:3 * F]
        PADS = S + 2
        uf = arena[:, 0:2 * PADS].rearrange("p (b t) -> p b t", b=B)
        o = 2 * PADS
        qf = arena[:, o:o + S]; o += S
        kf = arena[:, o:o + S].rearrange("p (t d) -> p t d", t=TB); o += S
        vx = arena[:, o:o + TB * (D + 1)].rearrange("p (t d) -> p t d", t=TB); o += TB * (D + 1)
        relu = arena[:, o:o + 2 * CW].rearrange("p (r n) -> p r n", r=2); o += 2 * CW
        assert o <= 2 * GH * CW + VX
        loc = work[:, 6 * CW:6 * CW + S]
        mix = loc
        yt = [work[:, o:o + 2 * D].rearrange("p (t d) -> p t d", t=2) for o in (0, 2 * D, 4 * CW, 4 * CW + 2 * D)]
        expo = work[:, CW:3 * CW].rearrange("p (r n) -> p r n", r=2)
        o = CW + S
        kx = work[:, o:o + P + H]; o += P + H
        den = work[:, o:o + 4 * H].rearrange("p (r e h) -> p r e h", r=2, e=2); o += 4 * H
        rden = work[:, o:o + 4 * H].rearrange("p (r e h) -> p r e h", r=2, e=2)
        pb = arena[:, 0:2 * GH * CW].rearrange("p (r h n) -> p r h n", r=2, h=GH)
        qkv0 = arena[:, 0:6 * D].rearrange("p (r n) -> p r n", r=2)
        rot0 = [arena[:, 6 * D + 2 * D * i:8 * D + 2 * D * i].rearrange("p (h d) -> p h d", d=HD) for i in range(4)]
        qkv = (qkv0, qkv1)
        va = arena[:, 2 * GH * CW:].rearrange("p (b t h d) -> p b t h d", b=B, t=TB, h=H)

        bank = [ctx.enter_context(nc.psum_tensor(f"bank{i}", [P, CW], F32)) for i in range(8)]
        T, ACC = bank[0], bank[7]

        x_loaded = [sem(f"x_loaded{c}") for c in range(NC)]
        q_loaded, small_loaded, a_loaded = sem("q_loaded"), sem("small_loaded"), sem("a_loaded")
        c_loaded, g_loaded = sem("c_loaded"), sem("g_loaded")
        dw_loaded, stored = sem("dw_loaded"), sem("stored")
        rows_ready, borders = sem("rows_ready"), sem("borders")
        ident_ready = sem("ident_ready")
        wl_ready = sem("wl_ready")
        consts, w1_ready, w1_hi, w2_ready, prep = (
            sem("consts"), sem("w1_ready"), sem("w1_hi"), sem("w2_ready"), sem("prep"))
        hi_ready = sem("hi_ready")
        stats_ready, rstd_ready, norm_ready, xadd_ready = (
            sem("stats_ready"), sem("rstd_ready"), sem("norm_ready"), sem("xadd_ready"))
        ub_ready = sem("ub_ready")
        ln_t, ft_ready, split_ready = sem("ln_t"), sem("ft_ready"), sem("split_ready")
        lg_ready = sem("lg_ready")
        x_ready, acc_ready = sem("x_ready"), sem("acc_ready")
        dch, pch, ach = sem("dve_chain"), sem("pool_chain"), sem("act_chain")
        y_full, h_ready = sem("y_full"), sem("h_ready")
        g_full, sg_ready, hm_ready = sem("g_full"), sem("sg_ready"), sem("hm_ready")
        down_done = sem("down_done")
        lg_full, dd_ready, th_ready, cs_ready, cw_full, cwt_ready = (
            sem("lg_full"), sem("dd_ready"), sem("th_ready"), sem("cs_ready"), sem("cw_full"), sem("cwt_ready"))
        q_full, eq_ready, qf_ready = sem("q_full"), sem("eq_ready"), sem("qf_ready")
        kv_full, ek_ready, kv_ready = sem("kv_full"), sem("ek_ready"), sem("kv_ready")
        s_full, kx_ready, o_full, yt_ready, yt_full, mix_ready = (
            sem("s_full"), sem("kx_ready"), sem("o_full"), sem("yt_ready"), sem("yt_full"), sem("mix_ready"))
        stg_dve, stg_pool = sem("stg_dve"), sem("stg_pool")
        qkv_full, qkv_ready, v_ready = (
            sem("qkv_full"), sem("qkv_ready"), sem("v_ready"))
        stg_clear, kz_clear, kz_ready = sem("stg_clear"), sem("kz_clear"), [sem(f"kz_ready{s}") for s in range(STEPS)]
        kt_full, kt_ready = sem("kt_full"), sem("kt_ready")
        a_full, a_free = sem("a_full"), sem("a_free")
        stm_ready, mx_full, qtb_ready = sem("stm_ready"), sem("mx_full"), sem("qtb_ready")
        b_full, p_ready, pv_done = sem("b_full"), sem("p_ready"), sem("pv_done")
        ysb_ready, yo_full, y_norm = sem("ysb_ready"), sem("yo_full"), sem("y_norm")
        fin_full, fin_ready = sem("fin_full"), sem("fin_ready")

        block = ctx.enter_context(nc.Block())

        def acc_done(L):
            p, c = divmod(L, 4)
            if p in FFNS:
                return down_done, FB * (L - 4 * p + 1) + (NC * FB if p == FFN1 else 0)
            if p in MOES:
                return down_done, 2 * NC * FB + NU * (c + 1) + (NC * NU if p == MOE1 else 0)
            return acc_ready, c + 1 + (NC if p == CAUSAL else 0)

        def stg_done(n):
            if n < TB and n % 2:
                return stg_dve, n // 2 + 1
            return stg_pool, n // 2 + 1 if n < TB else TB // 2 + n - TB + 1

        def slot(b, g):
            return (g + 2) % G if b == 0 else g + 2

        def kz(s, h, half):
            if s % 2 == 0 and half:
                return (uh, ul)[h // 2][:, h % 2 * CW:(h % 2 + 1) * CW]
            return kza[0 if s % 2 == 0 else 1 + half][:, h, :]

        def lin_bank(b, n):
            return bank[1 + (n + b) % 6]

        def s_bank(n):
            return bank[1 + n % S_DEEP]

        def a_bank(n):
            return bank[1 + n % 5] if n < NBLK * GH else bank[1 + S_DEEP + n % A_DEEP]

        def tok(c):
            return slice(c * CW, (c + 1) * CW)

        @block.sync
        def _(sp):
            xv = x_in.rearrange("(t p) d -> p t d", p=P)
            ov = out.rearrange("b (t p) d -> p b t d", p=P)
            for c in range(NC):
                sp.dma_start(x[:, c * CT:(c + 1) * CT, :], xv[:, c * CT:(c + 1) * CT, :]).then_inc(x_loaded[c], 16)
                if c == 0:
                    sp.dma_start(raw_q[:, 0, :], q1_in).then_inc(q_loaded, 16)
                    sp.dma_start(raw_q[:, 1, :], q2_in).then_inc(q_loaded, 16)
            sp.dma_start(raw_g, gw_in).then_inc(g_loaded, 16)
            sp.dma_start(raw_u, uw_in).then_inc(g_loaded, 16)
            sp.dma_start(dw[:, :, :].rearrange("p u d -> p (u d)"), dw_in).then_inc(dw_loaded, 16)
            for c in range(NC):
                sp.wait_ge(x_ready, 4 * MOE1 + c + 1)
                sp.dma_start(ov[:, c // 2, (c % 2) * CT:(c % 2 + 1) * CT, :],
                             x[:, c * CT:(c + 1) * CT, :]).then_inc(stored, 16)
            sp.wait_ge(stored, 16 * NC)

        @block.gpsimd
        def _(pool):
            chain = [0]

            def link(ins):
                chain[0] += 1
                ins.then_inc(pch, 1)
                pool.wait_ge(pch, chain[0])

            def rstd(L):
                r = L % 2
                pool.wait_ge(stats_ready, L + 1)
                var = mv[:, r, :, 1]
                r1, r2, r3 = (rs[:, r, n, :] for n in range(3))
                t = rtmp[:, r, :]
                link(pool.tensor_scalar(t, var, EPS, None, ALU.add))
                p = pool.tensor_tensor(r1, t, nhalf[:, :], ALU.pow)
                if L // 4 not in FFNS:
                    p.then_inc(rstd_ready, 1)
                    return
                link(p)
                link(pool.tensor_tensor(t, r1, r1, ALU.mult))
                link(pool.tensor_tensor(t, t, var, ALU.mult))
                link(pool.tensor_scalar(t, t, EPS, None, ALU.add))
                link(pool.tensor_tensor(r2, t, nhalf[:, :], ALU.pow))
                if L >= 2:
                    pool.wait_ge(ub_ready, L - 1 if L < 4 else L - 5)
                pool.tensor_scalar(own[:, r, 0, :], r1, 0.5, 1.0, ALU.mult, ALU.add)
                link(pool.tensor_tensor(t, r1, mv[:, r, :, 0], ALU.mult))
                pool.tensor_scalar(own[:, r, 1, :], t, -0.5, None, ALU.mult)
                pool.tensor_tensor(r3, r1, r2, ALU.mult).then_inc(rstd_ready, 1)

            def xadd(L):
                c = L % 4
                row = bprow if L // 4 == LIN else b2q
                pool.wait_ge(norm_ready, L + 1)
                if L // 4 in FFNS:
                    pool.wait_ge(ub_ready, L % 4 + 1 + (4 if L // 4 == FFN1 else 0))
                xc = x[:, c * CT:(c + 1) * CT, :]
                pool.tensor_tensor(xc, xc, row[:, :].unsqueeze(1).to_broadcast([P, CT, D]), ALU.add)\
                    .then_inc(xadd_ready, 1)

            def rotate(b, i):
                n = TB * b + i
                a1, a2 = (ra, rb) if b else rot0[0:2]
                pool.wait_ge(qkv_ready, n + 1)
                s = stg[:, n % 2, :, :]
                qk = qkv[b][:, n % 2, 0:2 * D].rearrange("p (h d) -> p h d", d=HD)
                pool.tensor_tensor(a1[:, :, :], qk, rope[:, 0, i, :].unsqueeze(1).to_broadcast([P, 2 * H, HD]),
                                   ALU.mult)
                hh = HD // 2
                for a in range(2):
                    src = slice((1 - a) * hh, (2 - a) * hh)
                    dst = slice(a * hh, (a + 1) * hh)
                    sin = rope[:, 1, i, dst].unsqueeze(1).to_broadcast([P, 2 * H, hh])
                    ins = pool.tensor_tensor(a2[:, :, dst], qk[:, :, src], sin, ALU.mult)
                link(ins)
                link(pool.tensor_tensor(a1[:, :, :], a1[:, :, :], a2[:, :, :], ALU.add))
                if n >= 2:
                    pool.wait_ge(kt_full, 2 * n - 2)
                pool.tensor_copy(s[:, 0:H, 0:2 * HD].rearrange("p h (a d) -> p h a d", a=2),
                                 a1[:, 0:H, :].unsqueeze(2).to_broadcast([P, H, 2, HD]))
                link(pool.tensor_copy(s[:, H:, 0:3 * HD].rearrange("p h (a d) -> p h a d", a=3)[:, :, 0:3:2, :],
                                      a1[:, H:, :].unsqueeze(2).to_broadcast([P, H, 2, HD])))
                sf = s.bitcast(F32)
                pool.tensor_tensor(s[:, 0:H, 2 * HD:3 * HD], a1[:, 0:H, :], sf[:, 0:H, 0:HD], ALU.subtract)
                pool.tensor_tensor(s[:, H:, HD:2 * HD], a1[:, H:, :], sf[:, H:, 0:HD], ALU.subtract)\
                    .then_inc(stg_pool, 1)
                pool.wait_ge(*stg_done(n))

            def tile(b, i):
                n = TB * b + i
                pool.wait_ge(qkv_ready, n + 1)
                pool.tensor_copy(va[:, b, i, :, 0:HD],
                                 qkv[b][:, n % 2, 2 * D:].rearrange("p (h d) -> p h d", h=H)).then_inc(v_ready, 1)
                pool.wait_ge(v_ready, n + 1)

            def alone(s, half):
                b, g = divmod(s, G)
                n = GH * half
                pool.wait_ge(kt_ready, 2 * (TB * b + CT * (half + 1)))
                if s >= 2:
                    pool.wait_ge(b_full, ((s - 2) * NBLK + (12 if half else 8)) * GH)
                for h in range(GH):
                    r = slice(h * SL, (h + 1) * SL)
                    pool.tensor_copy(kz(s, h, half)[r, :], kt[r, slot(b, g), tok(half)].bitcast(F32))\
                        .then_inc(kz_ready[s], 1)
                    pool.wait_ge(kz_ready[s], n + h + 1)

            pool.memset(nhalf[:, :], -0.5)
            rstd(0)
            pool.wait_ge(small_loaded, 32)
            pool.tensor_scalar(b2q[:, :], rows[:, R_B2:R_B2 + D], 0.25, None, ALU.mult)
            pool.tensor_copy(bprow[:, :], rows[:, R_BP:R_BP + D]).then_inc(rows_ready, 1)
            pool.wait_ge(rows_ready, 1)
            rstd(1)
            xadd(0)
            rstd(2)
            xadd(1)
            rstd(3)
            pool.wait_ge(c_loaded, 16)
            pool.tensor_copy(identb[:, :], raw_c[:, C_ID:C_ID + P])
            pool.memset(mask_qk[:, 0:CW - P], 0.0)
            pool.tensor_copy(mask_qk[:, CW - P:], raw_c[:, C_MA:C_MA + P])
            pool.tensor_copy(mask_kq[:, :], raw_c[:, C_MB:C_MB + P])
            pool.tensor_copy(bmask[:, :], raw_c[:, C_BM:C_BM + P + H])
            pool.tensor_copy(iota[:, :], raw_c[:, C_IO:C_IO + E_])
            pool.tensor_copy(rope[:, :, :, :], raw_c[:, C_COS:C_COS + 2 * TB * HD]
                             .rearrange("p (a t d) -> p a t d", a=2, t=TB)).then_inc(consts, 1)
            pool.wait_ge(hi_ready, 1)
            pool.tensor_tensor(wl[:, :], raw_a, wh[:, :].bitcast(F32), ALU.subtract).then_inc(wl_ready, 1)
            xadd(2)
            for L in range(4, 20):
                if L == 16:
                    pool.wait_ge(x_ready, 4 * LIN + 4)
                    pool.memset(va[:, :, :, :, HD:HD + 1], 1.0)
                    pool.wait_ge(x_ready, 4 * FFN1 + 4)
                    link(pool.memset(stg[:, :, :, :].bitcast(F32), 0.0))
                    pool.memset(stg[:, :, H:, 3 * HD:3 * HD + 2].bitcast(F32), 1.0).then_inc(stg_clear, 1)
                if L < 18:
                    rstd(L)
                    if L <= 12:
                        xadd(L - 1)
                if L == 14:
                    pool.memset(stm[:, :, :, :, :].bitcast(F32), 0.0)
                    for z in kza:
                        pool.memset(z[:, :, :].bitcast(F32), 0.0)
            for i in range(TB):
                tile(0, i)
                if i % 2 == 0:
                    rotate(0, i)
                if i == 4:
                    rstd(18)
            rstd(19)
            for s in range(-1, STEPS):
                for k in range(NBLK):
                    for todo in HOOKS.get(("pool", s, k), []):
                        if todo[0] == "rope":
                            tile(*todo[1:])
                            rotate(1, todo[2])
                        if todo[0] == "alone":
                            alone(*todo[1:])
                        if todo[0] == "norm":
                            rstd(todo[1])
                            pool.wait_ge(rstd_ready, todo[1] + 1)
            rstd(22)
            rstd(23)

        @block.scalar
        def _(act):
            chain = [0]

            def link(ins):
                chain[0] += 1
                ins.then_inc(ach, 1)
                act.wait_ge(ach, chain[0])

            act.dma_start(small[:, :], small_in).then_inc(small_loaded, 16)
            act.dma_start(rows, rows_in.to_broadcast([P, R_END])).then_inc(small_loaded, 16)
            act.dma_start(raw_c, const_in).then_inc(c_loaded, 16)
            act.dma_start(raw_a, wa_in).then_inc(a_loaded, 16)
            act.dma_start(wp[:, :, :].rearrange("p a n -> p (a n)"), wp_in).then_inc(a_loaded, 16)

            def ln(L):
                p, c = divmod(L, 4)
                act.wait_ge(ln_t, L + 1)
                if L >= 1:
                    act.wait_ge(split_ready, L)
                dst = ft[:, :]
                if p == LIN:
                    dst = uf[:, c // 2, 1 + (c % 2) * CW:1 + (c % 2 + 1) * CW]
                    act.wait_ge(prep, 2)
                    act.wait_ge(consts, 2)
                    act.wait_ge(wl_ready, 1)
                    act.wait_ge(w2_ready, 2)
                if p in FFNS:
                    ins = act.activation(dst, T[:, :], ACT.Identity, bias=small[:, S_BE:S_BE + 1],
                                         scale=small[:, S_GA:S_GA + 1])
                else:
                    ins = act.activation(dst, T[:, :], ACT.Copy)
                ins.then_inc(ft_ready, 1)

            def residual(L):
                r, c = L % 2, L % 4
                for t in range(CT):
                    xt = x[:, c * CT + t, :]
                    ins = act.activation(xt, xt, ACT.Identity, bias=own[:, r, 1, t:t + 1],
                                         scale=own[:, r, 0, t:t + 1])
                ins.then_inc(ub_ready, 1)

            def ffn(p):
                for n in range(NC * FB):
                    k, m = n % FB, n + (16 if p == FFN1 else 0)
                    act.wait_ge(y_full, m + 1)
                    if m >= 4:
                        act.wait_ge(down_done, m - 3)
                    act.activation(hbuf[:, m % 4, :], bank[1 + m % 4][:, :], ACT.Silu,
                                   bias=small[:, S_B1 + k:S_B1 + k + 1],
                                   scale=small[:, S_S1 + k:S_S1 + k + 1]).then_inc(h_ready, 1)
                    if k == 1:
                        ln(4 * p + n // FB + 1)
                    if k == 2 and n // FB < NC - 1:
                        residual(4 * p + n // FB + 1)
                    if p == FFN0 and k == 3:
                        if n // FB == 0:
                            act.wait_ge(g_loaded, 32)
                            act.activation(gh[:, :], raw_g, ACT.Copy).then_inc(hi_ready, 1)
                        if n // FB == 1:
                            act.activation(vh[:, :], raw_u, ACT.Copy).then_inc(hi_ready, 1)
                        if n // FB == 2:
                            act.activation(sel[:, :, :], raw_c[0:3 * NR, C_SEL:C_END]
                                           .rearrange("p (u n) -> p u n", u=NU), ACT.Copy).then_inc(consts, 1)
                if p == FFN1:
                    route(0)

            def features(dst_r, dst_e, src):
                act.activation(dst_r, src, ACT.Relu)
                return act.activation(dst_e, src, ACT.Exp)

            def q_features(b, c):
                act.wait_ge(q_full, 2 * b + c + 1)
                if b:
                    act.wait_ge(kv_ready, 3 + c)
                features(relu[:, c, :], expo[:, c, :], lin_bank(b, c)[:, :]).then_inc(eq_ready, 1)

            def kv_features(b, t):
                n = 4 * b + t
                act.wait_ge(kv_full, n + 1)
                act.wait_ge(qf_ready, 2 * b + t + 1) if t < 2 else act.wait_ge(kv_ready, n - 1)
                kvp = lin_bank(b, 2 + t)[:, :].rearrange("p (t n) -> p t n", t=2)
                features(relu[:, t % 2, 0:2 * D].rearrange("p (t n) -> p t n", t=2),
                         expo[:, t % 2, 0:2 * D].rearrange("p (t n) -> p t n", t=2), kvp[:, :, 0:D])
                act.activation(vx[:, 2 * t:2 * t + 2, 0:D], kvp[:, :, D:2 * D], ACT.Copy).then_inc(ek_ready, 1)

            def linear():
                ln(5)
                q_features(0, 0)
                q_features(0, 1)
                for t in range(4):
                    kv_features(0, t)
                ln(6)
                ln(7)
                q_features(1, 0)
                q_features(1, 1)
                for t in range(4):
                    kv_features(1, t)
                ln(8)
                residual(8)

            def route(r):
                act.wait_ge(dd_ready, r + 1)
                act.activation(th[:, :, :], dd[:, :, :], ACT.Tanh, scale=0.5).then_inc(th_ready, 1)

            def weights(r):
                act.wait_ge(cw_full, r + 1)
                act.activation(cwt[:, r % 2, :], T[0:3 * NR, 0:CW // 2].bitcast(BF16), ACT.Copy)\
                    .then_inc(cwt_ready, 1)

            def moe(p):
                r0 = 4 if p == MOE1 else 0
                if p == MOE0:
                    weights(r0)
                for n in range(NC * NU):
                    c, u = divmod(n, NU)
                    m = n + (NC * NU if p == MOE1 else 0)
                    if p == MOE0:
                        tiles(n, " first")
                    act.wait_ge(g_full, m + 1)
                    if m >= 2:
                        act.wait_ge(hm_ready, m - 1)
                    act.activation(sg[:, m % 2, :], bank[1 + m % 2][:, :], ACT.Silu).then_inc(sg_ready, 1)
                    L = 4 * p + c + 1
                    if u == 1 and L < 24 and L != 16:
                        ln(L)
                    if p == MOE0:
                        tiles(n)
                    if c < 3 and u == 5:
                        route(r0 + c + 1)
                    if c < 3 and u == 8:
                        weights(r0 + c + 1)

            def tiles(n, first=""):
                for todo in EARLY.get(("act" + first, n), []):
                    if todo[0] == "ln":
                        ln(todo[1])
                    if todo[0] == "qkv":
                        qkv_out(*todo[1:])
                    if todo[0] == "parts":
                        parts(*todo[1:])
                    if todo[0] == "alone":
                        alone(*todo[1:])

            def qkv_out(b, i):
                n = TB * b + i
                act.wait_ge(qkv_full, n + 1)
                if n % TB >= 2:
                    act.wait_ge(*stg_done(n - 2))
                    act.wait_ge(v_ready, n - 1)
                act.activation(qkv[b][:, n % 2, :], T[:, 0:3 * D], ACT.Copy).then_inc(qkv_ready, 1)

            def parts(b, i, which):
                n = 2 * (TB * b + i) + which
                act.wait_ge(kt_full, n + 1)
                act.activation((kt, qta)[which][:, 2 * b:2 * b + G, i * P:(i + 1) * P],
                               T[:, :].rearrange("p (g t) -> p g t", g=G), ACT.Copy).then_inc(kt_ready, 1)

            def maxima(s, half):
                act.wait_ge(mx_full, 2 * s + half + 1)
                act.activation(qtb[:, s % 2, tok(half)], T[:, :], ACT.Copy).then_inc(qtb_ready, 1)

            def alone(s, half, h):
                b, g = divmod(s, G)
                r = slice(h * SL, (h + 1) * SL)
                if h == 0:
                    act.wait_ge(kt_ready, 2 * (TB * b + CT * (half + 1)))
                    if s == 0 and half:
                        act.wait_ge(kz_clear, 1)
                    if s >= 2:
                        act.wait_ge(b_full, ((s - 2) * NBLK + (12 if half else 8)) * GH)
                act.activation(kz(s, h, half)[r, :], kt[r, slot(b, g), tok(half)].bitcast(F32), ACT.Copy)\
                    .then_inc(kz_ready[s], 1)

            def causal():
                for n in range(NC * NU, NC * NU + 4):
                    tiles(n, " first")
                    tiles(n)
                for s in range(2):
                    for h in range(GH):
                        alone(s, 1, h)
                for s in range(-1, STEPS):
                    for k, (c, j) in enumerate(B_BLOCKS):
                        if s >= 0:
                            blk = s * NBLK + k
                            w = min(CW, CW * (c + 1) - j * P)
                            for h in range(GH):
                                n = blk * GH + h
                                act.wait_ge(b_full, n + 1)
                                if h == 0 and blk >= 2:
                                    act.wait_ge(pv_done, blk - 1)
                                act.activation(pb[:, blk % 2, h, 0:w], s_bank(n)[:, 0:w], ACT.Exp,
                                               scale=SCALE).then_inc(p_ready, 1)
                        for todo in HOOKS.get(("act", s, k), []):
                            if todo[0] == "ln":
                                ln(todo[1])
                            if todo[0] == "qkv":
                                qkv_out(*todo[1:])
                            if todo[0] == "parts":
                                parts(*todo[1:])
                            if todo[0] == "max":
                                maxima(*todo[1:])
                            if todo[0] == "yraw":
                                yraw(*todo[1:])
                            if todo[0] == "final":
                                final(*todo[1:])
                            if todo[0] == "alone":
                                alone(*todo[1:])
                            if todo[0] == "route":
                                route(4)
                            if todo[0] == "weights":
                                weights(4)
                yraw(STEPS - 1, 1)
                final(1, 1)

            def yraw(s, c):
                n = 2 * s + c
                act.wait_ge(pv_done, s * NBLK + (4 if c == 0 else 12))
                if n >= 2:
                    act.wait_ge(yo_full, n - 1)
                act.activation(ysb[:, n % 2, :], bank[7][:, :], ACT.Copy).then_inc(ysb_ready, 1)

            def final(b, c):
                f = 2 * b + c
                act.wait_ge(fin_full, f + 1)
                if f >= 1:
                    act.wait_ge(*acc_done(4 * CAUSAL + f - 1))
                act.activation(hbuf[:, 0, :], T[:, :], ACT.Copy).then_inc(fin_ready, 1)

            act.wait_ge(w1_ready, 1)
            act.activation(w1h[:, :], w1f[:, :], ACT.Copy).then_inc(w1_hi, 1)
            act.wait_ge(c_loaded, 16)
            act.activation(identr[:, :], raw_c[:, C_ID:C_ID + P], ACT.Copy).then_inc(ident_ready, 1)
            ln(0)
            residual(0)
            act.wait_ge(a_loaded, 32)
            act.activation(wh[:, :], raw_a, ACT.Copy).then_inc(hi_ready, 1)
            ffn(FFN0)
            linear()
            ffn(FFN1)
            moe(MOE0)
            causal()
            moe(MOE1)

        @block.vector
        def _(dve):
            chain = [0]

            def link(ins):
                chain[0] += 1
                ins.then_inc(dch, 1)
                dve.wait_ge(dch, chain[0])

            def moments(L):
                p, c = divmod(L, 4)
                r = L % 2
                if p == 0:
                    dve.wait_ge(x_loaded[c], 16)
                else:
                    dve.wait_ge(x_ready, L - 3)
                if L >= 1:
                    dve.wait_ge(stats_ready, L)
                for t in range(CT):
                    ins = dve.bn_stats(stats[:, t, :], x[:, c * CT + t, :])
                link(ins)
                for t in range(CT):
                    ins = dve.bn_aggr(mv[:, r, t, :], stats[:, t, :])
                ins.then_inc(stats_ready, 1)

            def norm(L):
                p, c = divmod(L, 4)
                r = L % 2
                dve.wait_ge(rstd_ready, L + 1)
                dve.wait_ge(stats_ready, L + 1)
                if L >= 2:
                    dve.wait_ge(ln_t, L - 1)
                for t in range(CT):
                    ins = dve.tensor_scalar(hn[:, r, t, :], x[:, c * CT + t, :], mv[:, r, t, 0:1],
                                            rs[:, r, 2 if p in FFNS else 0, t:t + 1], ALU.subtract, ALU.mult)
                ins.then_inc(norm_ready, 1)

            def split(L):
                p, c = divmod(L, 4)
                dve.wait_ge(ft_ready, L + 1)
                src = ft[:, :]
                if p == LIN:
                    src = uf[:, c // 2, 1 + (c % 2) * CW:1 + (c % 2 + 1) * CW]
                if L in (20, 21):
                    dve.wait_ge(b_full, 7 * NBLK * GH)
                link(dve.tensor_copy(uh[:, tok(c)], src))
                dve.tensor_tensor(ul[:, tok(c)], src, uh[:, tok(c)].bitcast(F32), ALU.subtract)\
                    .then_inc(split_ready, 1)

            def update(L, scale, acc=ACC):
                c = L % 4
                dve.wait_ge(*acc_done(L))
                if L < 12:
                    dve.wait_ge(xadd_ready, L + 1)
                xc = x[:, c * CT:(c + 1) * CT, :]
                dve.scalar_tensor_tensor(out=xc, in0=acc[:, :].rearrange("p (t d) -> p t d", t=CT), scalar=scale,
                                         in1=xc, op0=ALU.mult, op1=ALU.add).then_inc(x_ready, 1)

            def ffn(p):
                for c in range(NC):
                    L = 4 * p + c
                    split(L + 1)
                    norm(L + 2)
                    if L + 1 == 4 * MOE0:
                        route(0)
                    update(L, 0.25)
                    if L + 1 == 4 * MOE0:
                        weigh(0)
                    moments(L + 3)
                    if p == FFN0 and c in (1, 2):
                        hi, lo, raw = ((gh, gl, raw_g), (vh, vl, raw_u))[c - 1]
                        dve.wait_ge(hi_ready, c + 1)
                        dve.tensor_tensor(lo[:, :], raw, hi[:, :].bitcast(F32), ALU.subtract).then_inc(prep, 1)
                    if p == FFN0 and c == 2:
                        dve.wait_ge(prep, 2)
                        dve.wait_ge(wl_ready, 1)
                        dve.wait_ge(consts, 2)
                        dve.memset(uf[:, :, 0:1], 0.0)
                        dve.memset(uf[:, :, S + 1:S + 2], 0.0)
                        dve.memset(vx[:, :, D:D + 1], 1.0).then_inc(borders, 1)

            def q_map(b, c):
                dve.wait_ge(eq_ready, 2 * b + c + 1)
                dve.scalar_tensor_tensor(out=qf[:, tok(c)], in0=expo[:, c, :], scalar=1.0, in1=relu[:, c, :],
                                         op0=ALU.min, op1=ALU.add).then_inc(qf_ready, 1)

            def k_map(b, t):
                dve.wait_ge(ek_ready, 4 * b + t + 1)
                n0 = relu[:, t % 2, 0:2 * D].rearrange("p (t n) -> p t n", t=2)
                n1 = expo[:, t % 2, 0:2 * D].rearrange("p (t n) -> p t n", t=2)
                dve.scalar_tensor_tensor(out=kf[:, 2 * t:2 * t + 2, :], in0=n1, scalar=1.0, in1=n0,
                                         op0=ALU.min, op1=ALU.add).then_inc(kv_ready, 1)

            def conv(b):
                u = uf[:, b, :]
                link(dve.tensor_scalar(loc, u[:, 0:S], small[:, S_CW:S_CW + 1], small[:, S_CB:S_CB + 1],
                                       ALU.mult, ALU.add))
                for w in range(1, 3):
                    link(dve.scalar_tensor_tensor(out=loc, in0=u[:, w:w + S],
                                                  scalar=small[:, S_CW + w:S_CW + w + 1], in1=loc,
                                                  op0=ALU.mult, op1=ALU.add))

            def state(b):
                dve.wait_ge(s_full, b + 1)
                sv = lin_bank(b, 0)
                dve.tensor_tensor(kx[:, 0:P], sv[:, 0:P], bmask[:, 0:P], ALU.mult)
                dve.tensor_scalar(kx[:, P:P + H], bmask[:, P:P + H], sv[:, P:P + 1], None, ALU.mult)\
                    .then_inc(kx_ready, 1)

            def divide(b, t):
                n = 4 * b + t
                dve.wait_ge(o_full, n + 1)
                ov = lin_bank(b, 1 + t)[:, :].rearrange("p (t n) -> p t n", t=2)
                link(dve.tensor_scalar(den[:, t % 2, :, :], ov[:, :, P:P + H], 1e-6, None, ALU.max))
                link(dve.reciprocal(rden[:, t % 2, :, :], den[:, t % 2, :, :]))
                if b:
                    dve.wait_ge(yt_full, n - 3)
                for e in range(2):
                    ins = dve.tensor_tensor(
                        yt[t][:, e, :].rearrange("p (h d) -> p h d", h=H),
                        ov[:, e, 0:P].rearrange("p (h d) -> p h d", h=H),
                        rden[:, t % 2, e, :].unsqueeze(2).to_broadcast([P, H, HD]), ALU.mult)
                ins.then_inc(yt_ready, 1)

            def add_local(b, t):
                dve.wait_ge(yt_full, 4 * b + t + 1)
                cols = slice(t * 2 * P, (t + 1) * 2 * P)
                dve.tensor_tensor(mix[:, cols], lin_bank(b, (5, 0)[t % 2])[:, 0:2 * P], loc[:, cols], ALU.add)\
                    .then_inc(mix_ready, 1)

            def linear():
                split(5)
                norm(6)
                q_map(0, 0)
                q_map(0, 1)
                moments(7)
                for t in range(4):
                    k_map(0, t)
                split(6)
                state(0)
                norm(7)
                conv(0)
                divide(0, 0)
                divide(0, 1)
                divide(0, 2)
                add_local(0, 0)
                divide(0, 3)
                split(7)
                add_local(0, 1)
                add_local(0, 2)
                update(4, 1.0)
                add_local(0, 3)
                moments(8)
                q_map(1, 0)
                q_map(1, 1)
                update(5, 1.0)
                k_map(1, 0)
                k_map(1, 1)
                moments(9)
                k_map(1, 2)
                k_map(1, 3)
                norm(8)
                state(1)
                conv(1)
                divide(1, 0)
                divide(1, 1)
                split(8)
                divide(1, 2)
                add_local(1, 0)
                divide(1, 3)
                add_local(1, 1)
                add_local(1, 2)
                update(6, 1.0)
                add_local(1, 3)
                norm(9)
                update(7, 1.0)
                moments(10)

            def route(r):
                dve.wait_ge(lg_full, r + 1)
                if r >= 1:
                    dve.wait_ge(cs_ready, r)
                lv = T[:, 0:CT * 32].rearrange("p (t n) -> p t n", t=CT)
                dve.tensor_copy(dd[:, 1, :], lv[:, :, E_])
                dve.tensor_copy(lg[:, :, :], lv[:, :, 0:NR + 1]).then_inc(lg_ready, 1)
                dve.wait_ge(lg_ready, r + 1)
                for t in range(CT):
                    ins = dve.max(m8[:, t, :], lg[:, t, 0:E_])
                link(ins)
                for t in range(CT):
                    dve.max_index(ix[:, t, :], m8[:, t, :], lg[:, t, 0:E_])
                dve.tensor_tensor(dd[:, 0, :], m8[:, :, 0], m8[:, :, 1], ALU.subtract).then_inc(dd_ready, 1)

            def weigh(r):
                dve.wait_ge(dd_ready, r + 1)
                dve.tensor_copy(ixf[:, :, :], ix[:, :, 0:2])
                dve.wait_ge(th_ready, r + 1)
                dve.tensor_scalar(tw[:, 0, :], th[:, 0, :], 0.5, 0.5, ALU.mult, ALU.add)
                dve.tensor_scalar(cw[:, :, E_], th[:, 1, :], 0.5, 0.5, ALU.mult, ALU.add)
                link(dve.tensor_scalar(tw[:, 1, :], th[:, 0, :], -0.5, 0.5, ALU.mult, ALU.add))
                io = iota[:, :].unsqueeze(1).to_broadcast([P, CT, E_])
                for a in range(2):
                    ins = dve.tensor_tensor(oh[:, a, :, :], io, ixf[:, :, a].unsqueeze(2).to_broadcast([P, CT, E_]),
                                            ALU.is_equal)
                link(ins)
                for a in range(2):
                    ins = dve.tensor_tensor(oh[:, a, :, :], oh[:, a, :, :],
                                            tw[:, a, :].unsqueeze(2).to_broadcast([P, CT, E_]), ALU.mult)
                link(ins)
                link(dve.tensor_tensor(cw[:, :, 0:E_], oh[:, 0, :, :], oh[:, 1, :, :], ALU.add))
                link(dve.tensor_copy(cs[:, :, 0, :], cw[:, :, :]))
                link(dve.tensor_tensor(cr[:, 0, :, :], cw[:, :, :], cs[:, :, 0, :], ALU.subtract))
                link(dve.tensor_copy(cs[:, :, 1, :], cr[:, 0, :, :]))
                dve.tensor_tensor(cs[:, :, 2, :], cr[:, 0, :, :], cs[:, :, 1, :], ALU.subtract).then_inc(cs_ready, 1)

            def moe(p):
                r0 = 4 if p == MOE1 else 0
                for n in range(NC * NU):
                    c, u = divmod(n, NU)
                    m = n + (NC * NU if p == MOE1 else 0)
                    L = 4 * p + c
                    dve.wait_ge(sg_ready, m + 1)
                    link(dve.tensor_tensor(su[:, m % 2, :], sg[:, m % 2, :], bank[3 + m % 2][:, :], ALU.mult))
                    if m >= 3:
                        dve.wait_ge(down_done, 2 * NC * FB + m - 2)
                    dve.tensor_tensor(hbuf[:, m % 3, :], su[:, m % 2, :], bank[5 + m % 2][:, :], ALU.mult)\
                        .then_inc(hm_ready, 1)
                    if u == 1 and c > 0:
                        update(L - 1, 0.5)
                    if u == 1 and L + 1 < 24 and L + 1 != 16:
                        split(L + 1)
                    if u == 2 and L + 2 < 24 and L + 2 not in (16, 17):
                        norm(L + 2)
                    if u == 3 and L + 3 < 24 and L + 3 != 17:
                        moments(L + 3)
                    if p == MOE0:
                        tiles(n)
                    if c < 3 and u == 4:
                        route(r0 + c + 1)
                    if c < 3 and u == 5:
                        weigh(r0 + c + 1)
                update(4 * p + 3, 0.5)

            def tiles(n):
                for todo in EARLY.get(("dve", n), []):
                    if todo[0] == "moments":
                        moments(todo[1])
                    if todo[0] == "norm":
                        norm(todo[1])
                    if todo[0] == "ln":
                        split(todo[1])
                    if todo[0] == "rope" and todo[2] % 2:
                        rotate(todo[2])

            def rotate(i):
                a1, a2 = rot0[2:4]
                dve.wait_ge(qkv_ready, i + 1)
                dve.wait_ge(stg_clear, 1)
                s = stg[:, i % 2, :, :]
                qk = qkv0[:, i % 2, 0:2 * D].rearrange("p (h d) -> p h d", d=HD)
                dve.tensor_tensor(a1[:, :, :], qk, rope[:, 0, i, :].unsqueeze(1).to_broadcast([P, 2 * H, HD]),
                                  ALU.mult)
                hh = HD // 2
                for a in range(2):
                    src = slice((1 - a) * hh, (2 - a) * hh)
                    dst = slice(a * hh, (a + 1) * hh)
                    sin = rope[:, 1, i, dst].unsqueeze(1).to_broadcast([P, 2 * H, hh])
                    ins = dve.tensor_tensor(a2[:, :, dst], qk[:, :, src], sin, ALU.mult)
                link(ins)
                link(dve.tensor_tensor(a1[:, :, :], a1[:, :, :], a2[:, :, :], ALU.add))
                if i >= 2:
                    dve.wait_ge(kt_full, 2 * i - 2)
                dve.tensor_copy(s[:, 0:H, 0:2 * HD].rearrange("p h (a d) -> p h a d", a=2),
                                a1[:, 0:H, :].unsqueeze(2).to_broadcast([P, H, 2, HD]))
                link(dve.tensor_copy(s[:, H:, 0:3 * HD].rearrange("p h (a d) -> p h a d", a=3)[:, :, 0:3:2, :],
                                     a1[:, H:, :].unsqueeze(2).to_broadcast([P, H, 2, HD])))
                sf = s.bitcast(F32)
                dve.tensor_tensor(s[:, 0:H, 2 * HD:3 * HD], a1[:, 0:H, :], sf[:, 0:H, 0:HD], ALU.subtract)
                dve.tensor_tensor(s[:, H:, HD:2 * HD], a1[:, H:, :], sf[:, H:, 0:HD], ALU.subtract)\
                    .then_inc(stg_dve, 1)

            def maxima(s, k):
                i, half = A_BLOCKS[k]
                w = min(CW, (i + 1) * P - half * CW)
                for h in range(GH):
                    n = (s * NBLK + k) * GH + h
                    dve.wait_ge(a_full, n + 1)
                    src = a_bank(n)[:, 0:w]
                    dst = mx[:, i, h, half:half + 1]
                    if i * P < half * CW + w:
                        ins = dve.tensor_tensor_reduce(out=src, in0=src, in1=mask_qk[:, CW - w:], scale=1.0,
                                                       scalar=-3e38, op0=ALU.add, op1=ALU.max, accum_out=dst)
                    else:
                        ins = dve.tensor_reduce(dst, src, AX.X, ALU.max)
                    ins.then_inc(a_free, 1)
                    if h == 1:
                        drains(s - 1, k)

            def drains(s, k):
                for todo in HOOKS.get(("dve", s, k), []):
                    if todo[0] == "yout":
                        yout(*todo[1:])
                    if todo[0] == "update":
                        update(todo[1], 1.0, T)
                    if todo[0] == "route":
                        route(4)
                    if todo[0] == "weigh":
                        weigh(4)

            def negate(s, half):
                n = 2 * s + half
                b, g = divmod(s, G)
                t0 = half * CT
                dve.wait_ge(a_free, s * NBLK * GH + (4 if half == 0 else NBLK) * GH)
                m = mx[:, t0:t0 + CT, :, 0]
                if half:
                    link(dve.tensor_tensor(mm8, m, mx[:, t0:t0 + CT, :, 1], ALU.max))
                    m = mm8
                if n >= 2:
                    dve.wait_ge(mx_full, n - 1)
                    dve.wait_ge(stm_ready, n - 1)
                st = stm[:, half, :, :, :]
                link(dve.tensor_scalar(st[:, :, :, 3 * HD], m, -1.0, None, ALU.mult))
                dve.scalar_tensor_tensor(out=st[:, :, :, 3 * HD + 1], in0=m, scalar=-1.0,
                                         in1=st[:, :, :, 3 * HD].bitcast(F32), op0=ALU.mult, op1=ALU.subtract)\
                    .then_inc(stm_ready, 1)

            def yout(s, c):
                n = 2 * s + c
                b, g = divmod(s, G)
                dve.wait_ge(yo_full, n + 1)
                if n >= 1:
                    dve.wait_ge(y_norm, n)
                v = T[:, :].rearrange("p (t h d) -> p t h d", t=CT, h=GH)
                if b:
                    dve.wait_ge(fin_full, c + 1)
                link(dve.reciprocal(yrec, v[:, :, :, HD]))
                dst = ytok[:, c * CT:(c + 1) * CT, g * GH * HD:(g + 1) * GH * HD]
                dve.tensor_tensor(dst.rearrange("p t (h d) -> p t h d", h=GH), v[:, :, :, 0:HD],
                                  yrec.unsqueeze(3).to_broadcast([P, CT, GH, HD]), ALU.mult)\
                    .then_inc(y_norm, 1)

            def causal():
                for n in range(NC * NU, NC * NU + 4):
                    tiles(n)
                dve.wait_ge(qkv_full, TB)
                dve.memset(uh[:, 0:2 * CW].bitcast(F32), 0.0)
                dve.memset(ul[:, 0:2 * CW].bitcast(F32), 0.0).then_inc(kz_clear, 1)
                norm(18)
                moments(19)
                for s in range(-1, STEPS):
                    for k in range(NBLK):
                        if s + 1 < STEPS:
                            maxima(s + 1, k)
                        else:
                            drains(s, k)
                        for todo in HOOKS.get(("dve", s, k), []):
                            if todo[0] == "ln":
                                split(todo[1])
                            if todo[0] == "moments":
                                moments(todo[1])
                            if todo[0] == "norm":
                                norm(todo[1])
                            if todo[0] == "negate":
                                negate(*todo[1:])
                yout(STEPS - 1, 1)
                update(4 * CAUSAL + 3, 1.0, T)
                moments(22)

            moments(0)
            dve.wait_ge(q_loaded, 32)
            dve.tensor_scalar(w1f[:, :], raw_q[:, 0, :], -128.0, None, ALU.add).then_inc(w1_ready, 1)
            dve.wait_ge(w1_hi, 1)
            dve.tensor_tensor(w1l[:, :], w1f[:, :], w1h[:, :].bitcast(F32), ALU.subtract).then_inc(w2_ready, 1)
            norm(0)
            moments(1)
            dve.wait_ge(small_loaded, 32)
            dve.scalar_tensor_tensor(out=w2[:, :, :].rearrange("p k n -> p (k n)"), in0=raw_q[:, 1, :], scalar=-128.0,
                                     in1=rows[:, R_S2:R_S2 + F], op0=ALU.add, op1=ALU.mult).then_inc(w2_ready, 1)
            split(0)
            norm(1)
            moments(2)
            ffn(FFN0)
            linear()
            ffn(FFN1)
            moe(MOE0)
            causal()
            moe(MOE1)

        @block.tensor
        def _(pe):
            drain = [None]

            def t_take(drained, value):
                if drain[0]:
                    pe.wait_ge(*drain[0])
                drain[0] = (drained, value)

            def mm3(dst, ah, al, bh, bl, start=True, stop=True):
                pe.matmul(dst, ah, bl, start=start, stop=False)
                pe.matmul(dst, al, bh, start=False, stop=False)
                return pe.matmul(dst, ah, bh, start=False, stop=stop)

            def ln(L):
                pe.wait_ge(norm_ready, L + 1)
                t_take(ft_ready, L + 1)
                for t in range(CT):
                    ins = pe.transpose(T[:, t * P:(t + 1) * P], hn[:, L % 2, t, :], ident[:, :])
                ins.then_inc(ln_t, 1)

            def acc_take(L):
                if L:
                    pe.wait_ge(x_ready, L)

            def ffn(p):
                if p:
                    pe.wait_ge(mix_ready, 8)
                for n in range(NC * FB + 2):
                    if n < NC * FB:
                        c, k = divmod(n, FB)
                        m = n + (16 if p == FFN1 else 0)
                        if k == 0:
                            pe.wait_ge(split_ready, 4 * p + c + 1)
                        if n >= 4:
                            pe.wait_ge(h_ready, m - 3)
                        f = slice(k * P, (k + 1) * P)
                        mm3(bank[1 + m % 4][:, :], w1h[:, f], w1l[:, f], uh[:, tok(c)], ul[:, tok(c)])\
                            .then_inc(y_full, 1)
                        if k == 1:
                            ln(4 * p + c + 1)
                        if n == NC * FB - 1 and p == FFN1:
                            route(4 * MOE0, 0)
                    if n >= 2:
                        c, k = divmod(n - 2, FB)
                        m = n - 2 + (16 if p == FFN1 else 0)
                        if k == 0:
                            acc_take(4 * p + c)
                        pe.wait_ge(h_ready, m + 1)
                        for t in range(CT):
                            ins = pe.matmul(ACC[:, t * P:(t + 1) * P], hbuf[:, m % 4, t * P:(t + 1) * P], w2[:, k, :],
                                            start=(k == 0 and t == 0), stop=(k == FB - 1), skip_group_check=True)
                        ins.then_inc(down_done, 1)

            def q_product(b, c):
                L = 4 * LIN + 2 * b + c
                pe.wait_ge(split_ready, L + 1)
                if b:
                    pe.wait_ge(yt_ready, c + 1)
                mm3(lin_bank(b, c)[:, :], wh[:, W_Q:W_Q + P], wl[:, W_Q:W_Q + P], uh[:, tok(2 * b + c)],
                    ul[:, tok(2 * b + c)]).then_inc(q_full, 1)

            def kv_product(b, t):
                pe.wait_ge(split_ready, 4 * LIN + 2 * b + t // 2 + 1)
                if b:
                    pe.wait_ge(yt_ready, 3 + t) if t < 2 else pe.wait_ge(mix_ready, 1 + t)
                for e in range(2):
                    i = TB * b + 2 * t + e
                    ins = mm3(lin_bank(b, 2 + t)[:, e * 256:(e + 1) * 256], uh[:, i * P:(i + 1) * P],
                              ul[:, i * P:(i + 1) * P], wh[:, W_KV:W_KV + 2 * P], wl[:, W_KV:W_KV + 2 * P])
                ins.then_inc(kv_full, 1)

            def state(b):
                pe.wait_ge(qf_ready, 2 * b + 1)
                for i in range(TB):
                    pe.wait_ge(kv_ready, 4 * b + i // 2 + 1)
                    ins = pe.matmul(lin_bank(b, 0)[:, 0:D + 1], kf[:, i, :], vx[:, i, :], start=(i == 0),
                                    stop=(i == TB - 1))
                ins.then_inc(s_full, 1)

            def attend(b):
                pe.wait_ge(kx_ready, b + 1)
                pe.wait_ge(qf_ready, 2 * b + 2)
                for t in range(4):
                    for e in range(2):
                        i = 2 * t + e
                        ins = pe.matmul(lin_bank(b, 1 + t)[:, e * 256:e * 256 + P + H], qf[:, i * P:(i + 1) * P],
                                        kx[:, :], start=True, stop=True)
                    ins.then_inc(o_full, 1)

            def turn(b, t):
                pe.wait_ge(yt_ready, 4 * b + t + 1)
                if t >= 2:
                    pe.wait_ge(mix_ready, 4 * b + t - 1)
                for e in range(2):
                    ins = pe.transpose(lin_bank(b, (5, 0)[t % 2])[:, e * P:(e + 1) * P], yt[t][:, e, :],
                                       ident[:, :])
                ins.then_inc(yt_full, 1)

            def project(b, t):
                pe.wait_ge(mix_ready, 4 * b + t + 1)
                if t % 2 == 0:
                    acc_take(4 * LIN + 2 * b + t // 2)
                for e in range(2):
                    i = 2 * t + e
                    ins = pe.matmul(ACC[:, (i % 4) * P:(i % 4 + 1) * P], mix[:, i * P:(i + 1) * P], wp[:, 0, :],
                                    start=True, stop=True)
                if t % 2:
                    ins.then_inc(acc_ready, 1)

            def linear():
                pe.wait_ge(h_ready, NC * FB)
                pe.wait_ge(wl_ready, 1)
                pe.wait_ge(borders, 1)
                ln(5)
                q_product(0, 0)
                q_product(0, 1)
                for t in range(4):
                    kv_product(0, t)
                ln(6)
                state(0)
                attend(0)
                ln(7)
                turn(0, 0)
                turn(0, 1)
                q_product(1, 0)
                turn(0, 2)
                project(0, 0)
                turn(0, 3)
                project(0, 1)
                q_product(1, 1)
                project(0, 2)
                kv_product(1, 0)
                project(0, 3)
                for t in range(1, 4):
                    kv_product(1, t)
                state(1)
                attend(1)
                ln(8)
                turn(1, 0)
                for t in range(1, 4):
                    turn(1, t)
                    project(1, t - 1)
                project(1, 3)

            def route(L, r):
                pe.wait_ge(split_ready, L + 1)
                t_take(lg_ready, r + 1)
                c = L % 4
                for t in range(CT):
                    i = c * CT + t
                    ins = mm3(T[:, t * 32:t * 32 + NR + 1], uh[:, i * P:(i + 1) * P], ul[:, i * P:(i + 1) * P],
                              wh[:, W_R:W_END], wl[:, W_R:W_END])
                ins.then_inc(lg_full, 1)

            def weights(r):
                pe.wait_ge(cs_ready, r + 1)
                t_take(cwt_ready, r + 1)
                tb = T[0:3 * NR, 0:CW // 2].bitcast(BF16)
                for t in range(CT):
                    ins = pe.transpose(tb[:, t * P:(t + 1) * P], cs[:, t, :, :].rearrange("p a n -> p (a n)"),
                                       identb[:, :])
                ins.then_inc(cw_full, 1)

            def moe(p):
                r0 = 4 if p == MOE1 else 0
                m0 = NC * NU if p == MOE1 else 0
                if p == MOE1:
                    pe.wait_ge(p_ready, STEPS * NBLK * GH)
                    pe.wait_ge(ysb_ready, 2 * STEPS)
                    pe.wait_ge(a_free, STEPS * NBLK * GH)
                if p == MOE0:
                    pe.wait_ge(h_ready, 2 * NC * FB)
                    pe.wait_ge(prep, 2)
                    pe.wait_ge(dw_loaded, 16)

                def gate_up(n):
                    c, u = divmod(n, NU)
                    m = m0 + n
                    if u == 0:
                        pe.wait_ge(split_ready, 4 * p + c + 1)
                    if n >= 2:
                        pe.wait_ge(hm_ready, m - 1)
                    f = slice(u * P, (u + 1) * P)
                    mm3(bank[1 + m % 2][:, :], gh[:, f], gl[:, f], uh[:, tok(c)], ul[:, tok(c)])
                    mm3(bank[3 + m % 2][:, :], vh[:, f], vl[:, f], uh[:, tok(c)], ul[:, tok(c)])

                gate_up(0)
                gate_up(1)
                if p == MOE0:
                    weights(r0)
                for n in range(NC * NU + 2):
                    if n < NC * NU:
                        c, u = divmod(n, NU)
                        m = m0 + n
                        L = 4 * p + c
                        if p == MOE0:
                            tiles(n, " first")
                        if n >= 2:
                            gate_up(n)
                        if u == 0:
                            pe.wait_ge(cwt_ready, r0 + c + 1)
                        pe.matmul(bank[5 + m % 2][:, :], sel[:, u, :], cwt[:, (r0 + c) % 2, :], start=True, stop=True)\
                            .then_inc(g_full, 1)
                        if u == 1 and L + 1 < 24 and L + 1 != 16:
                            ln(L + 1)
                        if p == MOE0:
                            tiles(n)
                        if c < 3 and u == 4:
                            route(L + 1, r0 + c + 1)
                        if c < 3 and u == 8:
                            weights(r0 + c + 1)
                    if n >= 2:
                        c, u = divmod(n - 2, NU)
                        m = m0 + n - 2
                        if u == 0:
                            acc_take(4 * p + c)
                        pe.wait_ge(hm_ready, m + 1)
                        for t in range(CT):
                            ins = pe.matmul(ACC[:, t * P:(t + 1) * P], hbuf[:, m % 3, t * P:(t + 1) * P], dw[:, u, :],
                                            start=(u == 0 and t == 0), stop=(u == NU - 1), skip_group_check=True)
                        ins.then_inc(down_done, 1)

            def tiles(n, first=""):
                for todo in EARLY.get(("pe" + first, n), []):
                    if todo[0] == "ln":
                        ln(todo[1])
                    if todo[0] == "qkv":
                        make_qkv(*todo[1:])
                    if todo[0] == "parts":
                        parts(*todo[1:])

            def make_qkv(b, i):
                n = TB * b + i
                pe.wait_ge(split_ready, 4 * CAUSAL + n // CT + 1)
                t_take(qkv_ready, n + 1)
                mm3(T[:, 0:3 * D], uh[:, n * P:(n + 1) * P], ul[:, n * P:(n + 1) * P],
                    wh[:, W_QKV:W_QKV + 3 * D], wl[:, W_QKV:W_QKV + 3 * D]).then_inc(qkv_full, 1)

            def parts(b, i, which):
                n = TB * b + i
                pe.wait_ge(*stg_done(n))
                t_take(kt_ready, 2 * n + which + 1)
                first = 0 if which else H
                for g in range(G):
                    o = slot(b, g) - 2 * b
                    ins = pe.transpose(T[:, o * P:(o + 1) * P].bitcast(F32R),
                                       stg[:, n % 2, first + g * GH:first + (g + 1) * GH, :]
                                       .rearrange("p h d -> p (h d)"), identr[:, :])
                ins.then_inc(kt_full, 1)

            def maxima(s, half):
                n = 2 * s + half
                pe.wait_ge(stm_ready, n + 1)
                t_take(qtb_ready, n + 1)
                b, g = divmod(s, G)
                for t in range(CT):
                    pe.matmul(T[:, t * P:(t + 1) * P], stm[:, half, t, :, :].rearrange("p h d -> p (h d)"),
                              identr[:, :], start=(t == 0), stop=False, skip_group_check=True)
                pe.matmul(T[:, :], identr[:, :], qta[:, slot(b, g), tok(half)], start=False, stop=True,
                          skip_group_check=True).then_inc(mx_full, 1)

            def sums(blk):
                s, k = divmod(blk, NBLK)
                c, j = B_BLOCKS[k]
                b, g = divmod(s, G)
                w = min(CW, CW * (c + 1) - j * P)
                pe.wait_ge(p_ready, GH * (blk + 1))
                pe.wait_ge(v_ready, TB * (b + 1))
                y = 2 * s + c
                if blk == 0:
                    pe.wait_ge(x_ready, 4 * CAUSAL)
                if j == 0 and y >= 1:
                    pe.wait_ge(ysb_ready, y)
                for h in range(GH):
                    ins = pe.matmul(bank[7][h * SL:h * SL + HD + 1, CW - w:CW], va[:, b, j, g * GH + h, :],
                                    pb[:, blk % 2, h, 0:w], start=(j == 0), stop=True,
                                    skip_group_check=True)
                ins.then_inc(pv_done, 1)

            def yout(s, c):
                n = 2 * s + c
                pe.wait_ge(ysb_ready, n + 1)
                t_take(y_norm, n + 1)
                for t in range(CT):
                    ins = pe.transpose(T[:, t * P:(t + 1) * P], ysb[:, n % 2, t * P:(t + 1) * P], ident[:, :])
                ins.then_inc(yo_full, 1)

            def final(b, c):
                f = 2 * b + c
                pe.wait_ge(y_norm, 2 * (G * b + G - 1) + c + 1)
                t_take(fin_ready, f + 1)
                for t in range(CT):
                    ins = pe.transpose(T[:, t * P:(t + 1) * P], ytok[:, c * CT + t, :], ident[:, :])
                ins.then_inc(fin_full, 1)

            def project_out(b, c):
                f = 2 * b + c
                t_take(x_ready, 4 * CAUSAL + f + 1)
                for t in range(CT):
                    ins = pe.matmul(T[:, t * P:(t + 1) * P], hbuf[:, 0, t * P:(t + 1) * P], wp[:, 1, :],
                                    start=True, stop=True)
                ins.then_inc(acc_ready, 1)

            def causal():
                def score(s, k, h):
                    c, j = B_BLOCKS[k]
                    b, g = divmod(s, G)
                    n = (s * NBLK + k) * GH + h
                    w = min(CW, CW * (c + 1) - j * P)
                    if h == 0:
                        pe.wait_ge(qtb_ready, 2 * s + c + 1)
                    if n == 0:
                        pe.wait_ge(a_free, NBLK * GH)
                    if n >= S_DEEP:
                        pe.wait_ge(p_ready, n - S_DEEP + 1)
                    ins = pe.matmul(s_bank(n)[:, 0:w], kz(s, h, j // CT)[:, j % CT * P:(j % CT + 1) * P],
                                    qtb[:, s % 2, (c + 1) * CW - w:(c + 1) * CW], start=True, stop=True)
                    if j < 4 * c:
                        ins.then_inc(b_full, 1)

                def mask(s, k, h):
                    c, j = B_BLOCKS[k]
                    n = (s * NBLK + k) * GH + h
                    if j >= 4 * c:
                        pe.matmul(s_bank(n)[:, 0:P], identb[:, :], mask_kq[:, :], start=False, stop=True,
                                  skip_group_check=True).then_inc(b_full, 1)

                def score_max(s, k, h):
                    i, half = A_BLOCKS[k]
                    b, g = divmod(s, G)
                    n = (s * NBLK + k) * GH + h
                    w = min(CW, (i + 1) * P - half * CW)
                    if h == 0 and g == 0:
                        pe.wait_ge(kt_ready, 2 * (TB * b + i + 1))
                    if h == 0 and k in (0, 8):
                        pe.wait_ge(kz_ready[s], GH * (1 + half))
                    if n < NBLK * GH:
                        if n >= 5:
                            pe.wait_ge(a_free, n - 4)
                    else:
                        pe.wait_ge(a_free, max(n - A_DEEP + 1, NBLK * GH))
                    pe.matmul(a_bank(n)[:, 0:w], qta[:, slot(b, g), i * P:(i + 1) * P],
                              kz(s, h, half)[:, 0:w], start=True, stop=True).then_inc(a_full, 1)

                for n in range(NC * NU, NC * NU + 4):
                    tiles(n, " first")
                    tiles(n)
                pe.wait_ge(hm_ready, NC * NU)
                for s in range(-1, STEPS):
                    for k in range(NBLK):
                        now, ahead = s >= 0, s + 1 < STEPS
                        for kind, h in BLOCK_ORDER:
                            if kind == "score" and now:
                                score(s, k, h)
                            if kind == "mask" and now:
                                mask(s, k, h)
                            if kind == "max" and ahead:
                                score_max(s + 1, k, h)
                            if kind == "sums" and now and s * NBLK + k >= 1:
                                sums(s * NBLK + k - 1)
                        for todo in HOOKS.get(("pe", s, k), []):
                            if todo[0] == "ln":
                                ln(todo[1])
                            if todo[0] == "qkv":
                                make_qkv(*todo[1:])
                            if todo[0] == "parts":
                                parts(*todo[1:])
                            if todo[0] == "max":
                                maxima(*todo[1:])
                            if todo[0] == "yout":
                                yout(*todo[1:])
                            if todo[0] == "final":
                                final(*todo[1:])
                            if todo[0] == "project":
                                project_out(*todo[1:])
                            if todo[0] == "route":
                                route(todo[1], 4)
                            if todo[0] == "weights":
                                weights(4)
                sums(STEPS * NBLK - 1)
                yout(STEPS - 1, 1)
                final(1, 1)
                project_out(1, 1)

            pe.wait_ge(ident_ready, 1)
            ln(0)
            pe.wait_ge(w2_ready, 2)
            ffn(FFN0)
            pe.wait_ge(consts, 2)
            linear()
            ffn(FFN1)
            moe(MOE0)
            causal()
            moe(MOE1)


def constants():
    import numpy as np
    c = np.zeros((P, C_END), np.float32)
    r = np.arange(P)
    c[:, C_ID:C_ID + P] = np.eye(P)
    c[:, C_MA:C_MA + P] = np.where(r[None, :] > r[:, None], -1e30, 0.0)
    c[:, C_MB:C_MB + P] = np.where(r[:, None] > r[None, :], -1e30, 0.0)
    c[:, C_BM:C_BM + P] = r[:, None] // HD == r[None, :] // HD
    c[:, C_HS:C_HS + H] = r[:, None] // HD == np.arange(H)[None, :]
    c[:, C_IO:C_IO + E_] = np.arange(E_)
    half = HD // 2
    theta = np.float32(1.0) / np.float32(10000.0) ** (np.arange(half, dtype=np.float32) / np.float32(half))
    freqs = np.arange(S, dtype=np.float32)[:, None] * theta[None, :].astype(np.float32)
    freqs = np.repeat(freqs, 2, axis=-1).astype(np.float64)
    sign = np.where(np.arange(HD) < half, -1.0, 1.0)
    c[:, C_COS:C_COS + TB * HD] = np.cos(freqs).reshape(TB, P, HD).transpose(1, 0, 2).reshape(P, -1)
    c[:, C_SIN:C_SIN + TB * HD] = (np.sin(freqs) * sign).reshape(TB, P, HD).transpose(1, 0, 2).reshape(P, -1)
    for u in range(NU):
        for f in range(P):
            e = 2 * u + f // FE if u < E_ // 2 else E_
            for part in range(3):
                c[part * NR + e, C_SEL + u * P + f] = 1.0
    return c


def kernel(**inputs):
    import numpy as np
    import concourse.bacc as bacc
    from concourse import mybir as mb
    from concourse.bass_utils import run_bass_kernel_spmd as run

    v = {n: np.asarray(a) for n, a in inputs.items()}
    cat = np.concatenate

    def blocks(a):
        k = a.shape[0] // P
        return a.reshape(k, P, -1).transpose(1, 0, 2).reshape(P, -1)

    def experts(w, shared):
        return cat([w.transpose(1, 0, 2).reshape(D, -1), shared], 1)

    f0 = "L0_ffn_"
    m = "L1_ffn_"
    arrays = {
        "x_in": v["L0_attn_x"].reshape(B * S, D),
        "wa_in": cat([v["L0_attn_Wq"].T, v["L0_attn_Wk"].T, v["L0_attn_Wv"].T, v["L1_attn_w_qkv"],
                      v[m + "router_w"].T, v[m + "shared_gate_w"], np.zeros((D, 1), np.float32)], 1),
        "wp_in": cat([v["L0_attn_Wp"].T, v["L1_attn_w_proj"]], 1),
        "gw_in": experts(v[m + "Wg"], v[m + "Sg"]),
        "uw_in": experts(v[m + "Wu"], v[m + "Su"]),
        "dw_in": blocks(cat([v[m + "Wd"].reshape(-1, D), v[m + "Sd"]], 0)),
        "q1_in": v[f0 + "fc1_q"],
        "q2_in": blocks(v[f0 + "fc2_q"]),
        "small_in": cat([v[f0 + "fc1_scales"].reshape(FB, P).T, v[f0 + "fc1_bias"].reshape(FB, P).T,
                         v[f0 + "ln_gamma"][:, None], v[f0 + "ln_beta"][:, None],
                         v["L0_attn_conv_w"], v["L0_attn_conv_b"][:, None]], 1),
        "rows_in": cat([v[f0 + "fc2_bias"], v["L0_attn_bp"], v[f0 + "fc2_scales"].reshape(-1)])[None, :],
        "const_in": constants(),
    }
    arrays = {n: np.ascontiguousarray(a) for n, a in arrays.items()}
    nc = bacc.Bacc("TRN2", target_bir_lowering=False, num_devices=1)
    args = [nc.dram_tensor(n, a.shape, mb.dt.from_np(a.dtype), kind="ExternalInput").ap() for n, a in arrays.items()]
    out = nc.dram_tensor("y_out", (B, S, D), mb.dt.float32, kind="ExternalOutput").ap()
    macaron(nc, *args, out)
    r = run(nc, [arrays], core_ids=[0])
    return r.results[0]["y_out"]
```
